# Optimizing a Trainium2 kernel written in Bass

```python
import numpy as np
import jax
import jax.numpy as jnp

def _softmax(x, axis=-1):
    return jax.nn.softmax(x, axis=axis)

def _gelu(x):
    return jax.nn.gelu(x, approximate=True)

def _silu(x):
    return jax.nn.silu(x)

def _sigmoid(x):
    return jax.nn.sigmoid(x)

def _layernorm(x, axis=-1, eps=1e-05):
    m = jnp.mean(x, axis=axis, keepdims=True)
    v = jnp.var(x, axis=axis, keepdims=True)
    return (x - m) / jnp.sqrt(v + eps)

def _scatter_add(tgt, idx, src, axis=0):
    return tgt.at[idx].add(src)

def _segment_sum(src, seg, n):
    return jax.ops.segment_sum(src, seg, n)
kernel_name = 'mk_gnn_preln_d1_gnn_r16_673c24'

def setup_inputs(seed: int=0):
    np.random.seed(seed)
    _w = jnp.asarray

    def _rec_inputs():
        import jax
        import jax.numpy as jnp
        _gk = jax.random.key(seed)
        x = 7.22e-05 + 1 * jax.random.normal(jax.random.fold_in(_gk, 1), (1024, 512), jnp.float32)
        src = jax.random.randint(jax.random.fold_in(_gk, 2), (16384,), 0, 1024, jnp.int32)
        dst = jax.random.randint(jax.random.fold_in(_gk, 3), (16384,), 0, 1024, jnp.int32)
        _o = jnp.argsort(dst, stable=True)
        src = src[_o]
        dst = dst[_o]
        return (x, src, dst)
    x, src, dst = _rec_inputs()

    def _L0_gnn_setup():
        import jax, jax.numpy as jnp
        import numpy as np
        N, D, BS, M, DC, H, DH, L, E = (1024, 512, 16, 256, 512, 8, 64, 4, 16384)
        EPS = 1e-05

        def _ln(x, w, b):
            mu = jnp.mean(x, -1, keepdims=True)
            var = jnp.var(x, -1, keepdims=True)
            return (x - mu) * jax.lax.rsqrt(var + EPS) * w + b

        def _gcn(x, src, dst, W, b, n):
            deg = jax.ops.segment_sum(jnp.ones_like(src, dtype=x.dtype), dst, num_segments=n)
            dinv = jnp.where(deg > 0, deg ** (-0.5), 0.0)
            norm = dinv[src] * dinv[dst]
            h = x @ W
            out = jax.ops.segment_sum(h[src] * norm[:, None], dst, num_segments=n)
            return out + b

        def _attn(xf, cond, Wq, Wk, Wv, Wo):
            n, d = xf.shape
            xb = xf.reshape(BS, n // BS, d)
            q = (xb @ Wq).reshape(BS, -1, H, DH)
            k = (cond @ Wk).reshape(BS, -1, H, DH)
            v = (cond @ Wv).reshape(BS, -1, H, DH)
            att = jnp.einsum('bnhd,bmhd->bhnm', q, k) * DH ** (-0.5)
            w = jax.nn.softmax(att, axis=-1)
            o = jnp.einsum('bhnm,bmhd->bnhd', w, v).reshape(BS, -1, H * DH)
            return (o @ Wo).reshape(n, d)
        key = jax.random.key(seed)
        ks = jax.random.split(key, 24)
        s = lambda fi, fo: (2.0 / (fi + fo)) ** 0.5
        inp = {'x': jax.random.normal(ks[0], (N, D), jnp.float32), 'edge_index': jax.random.randint(ks[1], (2, E), 0, N, jnp.int64), 'cond': jax.random.normal(ks[2], (BS, M, DC), jnp.float32), 'bn_w': jnp.ones((D,), jnp.float32), 'bn_b': jnp.zeros((D,), jnp.float32), 'gcn_in_w': jax.random.normal(ks[3], (D, D), jnp.float32) * s(D, D), 'gcn_in_b': jnp.zeros((D,), jnp.float32), 'gcn_out_w': jax.random.normal(ks[4], (D, D), jnp.float32) * s(D, D), 'gcn_out_b': jnp.zeros((D,), jnp.float32), 'Wq': jax.random.normal(ks[5], (L, D, H * DH), jnp.float32) * s(D, H * DH), 'Wk': jax.random.normal(ks[6], (L, DC, H * DH), jnp.float32) * s(DC, H * DH), 'Wv': jax.random.normal(ks[7], (L, DC, H * DH), jnp.float32) * s(DC, H * DH), 'Wo': jax.random.normal(ks[8], (L, H * DH, D), jnp.float32) * s(H * DH, D), 'ln2_w': jnp.ones((L, D), jnp.float32), 'ln2_b': jnp.zeros((L, D), jnp.float32), 'ln3_w': jnp.ones((L, D), jnp.float32), 'ln3_b': jnp.zeros((L, D), jnp.float32), 'geglu_w': jax.random.normal(ks[9], (L, D, 8 * D), jnp.float32) * s(D, 8 * D), 'geglu_b': jnp.zeros((L, 8 * D), jnp.float32), 'ffo_w': jax.random.normal(ks[10], (L, 4 * D, D), jnp.float32) * s(4 * D, D), 'ffo_b': jnp.zeros((L, D), jnp.float32)}
        return inp
    _L0_gnn_all = _L0_gnn_setup()
    _L0_gnn_in = {k: v for k, v in _L0_gnn_all.items() if k in ('cond', 'bn_w', 'bn_b', 'gcn_in_w', 'gcn_in_b', 'gcn_out_w', 'gcn_out_b', 'Wq', 'Wk', 'Wv', 'Wo', 'ln2_w', 'ln2_b', 'ln3_w', 'ln3_b', 'geglu_w', 'geglu_b', 'ffo_w', 'ffo_b')}
    del _L0_gnn_all
    return {'x': x, 'src': src, 'dst': dst, 'L0_gnn_cond': _L0_gnn_in['cond'], 'L0_gnn_bn_w': _L0_gnn_in['bn_w'], 'L0_gnn_bn_b': _L0_gnn_in['bn_b'], 'L0_gnn_gcn_in_w': _L0_gnn_in['gcn_in_w'], 'L0_gnn_gcn_in_b': _L0_gnn_in['gcn_in_b'], 'L0_gnn_gcn_out_w': _L0_gnn_in['gcn_out_w'], 'L0_gnn_gcn_out_b': _L0_gnn_in['gcn_out_b'], 'L0_gnn_Wq': _L0_gnn_in['Wq'], 'L0_gnn_Wk': _L0_gnn_in['Wk'], 'L0_gnn_Wv': _L0_gnn_in['Wv'], 'L0_gnn_Wo': _L0_gnn_in['Wo'], 'L0_gnn_ln2_w': _L0_gnn_in['ln2_w'], 'L0_gnn_ln2_b': _L0_gnn_in['ln2_b'], 'L0_gnn_ln3_w': _L0_gnn_in['ln3_w'], 'L0_gnn_ln3_b': _L0_gnn_in['ln3_b'], 'L0_gnn_geglu_w': _L0_gnn_in['geglu_w'], 'L0_gnn_geglu_b': _L0_gnn_in['geglu_b'], 'L0_gnn_ffo_w': _L0_gnn_in['ffo_w'], 'L0_gnn_ffo_b': _L0_gnn_in['ffo_b']}

def reference(x, src, dst, L0_gnn_cond, L0_gnn_bn_w, L0_gnn_bn_b, L0_gnn_gcn_in_w, L0_gnn_gcn_in_b, L0_gnn_gcn_out_w, L0_gnn_gcn_out_b, L0_gnn_Wq, L0_gnn_Wk, L0_gnn_Wv, L0_gnn_Wo, L0_gnn_ln2_w, L0_gnn_ln2_b, L0_gnn_ln3_w, L0_gnn_ln3_b, L0_gnn_geglu_w, L0_gnn_geglu_b, L0_gnn_ffo_w, L0_gnn_ffo_b):
    import jax
    import jax.numpy as jnp

    def _L0_gnn_ref(x, edge_index, cond, bn_w, bn_b, gcn_in_w, gcn_in_b, gcn_out_w, gcn_out_b, Wq, Wk, Wv, Wo, ln2_w, ln2_b, ln3_w, ln3_b, geglu_w, geglu_b, ffo_w, ffo_b):
        import jax, jax.numpy as jnp
        import numpy as np
        N, D, BS, M, DC, H, DH, L, E = (1024, 512, 16, 256, 512, 8, 64, 4, 16384)
        EPS = 1e-05

        def _ln(x, w, b):
            mu = jnp.mean(x, -1, keepdims=True)
            var = jnp.var(x, -1, keepdims=True)
            return (x - mu) * jax.lax.rsqrt(var + EPS) * w + b

        def _gcn(x, src, dst, W, b, n):
            deg = jax.ops.segment_sum(jnp.ones_like(src, dtype=x.dtype), dst, num_segments=n)
            dinv = jnp.where(deg > 0, deg ** (-0.5), 0.0)
            norm = dinv[src] * dinv[dst]
            h = x @ W
            out = jax.ops.segment_sum(h[src] * norm[:, None], dst, num_segments=n)
            return out + b

        def _attn(xf, cond, Wq, Wk, Wv, Wo):
            n, d = xf.shape
            xb = xf.reshape(BS, n // BS, d)
            q = (xb @ Wq).reshape(BS, -1, H, DH)
            k = (cond @ Wk).reshape(BS, -1, H, DH)
            v = (cond @ Wv).reshape(BS, -1, H, DH)
            att = jnp.einsum('bnhd,bmhd->bhnm', q, k) * DH ** (-0.5)
            w = jax.nn.softmax(att, axis=-1)
            o = jnp.einsum('bhnm,bmhd->bnhd', w, v).reshape(BS, -1, H * DH)
            return (o @ Wo).reshape(n, d)
        n = x.shape[0]
        loops = jnp.arange(n)
        src = jnp.concatenate([edge_index[0], loops])
        dst = jnp.concatenate([edge_index[1], loops])
        x_in = x
        mu = jnp.mean(x, 0)
        var = jnp.var(x, 0)
        h = (x - mu) * jax.lax.rsqrt(var + EPS) * bn_w + bn_b
        h = _gcn(h, src, dst, gcn_in_w, gcn_in_b, n)
        for i in range(L):
            a = _attn(_ln(h, ln2_w[i], ln2_b[i]), cond, Wq[i], Wk[i], Wv[i], Wo[i])
            h = h + a
            u = _ln(h, ln3_w[i], ln3_b[i]) @ geglu_w[i] + geglu_b[i]
            val, gate = jnp.split(u, 2, axis=-1)
            f = val * jax.nn.gelu(gate, approximate=False)
            h = h + f @ ffo_w[i] + ffo_b[i]
        h = _gcn(h, src, dst, gcn_out_w, gcn_out_b, n)
        return h + x_in
    edge_index = jnp.stack([src, dst])
    h = jnp.maximum(_layernorm(x, axis=-1), 0.0)
    x = x + _L0_gnn_ref(h, edge_index, L0_gnn_cond, L0_gnn_bn_w, L0_gnn_bn_b, L0_gnn_gcn_in_w, L0_gnn_gcn_in_b, L0_gnn_gcn_out_w, L0_gnn_gcn_out_b, L0_gnn_Wq, L0_gnn_Wk, L0_gnn_Wv, L0_gnn_Wo, L0_gnn_ln2_w, L0_gnn_ln2_b, L0_gnn_ln3_w, L0_gnn_ln3_b, L0_gnn_geglu_w, L0_gnn_geglu_b, L0_gnn_ffo_w, L0_gnn_ffo_b)
    return x

_drawn_inputs = setup_inputs


def setup_inputs(seed=0):
    import zlib

    import numpy as np

    out = dict(_drawn_inputs(seed))
    spreads = {'L0_gnn_bn_w': (1.0, 0.6),
     'L0_gnn_bn_b': (0.0, 0.1),
     'L0_gnn_gcn_in_b': (0.0, 0.1),
     'L0_gnn_gcn_out_b': (0.0, 0.1),
     'L0_gnn_ln2_w': (1.0, 0.6),
     'L0_gnn_ln2_b': (0.0, 0.8),
     'L0_gnn_ln3_w': (1.0, 0.584),
     'L0_gnn_ln3_b': (0.0, 0.406),
     'L0_gnn_geglu_b': (0.0, 0.1),
     'L0_gnn_ffo_b': (0.0, 0.1)}
    factors = {}
    for name, (base, spread) in spreads.items():
        noise = np.random.default_rng([zlib.crc32(name.encode()), seed]).standard_normal(out[name].shape)
        drawn = base * np.exp(spread * noise) if base else spread * noise
        out[name] = jnp.asarray(drawn.astype(out[name].dtype))
    for name, factor in factors.items():
        out[name] = (out[name] * factor).astype(out[name].dtype)
    return out
```

```python
import concourse.bass as bass
from concourse import mybir
from contextlib import ExitStack


def gnn_preln_kernel(
    nc: bass.Bass,
    x: bass.AP,
    src: bass.AP,
    dst: bass.AP,
    condT: bass.AP,
    pieces: bass.AP,
    cols: bass.AP,
    rows: bass.AP,
    out: bass.AP,
):
    f32 = mybir.dt.float32
    f32r = mybir.dt.float32r
    f16 = mybir.dt.float16
    i32 = mybir.dt.int32
    ALU = mybir.AluOpType
    ACT = mybir.ActivationFunctionType
    AX = mybir.AxisListType

    P = 128
    N, D = x.shape
    NT, KC = N // P, D // P
    GROUPS = condT.shape[0]
    M = condT.shape[3] // 2
    PAIRS = 4
    E = src.shape[0] * src.shape[1]
    CHUNKS = E // P
    HALF = N // 2
    L = (pieces.shape[0] - 10) // 32
    UNITS = GROUPS * PAIRS
    MG = 8
    PIECES = 4 * MG
    FIRST_PIECES = 10
    COL = {"bn_w": 0, "bn_b": 4, "ln2_w": 8, "ln2_b": 24, "ln3_w": 40, "ln3_b": 56, "geglu_b": 72}
    EPS = 1e-5
    Q_SCALE = 0.125
    assert NT == GROUPS and L * 32 == 128

    with ExitStack() as ctx:
        def sb(name, shape, dt, where=ctx):
            return where.enter_context(nc.sbuf_tensor(name, shape, dt))

        def sem(name):
            return ctx.enter_context(nc.semaphore(name))

        h = sb("h", [P, NT, D], f32)
        w_hi = sb("w_hi", [P, 4, KC, D], f32r)
        w_lo = sb("w_lo", [P, 4, KC, D], f32r)
        stage = sb("stage", [P, 2, 1024], f32)
        oT_hi = sb("oT_hi", [P, PAIRS, P], f32r)
        oT_lo = sb("oT_lo", [P, PAIRS, P], f32r)
        full = sb("full", [P, 2, D], f32)
        bias_row = sb("bias_row", [P, D], f32)
        cols_sb = sb("cols_sb", [P, cols.shape[1]], f32)
        ident = sb("ident", [P, P], f32)
        mhalf = sb("mhalf", [P, NT], f32)
        ones = sb("ones", [P, 2], f32r)
        stats = sb("stats", [P, 2, 6], f32)
        mv = sb("mv", [P, 2], f32)
        veps = sb("veps", [P, 1], f32)
        rstd = sb("rstd", [P, 1], f32)
        nmx = sb("nmx", [P, 2], f32)
        rsum = sb("rsum", [P, 2], f32)
        rinv = sb("rinv", [P, 2], f32)
        deg = sb("deg", [P, NT], f32)
        dinv = sb("dinv", [P, NT], f32)
        bn = sb("bn", [P, 8], f32)
        zeros = sb("zeros", [P, HALF], f16)

        def overlay(*uses):
            made = []
            for use in uses:
                with ExitStack() as where:
                    made.append([sb(*one, where) for one in use])
            big = max(sum(size(one) for one in use) for use in uses)
            ctx.enter_context(nc.sbuf_tensor(f"room_of_{uses[0][0][0]}", [P, big], mybir.dt.int8))
            return made

        def size(one):
            n = 2 if one[2] == f16 else 4
            for d in one[1][1:]:
                n *= d
            return n

        (at_hi,), (cond_hi, cond_lo), (xT3_hi, xT3_lo) = overlay(
            [("at_hi", [P, NT, N], f32r)],
            [("cond_hi", [P, 2, KC, 2 * M], f32r), ("cond_lo", [P, 2, KC, 2 * M], f32r)],
            [("xT3_hi", [P, KC, N], f32r), ("xT3_lo", [P, KC, N], f32r)])
        (at_lo,), (v_hi, v_lo), (wg_hi, wg_lo) = overlay(
            [("at_lo", [P, NT, N], f32r)],
            [("v_hi", [P, 2, 4, D], f32r), ("v_lo", [P, 2, 4, D], f32r)],
            [("wg_hi", [P, 2, KC, 2, 256], f32r), ("wg_lo", [P, 2, KC, 2, 256], f32r)])
        (x0T,), (xs,), (kT_hi, kT_lo, pT_hi, pT_lo), (wf_hi, wf_lo) = overlay(
            [("x0T", [P, KC, N], f32)],
            [("xs", [P, NT, D], f32)],
            [("kT_hi", [P, 2 * M], f32r), ("kT_lo", [P, 2 * M], f32r),
             ("pT_hi", [P, 4, P], f32r), ("pT_lo", [P, 4, P], f32r)],
            [("wf_hi", [P, 2, 2, D], f32r), ("wf_lo", [P, 2, 2, D], f32r)])
        (oh_s, oh_d, iota), (xs_hi,), (pe_, pn, q_sb, z2, xT2_hi, xT2_lo), (f0_hi, f0_lo) = overlay(
            [("oh_s", [P, 4, N], f16), ("oh_d", [P, 4, HALF], f16), ("iota", [P, N], f16)],
            [("xs_hi", [P, NT, D], f32r)],
            [("p_exp", [P, 2, M], f32), ("p_norm", [P, 2, M], f32), ("q_sb", [P, D], f32),
             ("z2", [P, D], f32), ("xT2_hi", [P, KC, P], f32r), ("xT2_lo", [P, KC, P], f32r)],
            [("f0_hi", [P, 2, N], f32r), ("f0_lo", [P, 2, N], f32r)])
        (c_in,), (xs_lo,), (z3,), (f1_hi, f1_lo) = overlay(
            [("c_in", [P, 2, KC * 2 * M], f32)],
            [("xs_lo", [P, NT, D], f32r)],
            [("z3", [P, NT, D], f32)],
            [("f1_hi", [P, 2, N], f32r), ("f1_lo", [P, 2, N], f32r)])
        (res,), (qbd_hi, qbd_lo), (gel, ff) = overlay(
            [("res", [P, 4, D], f32)],
            [("qbd_hi", [P, PAIRS, 2, P], f32r), ("qbd_lo", [P, PAIRS, 2, P], f32r)],
            [("gel", [P, 2, D], f32), ("ff", [P, 2, D], f32)])
        ends_i = sb("ends_i", [P, 2, CHUNKS], i32)
        ends_f = sb("ends_f", [P, 2, CHUNKS], f32)

        yT_hi = w_hi[:, 1:3].rearrange("p a c n -> p (a c n)").rearrange("p (k n) -> p k n", n=N)
        yT_lo = w_lo[:, 1:3].rearrange("p a c n -> p (a c n)").rearrange("p (k n) -> p k n", n=N)
        f_hi, f_lo = [f0_hi, f1_hi], [f0_lo, f1_lo]

        ps = ctx.enter_context(nc.psum_tensor("ps", [P, 8, 512], f32))
        K_BANK, V_BANK, S_BANK, T_BANK, PV_BANK, X_BANK, Y_BANK = 0, 1, 2, 3, 4, 6, 7

        cond_s = [nc.dram_tensor(f"cond_{part}_s", [GROUPS, P, KC * 2 * M], f32, kind="Internal").ap()
                  for part in ("hi", "lo")]
        at_s = [nc.dram_tensor(f"at_{part}_s", [P, NT * N], f32, kind="Internal").ap()
                for part in ("hi", "lo")]
        res_s = nc.dram_tensor("res_s", [N, D], f32, kind="Internal").ap()

        x_in, cols_in, ends_in, row_in = sem("x_in"), sem("cols_in"), sem("ends_in"), sem("row_in")
        stage_in = [sem("stage_in0"), sem("stage_in1")]
        c_in_in = [sem("c_in_in0"), sem("c_in_in1")]
        cond_out = [sem("cond_out0"), sem("cond_out1")]
        cond_in = [sem("cond_in0"), sem("cond_in1")]
        res_out = [sem("res_out0"), sem("res_out1")]
        res_in = [sem("res_in0"), sem("res_in1")]
        at_out, at_in, out_done = sem("at_out"), sem("at_in"), sem("out_done")
        waited = sem("waited")
        const_ok, ones_ok, iota_ok, ends_ok = sem("const_ok"), sem("ones_ok"), sem("iota_ok"), sem("ends_ok")
        ln = sem("ln")
        rs = sem("rs")
        x0_ok, res_ok, x0_mm, x0T_ok = sem("x0_ok"), sem("res_ok"), sem("x0_mm"), sem("x0T_ok")
        bn_ok, bnf_ok, y_hi, y_lo = sem("bn_ok"), sem("bnf_ok"), sem("y_hi"), sem("y_lo")
        c_hi, c_lo = sem("c_hi"), sem("c_lo")
        oh_ok, oh_used, a_mm, a_hi, a_lo = sem("oh_ok"), sem("oh_used"), sem("a_mm"), sem("a_hi"), sem("a_lo")
        deg_mm, deg_ok, dinv_ok = sem("deg_mm"), sem("deg_ok"), sem("dinv_ok")
        g_mm, xs_ok, xs_hi_ok, xs_lo_ok, agg_mm, agg_s, gcn_ok = (
            sem("g_mm"), sem("xs_ok"), sem("xs_hi_ok"), sem("xs_lo_ok"), sem("agg_mm"), sem("agg_s"),
            sem("gcn_ok"))
        hT_mm = sem("hT_mm")
        w_hi_ok, w_ok = sem("w_hi_ok"), sem("w_ok")
        k_mm, k_hi_ok, k_ok = sem("k_mm"), sem("k_hi_ok"), sem("k_ok")
        v_mm, v_hi_ok, v_ok = sem("v_mm"), sem("v_hi_ok"), sem("v_ok")
        s_mm, mx_ok, exp_ok, rinv_ok, pn_ok = (sem("s_mm"), sem("mx_ok"), sem("exp_ok"), sem("rinv_ok"),
                                               sem("pn_ok"))
        t_mm, pT_hi_ok, pT_ok, pv_mm = sem("t_mm"), sem("pT_hi_ok"), sem("pT_ok"), sem("pv_mm")
        z2_ok, t2_mm, full2_ok, x2_hi_ok, x2_ok = (sem("z2_ok"), sem("t2_mm"), sem("full2_ok"),
                                                   sem("x2_hi_ok"), sem("x2_ok"))
        q_mm, q_ok, qt_mm, qb_hi_ok, qb_ok, qb_zero = (sem("q_mm"), sem("q_ok"), sem("qt_mm"),
                                                       sem("qb_hi_ok"), sem("qb_ok"), sem("qb_zero"))
        o_hi_ok, o_ok, wo_mm, h_att, z3_ok, h_bias = (sem("o_hi_ok"), sem("o_ok"), sem("wo_mm"),
                                                      sem("h_att"), sem("z3_ok"), sem("h_bias"))
        t3_mm, full3_ok, x3_hi_ok, x3_ok = sem("t3_mm"), sem("full3_ok"), sem("x3_hi_ok"), sem("x3_ok")
        u_mm, gel_ok, ff_ok, f_hi_ok, f_ok, ffo_mm, h_ffo = (
            sem("u_mm"), sem("gel_ok"), sem("ff_ok"), sem("f_hi_ok"), sem("f_ok"), sem("ffo_mm"),
            sem("h_ffo"))

        block = ctx.enter_context(nc.Block())

        def wait_apart(eng, on, value):
            eng.wait_ge(on, value)
            eng.sem_inc(waited, 1)

        def bits(ap):
            return ap.bitcast(f32)

        @block.sync
        def _(sp):
            sp.dma_start(cols_sb[:, :], cols).then_inc(cols_in, 16)
            sp.dma_start(h[:, :, :], x.rearrange("(t p) d -> p t d", p=P)).then_inc(x_in, 16)
            sp.dma_start(ends_i[:, 0, :], src).then_inc(ends_in, 16)
            sp.dma_start(ends_i[:, 1, :], dst).then_inc(ends_in, 16)
            sp.dma_start(bias_row[:, :], rows[0:1, :].partition_broadcast(P)).then_inc(row_in, 16)

            def piece(n, slot, first=False):
                if not first:
                    sp.wait_ge(w_ok, n - 1)
                sp.dma_start(stage[:, slot, :], pieces[n]).then_inc(stage_in[slot], 16)

            piece(0, 0, True)
            piece(1, 1, True)
            for t in range(NT):
                sp.wait_ge(res_ok, t + 1)
                sp.dma_start(res_s[t * P:(t + 1) * P, :], res[:, 2 + t % 2, :]).then_inc(res_out[t % 2], 16)
            sp.dma_start(c_in[:, 0, :], condT[0].rearrange("p k n -> p (k n)")).then_inc(c_in_in[0], 16)
            for g in range(GROUPS):
                s = g % 2
                if g + 1 < GROUPS:
                    if g:
                        sp.wait_ge(c_lo, g)
                    sp.dma_start(c_in[:, 1 - s, :], condT[g + 1].rearrange("p k n -> p (k n)"))\
                      .then_inc(c_in_in[1 - s], 16)
                sp.wait_ge(c_lo, g + 1)
                for part, buf in zip(cond_s, (cond_hi, cond_lo)):
                    sp.dma_start(part[g], bits(buf[:, s].rearrange("p k n -> p (k n)"))).then_inc(cond_out[s], 16)
            sp.wait_ge(a_lo, 2 * NT)
            for part, buf in zip(at_s, (at_hi, at_lo)):
                sp.dma_start(part, bits(buf[:, :, :].rearrange("p t n -> p (t n)"))).then_inc(at_out, 16)
            sp.wait_ge(g_mm, NT)
            for n in range(2, FIRST_PIECES):
                piece(n, n % 2)
            sp.wait_ge(gcn_ok, NT)
            sp.dma_start(bias_row[:, :], rows[1:2, :].partition_broadcast(P)).then_inc(row_in, 16)
            sp.wait_ge(agg_mm, NT)
            sp.wait_ge(at_out, 32)

            with sp.Fori(0, L) as l:
                def load_cond(g, slot):
                    for part, buf in zip(cond_s, (cond_hi, cond_lo)):
                        sp.dma_start(bits(buf[:, slot].rearrange("p k n -> p (k n)")), part[g])\
                          .then_inc(cond_in[slot], 16)
                load_cond(0, 0)
                load_cond(1, 1)
                with sp.Fori(1, GROUPS // 2) as i:
                    for a in range(2):
                        sp.wait_ge(k_mm, UNITS * l + 2 * PAIRS * i + PAIRS * (a - 1))
                        load_cond(2 * i + a, a)
                with sp.Fori(0, MG // 2) as j:
                    for a in range(2):
                        for r in range(4):
                            n = FIRST_PIECES + PIECES * l + 8 * j + 4 * a + r
                            sp.wait_ge(w_ok, n - 1)
                            sp.dma_start(stage[:, r % 2, :], pieces[n]).then_inc(stage_in[r % 2], 16)
                sp.wait_ge(h_bias, GROUPS * l + GROUPS)
                sp.dma_start(bias_row[:, :], rows[bass.ds(2 + l, 1), :].partition_broadcast(P)).then_inc(row_in, 16)
                wait_apart(sp, u_mm, 32 * l + 32)

            for part, buf in zip(at_s, (at_hi, at_lo)):
                sp.dma_start(bits(buf[:, :, :].rearrange("p t n -> p (t n)")), part).then_inc(at_in, 16)
            sp.wait_ge(qb_zero, 2 * (L + 1))
            for t in range(NT):
                if t >= 2:
                    sp.wait_ge(res_ok, NT + t - 1)
                sp.dma_start(res[:, t % 2, :], res_s[t * P:(t + 1) * P, :]).then_inc(res_in[t % 2], 16)
                if t >= 1:
                    sp.wait_ge(res_ok, NT + t)
                    sp.dma_start(out[(t - 1) * P:t * P, :], h[:, t - 1, :]).then_inc(out_done, 16)
            sp.wait_ge(res_ok, 2 * NT)
            sp.dma_start(out[(NT - 1) * P:N, :], h[:, NT - 1, :]).then_inc(out_done, 16)
            sp.wait_ge(out_done, 16 * NT)
            for s in range(2):
                sp.wait_ge(res_out[s], 16 * NT // 2)
                sp.wait_ge(cond_out[s], 32 * GROUPS // 2)

        @block.gpsimd
        def _(pool):
            pool.sem_inc(f_ok, 2)
            pool.sem_inc(x3_ok, 2)
            pool.memset(ident[:, :], 0.0).then_inc(const_ok, 1)
            pool.memset(mhalf[:, :], -0.5).then_inc(const_ok, 1)
            pool.wait_ge(const_ok, 2)
            pool.affine_select(out=ident[:, :], in_=ident[:, :], compare_op=ALU.not_equal, fill=1.0, base=0,
                               pattern=[[-1, P]], channel_multiplier=1).then_inc(const_ok, 1)
            pool.memset(zeros[:, :], 0.0).then_inc(const_ok, 1)
            pool.iota(iota[:, :], pattern=[[1, N]], base=0, channel_multiplier=0,
                      allow_small_or_imprecise_dtypes=True).then_inc(iota_ok, 1)

            def rsqrt(k):
                wait_apart(pool, ln, 2 * k + 2)
                pool.tensor_scalar(veps[:, :], mv[:, 1:2], EPS, None, ALU.add).then_inc(rs, 1)
                pool.wait_ge(rs, 2 * k + 1)
                pool.tensor_tensor(rstd[:, :], veps[:, :], mhalf[:, 0:1], ALU.pow).then_inc(rs, 1)

            def split(n, slot, hi, lo):
                wait_apart(pool, stage_in[slot], 8 * n + (16 if slot == 0 else 8))
                pool.tensor_copy(hi, stage[:, slot, :]).then_inc(w_hi_ok, 1)
                pool.wait_ge(w_hi_ok, n + 1)
                pool.tensor_tensor(lo, stage[:, slot, :], bits(hi), ALU.subtract).then_inc(w_ok, 1)

            def attn_part(buf, which, half):
                return buf[:, which, 2 * half:2 * half + 2, :].rearrange("p k n -> p (k n)")

            for t in range(NT):
                rsqrt(t)
            for n in range(2):
                split(n, n, attn_part(w_hi, 0, n), attn_part(w_lo, 0, n))
            for k in range(KC):
                rsqrt(NT + k)
                pool.wait_ge(y_hi, k + 1)
                pool.tensor_tensor(yT_lo[:, k, :], full[:, :, :].rearrange("p a n -> p (a n)"),
                                   bits(yT_hi[:, k, :]), ALU.subtract).then_inc(y_lo, 1)
            for g in range(GROUPS):
                s = g % 2
                if g >= 2:
                    pool.wait_ge(cond_out[s], 32 * (g // 2))
                pool.wait_ge(c_hi, g + 1)
                pool.tensor_tensor(cond_lo[:, s].rearrange("p k n -> p (k n)"), c_in[:, s, :],
                                   bits(cond_hi[:, s].rearrange("p k n -> p (k n)")), ALU.subtract)\
                    .then_inc(c_lo, 1)
            def zero_q():
                pool.memset(bits(qbd_hi[:, :, :, :]), 0.0).then_inc(qb_zero, 1)
                pool.memset(bits(qbd_lo[:, :, :, :]), 0.0).then_inc(qb_zero, 1)

            for s in range(2):
                pool.wait_ge(res_out[s], 16 * NT // 2)
            zero_q()
            pool.wait_ge(deg_ok, 1)
            pool.tensor_tensor(dinv[:, :], deg[:, :], mhalf[:, :], ALU.pow).then_inc(dinv_ok, 1)

            def xs_split(use):
                for t in range(NT):
                    pool.wait_ge(xs_hi_ok, NT * use + t + 1)
                    pool.tensor_tensor(xs_lo[:, t, :], xs[:, t, :], bits(xs_hi[:, t, :]), ALU.subtract)\
                        .then_inc(xs_lo_ok, 1)

            xs_split(0)
            pool.wait_ge(g_mm, NT)
            for n in range(2, FIRST_PIECES):
                split(n, n % 2, attn_part(w_hi, (n - 2) // 2, n % 2), attn_part(w_lo, (n - 2) // 2, n % 2))

            with pool.Fori(0, L) as l:
                norm0 = NT + KC + 2 * NT * l

                def x2_low(g):
                    pool.wait_ge(x2_hi_ok, GROUPS * l + g + 1)
                    pool.tensor_tensor(xT2_lo[:, :, :].rearrange("p k n -> p (k n)"), full[:, 0, :],
                                       bits(xT2_hi[:, :, :].rearrange("p k n -> p (k n)")),
                                       ALU.subtract).then_inc(x2_ok, 1)

                rsqrt(norm0)
                x2_low(0)
                with pool.Fori(0, GROUPS - 1) as g:
                    rsqrt(norm0 + 2 * g + 1)
                    x2_low(g + 1)
                    rsqrt(norm0 + 2 * g + 2)
                rsqrt(norm0 + 2 * NT - 1)

                def weights(j, a):
                    for r in range(2):
                        split(FIRST_PIECES + PIECES * l + 8 * j + 4 * a + r, r,
                              wg_hi[:, a, 2 * r:2 * r + 2].rearrange("p k v n -> p (k v n)"),
                              wg_lo[:, a, 2 * r:2 * r + 2].rearrange("p k v n -> p (k v n)"))

                def weights_out(j, a):
                    n = FIRST_PIECES + PIECES * l + 8 * j + 4 * a
                    split(n + 2, 0, wf_hi[:, a].rearrange("p c n -> p (c n)"),
                          wf_lo[:, a].rearrange("p c n -> p (c n)"))
                    split(n + 3, 1, attn_part(w_hi, j, a), attn_part(w_lo, j, a))

                def x3_low(t):
                    pool.wait_ge(x3_hi_ok, NT * l + t + 1)
                    pool.tensor_tensor(xT3_lo[:, :, t * P:(t + 1) * P],
                                       full[:, t % 2, :].rearrange("p (k n) -> p k n", n=P),
                                       bits(xT3_hi[:, :, t * P:(t + 1) * P]),
                                       ALU.subtract).then_inc(x3_ok, 1)

                def f_low(j, a, s):
                    half, c = s // 2, s % 2
                    pool.wait_ge(f_hi_ok, 32 * l + 8 * j + 4 * a + s + 1)
                    pool.tensor_tensor(f_lo[a][:, c, half * HALF:(half + 1) * HALF], ff[:, s % 2, :],
                                       bits(f_hi[a][:, c, half * HALF:(half + 1) * HALF]),
                                       ALU.subtract).then_inc(f_ok, 1)

                for t in range(4):
                    x3_low(t)
                pool.wait_ge(wo_mm, GROUPS * l + GROUPS)
                weights(0, 0)
                for t in range(4, NT):
                    x3_low(t)
                weights_out(0, 0)

                def mlp_group(j, a, first=False, last=False):
                    nj, na = (j, 1) if a == 0 else (j + 1, 0)
                    if not last:
                        if not first:
                            pool.wait_ge(u_mm, 32 * l + 8 * j + 4 * a)
                            weights(nj, na)
                    for s in range(4):
                        f_low(j, a, s)
                        if first and s == 1:
                            weights(nj, na)
                    if not last:
                        if not first:
                            pool.wait_ge(ffo_mm, 64 * l + 16 * j + 8 * a)
                        weights_out(nj, na)

                mlp_group(0, 0, first=True)
                mlp_group(0, 1)
                with pool.Fori(1, MG // 2 - 1) as j:
                    mlp_group(j, 0)
                    mlp_group(j, 1)
                mlp_group(MG // 2 - 1, 0)
                mlp_group(MG // 2 - 1, 1, last=True)
                wait_apart(pool, f_ok, 2 + 32 * l + 32)
                zero_q()

            for t in range(NT):
                pool.wait_ge(y_hi, KC + t + 1)
                pool.tensor_tensor(yT_lo[:, :, t * P:(t + 1) * P],
                                   full[:, t % 2, :].rearrange("p (k n) -> p k n", n=P),
                                   bits(yT_hi[:, :, t * P:(t + 1) * P]), ALU.subtract).then_inc(y_lo, 1)
            xs_split(1)

        @block.scalar
        def _(act):
            for t in range(NT):
                act.wait_ge(x0_mm, t + 1)
                act.activation(x0T[:, :, t * P:(t + 1) * P],
                               ps[:, t % 2, :].rearrange("p (k n) -> p k n", n=P), ACT.Copy)\
                    .then_inc(x0T_ok, 1)
            for k in range(KC):
                act.wait_ge(bnf_ok, k + 1)
                act.activation(yT_hi[:, k, :], full[:, :, :].rearrange("p a n -> p (a n)"), ACT.Copy)\
                    .then_inc(y_hi, 1)
            act.wait_ge(cols_in, 16)
            act.activation(ones[:, :], cols_sb[:, 0:2], ACT.Copy, bias=1.0, scale=0.0).then_inc(ones_ok, 1)
            for g in range(GROUPS):
                s = g % 2
                if g >= 2:
                    act.wait_ge(cond_out[s], 32 * (g // 2))
                act.wait_ge(c_in_in[s], 16 * (g // 2 + 1))
                act.activation(cond_hi[:, s].rearrange("p k n -> p (k n)"), c_in[:, s, :], ACT.Copy)\
                    .then_inc(c_hi, 1)
            for s in range(2):
                act.wait_ge(cond_out[s], 32 * GROUPS // 2)
            for half in range(2):
                for t in range(NT):
                    act.wait_ge(a_mm, NT * half + t + 1)
                    act.activation(at_hi[:, t, half * HALF:(half + 1) * HALF], ps[:, t, :], ACT.Copy)\
                        .then_inc(a_hi, 1)

            def xs_high(use):
                for t in range(NT):
                    act.wait_ge(xs_ok, NT * use + t + 1)
                    act.activation(xs_hi[:, t, :], xs[:, t, :], ACT.Copy).then_inc(xs_hi_ok, 1)

            xs_high(0)

            with act.Fori(0, L) as l:
                def v_high(u, mc, slot):
                    act.wait_ge(v_mm, u + 1)
                    act.activation(v_hi[:, slot, mc, :], ps[:, V_BANK, :], ACT.Copy).then_inc(v_hi_ok, 1)

                def k_high(u):
                    act.wait_ge(k_mm, u + 1)
                    act.activation(kT_hi[:, :], ps[:, K_BANK, :], ACT.Copy).then_inc(k_hi_ok, 1)

                def x2_high(g):
                    act.wait_ge(full2_ok, g + 1)
                    act.activation(xT2_hi[:, :, :].rearrange("p k n -> p (k n)"), full[:, 0, :], ACT.Copy)\
                        .then_inc(x2_hi_ok, 1)

                def q_copy(g):
                    act.wait_ge(q_mm, g + 1)
                    act.activation(q_sb[:, :], ps[:, Y_BANK, :], ACT.Copy, scale=Q_SCALE).then_inc(q_ok, 1)

                def q_high(g):
                    act.wait_ge(qt_mm, g + 1)
                    for e in range(2):
                        r = slice(64 * e, 64 * e + 64)
                        last = act.activation(
                            qbd_hi[r, :, :, r],
                            ps[r, X_BANK, :].rearrange("d (p b n) -> d p b n", p=PAIRS, b=2), ACT.Copy)
                    last.then_inc(qb_hi_ok, 1)

                def o_high(g):
                    act.wait_ge(pv_mm, PAIRS * g + PAIRS)
                    for e in range(2):
                        r = slice(64 * e, 64 * e + 64)
                        o_ps = ps[r, PV_BANK:PV_BANK + 2, :].rearrange("d a (p b n) -> d (a p b) n", p=2, b=2)
                        last = act.activation(oT_hi[r, :, :].rearrange("d p (b n) -> d (p b) n", b=2),
                                              o_ps[:, :, r], ACT.Copy)
                    last.then_inc(o_hi_ok, 1)

                def unit(u, g, p, par, last=False):
                    act.wait_ge(mx_ok, u + 1)
                    for b in range(2):
                        e = act.activation(pe_[:, b, :], ps[:, S_BANK, b * M:(b + 1) * M], ACT.Exp,
                                           bias=nmx[:, b:b + 1], accum_out=rsum[:, b:b + 1])
                    e.then_inc(exp_ok, 1)
                    if not (last and p == 3):
                        k_high(u + 1)
                    if p == 3 and not last:
                        q_high(g + 1)
                    if p == 0:
                        o_high(g - 1)
                    if not (last and p >= 1):
                        v_high(u + 3, (p + 3) % 4, par if p == 0 else 1 - par)
                    act.wait_ge(t_mm, u + 1)
                    act.activation(pT_hi[:, :, :].rearrange("p c n -> p (c n)"), ps[:, T_BANK, :], ACT.Copy)\
                        .then_inc(pT_hi_ok, 1)
                    if p == 1 and not last:
                        x2_high(g + 1)
                    if p == 2 and not last:
                        q_copy(g + 1)

                def first_unit(u):
                    act.wait_ge(mx_ok, u + 1)
                    for b in range(2):
                        e = act.activation(pe_[:, b, :], ps[:, S_BANK, b * M:(b + 1) * M], ACT.Exp,
                                           bias=nmx[:, b:b + 1], accum_out=rsum[:, b:b + 1])
                    e.then_inc(exp_ok, 1)
                    k_high(u + 1)
                    v_high(u + 3, 3, 0)
                    act.wait_ge(t_mm, u + 1)
                    act.activation(pT_hi[:, :, :].rearrange("p c n -> p (c n)"), ps[:, T_BANK, :], ACT.Copy)\
                        .then_inc(pT_hi_ok, 1)

                def body(g, par, last=False):
                    u, gg = UNITS * l + PAIRS * g, GROUPS * l + g
                    for p in range(1, 4):
                        unit(u + p, gg, p, par, last)
                    if not last:
                        unit(u + 4, gg + 1, 0, 1 - par)

                for mc in range(3):
                    v_high(UNITS * l + mc, mc, 0)
                k_high(UNITS * l)
                x2_high(GROUPS * l)
                q_copy(GROUPS * l)
                act.wait_ge(qb_zero, 2 * l + 2)
                q_high(GROUPS * l)
                first_unit(UNITS * l)
                with act.Fori(0, GROUPS // 2 - 1) as i:
                    body(2 * i, 0)
                    body(2 * i + 1, 1)
                body(GROUPS - 2, 0)
                body(GROUPS - 1, 1, last=True)
                o_high(GROUPS * l + GROUPS - 1)

                def x3_high(t):
                    act.wait_ge(full3_ok, NT * l + t + 1)
                    act.activation(xT3_hi[:, :, t * P:(t + 1) * P],
                                   full[:, t % 2, :].rearrange("p (k n) -> p k n", n=P), ACT.Copy)\
                        .then_inc(x3_hi_ok, 1)

                def mlp_step(j, a, s):
                    n = 32 * l + 8 * j + 4 * a + s
                    half, c = s // 2, s % 2
                    b = COL["geglu_b"] + 32 * l + 16 + 4 * j + 2 * a + c
                    wait_apart(act, u_mm, n + 1)
                    act.activation(gel[:, s % 2, :], ps[:, 2 * (s % 2) + 1, :], ACT.Gelu,
                                   bias=cols_sb[:, bass.ds(b, 1)]).then_inc(gel_ok, 1)
                    act.wait_ge(ff_ok, n + 1)
                    act.activation(f_hi[a][:, c, half * HALF:(half + 1) * HALF], ff[:, s % 2, :], ACT.Copy)\
                        .then_inc(f_hi_ok, 1)

                for t in range(4):
                    x3_high(t)
                for s in range(2):
                    mlp_step(0, 0, s)
                for t in range(4, NT):
                    x3_high(t)
                for s in range(2, 4):
                    mlp_step(0, 0, s)
                for s in range(4):
                    mlp_step(0, 1, s)
                with act.Fori(1, MG // 2) as j:
                    for a in range(2):
                        for s in range(4):
                            mlp_step(j, a, s)

            act.wait_ge(w_ok, FIRST_PIECES + PIECES * L)
            for t in range(NT):
                act.wait_ge(bnf_ok, KC + t + 1)
                act.activation(yT_hi[:, :, t * P:(t + 1) * P],
                               full[:, t % 2, :].rearrange("p (k n) -> p k n", n=P), ACT.Copy)\
                    .then_inc(y_hi, 1)
            xs_high(1)

        @block.vector
        def _(dve):
            dve.sem_inc(h_att, 1)

            def norm(k, parts):
                for n, part in enumerate(parts):
                    st = dve.bn_stats(stats[:, n, :], part)
                st.then_inc(ln, 1)
                wait_apart(dve, ln, 2 * k + 1)
                dve.bn_aggr(mv[:, :], stats[:, 0:len(parts), :].rearrange("p a s -> p (a s)"))\
                    .then_inc(ln, 1)
                dve.wait_ge(ln, 2 * k + 2)
                dve.wait_ge(rs, 2 * k + 2)

            dve.wait_ge(x_in, 16)
            for t in range(NT):
                norm(t, [h[:, t, :]])
                if t >= 2:
                    dve.wait_ge(x0_mm, t - 1)
                    dve.wait_ge(res_out[t % 2], 16 * (t // 2))
                dve.tensor_scalar(res[:, t % 2, :], h[:, t, :], mv[:, 0:1], rstd[:, 0:1],
                                  ALU.subtract, ALU.mult).then_inc(x0_ok, 1)
                dve.wait_ge(x0_ok, 2 * t + 1)
                dve.tensor_scalar(res[:, t % 2, :], res[:, t % 2, :], 0.0, None, ALU.max).then_inc(x0_ok, 1)
                dve.wait_ge(x0_ok, 2 * t + 2)
                dve.tensor_tensor(res[:, 2 + t % 2, :], res[:, t % 2, :], h[:, t, :], ALU.add)\
                    .then_inc(res_ok, 1)
            dve.wait_ge(cols_in, 16)
            dve.wait_ge(x0T_ok, NT)
            for k in range(KC):
                norm(NT + k, [x0T[:, k, 0:HALF], x0T[:, k, HALF:N]])
                sc, sh = bn[:, 2 * k:2 * k + 1], bn[:, 2 * k + 1:2 * k + 2]
                w, b = (cols_sb[:, COL[n] + k:COL[n] + k + 1] for n in ("bn_w", "bn_b"))
                dve.tensor_scalar(sc, rstd[:, :], w, None, ALU.mult).then_inc(bn_ok, 1)
                dve.wait_ge(bn_ok, 3 * k + 1)
                dve.tensor_scalar(sh, mv[:, 0:1], sc, None, ALU.mult).then_inc(bn_ok, 1)
                dve.wait_ge(bn_ok, 3 * k + 2)
                dve.tensor_tensor(sh, b, sh, ALU.subtract).then_inc(bn_ok, 1)
                dve.wait_ge(bn_ok, 3 * k + 3)
                if k:
                    dve.wait_ge(y_lo, k)
                dve.tensor_scalar(full[:, :, :].rearrange("p a n -> p (a n)"), x0T[:, k, :], sc, sh,
                                  ALU.mult, ALU.add).then_inc(bnf_ok, 1)

            dve.wait_ge(ends_in, 32)
            dve.wait_ge(iota_ok, 1)
            dve.tensor_copy(ends_f[:, :, :], ends_i[:, :, :]).then_inc(ends_ok, 1)
            dve.wait_ge(ends_ok, 1)
            for half in range(2):
                with dve.Fori(0, CHUNKS // 4) as c4:
                    for c in range(4):
                        dve.wait_ge(oh_used, CHUNKS * half + 4 * c4 + c + 1)
                        dve.tensor_scalar(oh_s[:, c, :], iota[:, :], ends_f[:, 0, bass.ds(4 * c4 + c, 1)],
                                          None, ALU.is_equal)
                        dve.tensor_scalar(oh_d[:, c, :], iota[:, half * HALF:(half + 1) * HALF],
                                          ends_f[:, 1, bass.ds(4 * c4 + c, 1)], None, ALU.is_equal)\
                            .then_inc(oh_ok, 1)
                for t in range(NT):
                    dve.wait_ge(a_hi, NT * half + t + 1)
                    dve.tensor_tensor(at_lo[:, t, half * HALF:(half + 1) * HALF], ps[:, t, :],
                                      bits(at_hi[:, t, half * HALF:(half + 1) * HALF]), ALU.subtract)\
                        .then_inc(a_lo, 1)
            dve.wait_ge(deg_mm, 1)
            dve.tensor_scalar(deg[:, :], ps[:, 0, 0:2 * NT:2], 1.0, None, ALU.add).then_inc(deg_ok, 1)
            dve.wait_ge(dinv_ok, 1)

            def gcn(use):
                for t in range(NT):
                    dve.wait_ge(g_mm, NT * use + t + 1)
                    dve.tensor_scalar(xs[:, t, :], ps[:, t, :], dinv[:, t:t + 1], None, ALU.mult)\
                        .then_inc(xs_ok, 1)
                dve.wait_ge(row_in, 16 if use == 0 else 16 * (L + 2))
                for t in range(NT):
                    dve.wait_ge(agg_mm, NT * use + t + 1)
                    dve.tensor_tensor(xs[:, t, :], ps[:, t, :], xs[:, t, :], ALU.add).then_inc(agg_s, 1)
                    dve.wait_ge(agg_s, NT * use + t + 1)
                    dve.scalar_tensor_tensor(h[:, t, :], xs[:, t, :], dinv[:, t:t + 1], bias_row[:, :],
                                             ALU.mult, ALU.add).then_inc(gcn_ok, 1)

            gcn(0)
            dve.wait_ge(gcn_ok, NT)

            with dve.Fori(0, L) as l:
                norm0 = NT + KC + 2 * NT * l

                def v_low(u, mc, slot):
                    dve.wait_ge(v_hi_ok, u + 1)
                    dve.tensor_tensor(v_lo[:, slot, mc, :], ps[:, V_BANK, :], bits(v_hi[:, slot, mc, :]),
                                      ALU.subtract).then_inc(v_ok, 1)

                def k_low(u):
                    dve.wait_ge(k_hi_ok, u + 1)
                    dve.tensor_tensor(kT_lo[:, :], ps[:, K_BANK, :], bits(kT_hi[:, :]), ALU.subtract)\
                        .then_inc(k_ok, 1)

                def x2_full(g):
                    dve.wait_ge(t2_mm, g + 1)
                    for k in range(KC):
                        last = dve.tensor_scalar(full[:, 0, k * P:(k + 1) * P], ps[:, X_BANK, k * P:(k + 1) * P],
                                                 cols_sb[:, bass.ds(COL["ln2_w"] + KC * l + k, 1)],
                                                 cols_sb[:, bass.ds(COL["ln2_b"] + KC * l + k, 1)],
                                                 ALU.mult, ALU.add)
                    last.then_inc(full2_ok, 1)

                def q_low(g):
                    dve.wait_ge(qb_hi_ok, g + 1)
                    for e in range(2):
                        r = slice(64 * e, 64 * e + 64)
                        last = dve.tensor_tensor(
                            qbd_lo[r, :, :, r], ps[r, X_BANK, :].rearrange("d (p b n) -> d p b n", p=PAIRS, b=2),
                            bits(qbd_hi[r, :, :, r]), ALU.subtract)
                    last.then_inc(qb_ok, 1)

                def o_low(g):
                    dve.wait_ge(o_hi_ok, g + 1)
                    for e in range(2):
                        r = slice(64 * e, 64 * e + 64)
                        o_ps = ps[r, PV_BANK:PV_BANK + 2, :].rearrange("d a (p b n) -> d (a p b) n", p=2, b=2)
                        last = dve.tensor_tensor(oT_lo[r, :, :].rearrange("d p (b n) -> d (p b) n", b=2),
                                                 o_ps[:, :, r],
                                                 bits(oT_hi[r, :, :]).rearrange("d p (b n) -> d (p b) n", b=2),
                                                 ALU.subtract)
                    last.then_inc(o_ok, 1)

                def softmax(u):
                    dve.wait_ge(s_mm, u + 1)
                    dve.tensor_reduce(nmx[:, :], ps[:, S_BANK, :].rearrange("p (b m) -> p b m", b=2),
                                      AX.X, ALU.max, negate=True).then_inc(mx_ok, 1)
                    dve.wait_ge(exp_ok, u + 1)
                    dve.reciprocal(rinv[:, :], rsum[:, :]).then_inc(rinv_ok, 1)
                    dve.wait_ge(rinv_ok, u + 1)
                    for b in range(2):
                        last = dve.tensor_scalar(pn[:, b, :], pe_[:, b, :], rinv[:, b:b + 1], None, ALU.mult)
                    last.then_inc(pn_ok, 1)

                def unit(u, g, p, par, last=False, first=False):
                    softmax(u)
                    if not (last and p == 3):
                        k_low(u + 1)
                    if p == 3 and not last:
                        q_low(g + 1)
                    if p == 0 and not first:
                        o_low(g - 1)
                    if not (last and p >= 1):
                        v_low(u + 3, (p + 3) % 4, par if p == 0 else 1 - par)
                    dve.wait_ge(pT_hi_ok, u + 1)
                    dve.tensor_tensor(pT_lo[:, :, :].rearrange("p c n -> p (c n)"), ps[:, T_BANK, :],
                                      bits(pT_hi[:, :, :].rearrange("p c n -> p (c n)")), ALU.subtract)\
                        .then_inc(pT_ok, 1)
                    if p == 1 and not last:
                        x2_full(g + 1)

                def residual(g):
                    gg = GROUPS * l + g
                    dve.wait_ge(wo_mm, gg + 1)
                    dve.tensor_tensor(h[:, g, :], h[:, g, :], ps[:, Y_BANK, :], ALU.add).then_inc(h_att, 1)
                    wait_apart(dve, h_att, gg + 2)
                    norm(norm0 + 2 * g + 2 if not isinstance(g, int) or g < NT - 1 else norm0 + 2 * NT - 1,
                         [h[:, g, :]])
                    dve.tensor_scalar(z3[:, g, :], h[:, g, :], mv[:, 0:1], rstd[:, 0:1],
                                      ALU.subtract, ALU.mult).then_inc(z3_ok, 1)
                    dve.wait_ge(z3_ok, gg + 1)
                    dve.tensor_tensor(h[:, g, :], h[:, g, :], bias_row[:, :], ALU.add).then_inc(h_bias, 1)

                def ln2(g, k):
                    norm(norm0 + k, [h[:, g, :]])
                    dve.tensor_scalar(z2[:, :], h[:, g, :], mv[:, 0:1], rstd[:, 0:1],
                                      ALU.subtract, ALU.mult).then_inc(z2_ok, 1)

                def body(g, par, last=False):
                    u, gg = UNITS * l + PAIRS * g, GROUPS * l + g
                    if not last:
                        ln2(g + 1, 2 * g + 1)
                    for p in range(1, 4):
                        unit(u + p, gg, p, par, last)
                    if not last:
                        unit(u + 4, gg + 1, 0, 1 - par)
                    else:
                        o_low(gg)
                    residual(g)

                dve.wait_ge(row_in, 16 * l + 32)
                ln2(0, 0)
                for mc in range(3):
                    v_low(UNITS * l + mc, mc, 0)
                k_low(UNITS * l)
                x2_full(GROUPS * l)
                q_low(GROUPS * l)
                unit(UNITS * l, GROUPS * l, 0, 0, first=True)
                with dve.Fori(0, GROUPS // 2 - 1) as i:
                    body(2 * i, 0)
                    body(2 * i + 1, 1)
                body(GROUPS - 2, 0)
                body(GROUPS - 1, 1, last=True)

                def x3_full(t):
                    dve.wait_ge(t3_mm, NT * l + t + 1)
                    dve.wait_ge(x3_ok, NT * l + t + 1)
                    for k in range(KC):
                        last = dve.tensor_scalar(full[:, t % 2, k * P:(k + 1) * P],
                                                 ps[:, 4 + t % 3, k * P:(k + 1) * P],
                                                 cols_sb[:, bass.ds(COL["ln3_w"] + KC * l + k, 1)],
                                                 cols_sb[:, bass.ds(COL["ln3_b"] + KC * l + k, 1)],
                                                 ALU.mult, ALU.add)
                    last.then_inc(full3_ok, 1)

                def mlp_step(j, a, s):
                    n = 32 * l + 8 * j + 4 * a + s
                    c = s % 2
                    dve.wait_ge(f_ok, n + 1)
                    dve.wait_ge(gel_ok, n + 1)
                    dve.scalar_tensor_tensor(
                        ff[:, s % 2, :], ps[:, 2 * (s % 2), :],
                        cols_sb[:, bass.ds(COL["geglu_b"] + 32 * l + 4 * j + 2 * a + c, 1)],
                        gel[:, s % 2, :], ALU.add, ALU.mult).then_inc(ff_ok, 1)

                def mlp_add(j, a):
                    for t in range(NT):
                        dve.wait_ge(ffo_mm, 64 * l + 16 * j + 8 * a + t + 1)
                        dve.tensor_tensor(h[:, t, :], h[:, t, :], ps[:, 4 + t % 4, :], ALU.add)\
                            .then_inc(h_ffo, 1)

                for t in range(4):
                    x3_full(t)
                for s in range(2):
                    mlp_step(0, 0, s)
                for t in range(4, NT):
                    x3_full(t)
                for s in range(2, 4):
                    mlp_step(0, 0, s)
                for s in range(4):
                    mlp_step(0, 1, s)
                mlp_add(0, 0)
                with dve.Fori(1, MG // 2) as j:
                    for s in range(4):
                        mlp_step(j, 0, s)
                    mlp_add(j - 1, 1)
                    for s in range(4):
                        mlp_step(j, 1, s)
                    mlp_add(j, 0)
                mlp_add(MG // 2 - 1, 1)
                dve.wait_ge(h_ffo, 64 * l + 64)

            for t in range(NT):
                dve.wait_ge(hT_mm, t + 1)
                if t >= 2:
                    dve.wait_ge(y_lo, KC + t - 1)
                dve.tensor_copy(full[:, t % 2, :], ps[:, t, :]).then_inc(bnf_ok, 1)
            gcn(1)
            for t in range(NT):
                dve.wait_ge(gcn_ok, NT + t + 1)
                dve.wait_ge(res_in[t % 2], 16 * (t // 2 + 1))
                dve.tensor_tensor(h[:, t, :], h[:, t, :], res[:, t % 2, :], ALU.add).then_inc(res_ok, 1)

        @block.tensor
        def _(pe):
            def product(bank, steps):
                n = len(steps)
                for i, (l_hi, l_lo, r_hi, r_lo) in enumerate(steps):
                    pe.matmul(bank, l_hi, r_hi, start=(i == 0), stop=False)
                    pe.matmul(bank, l_hi, r_lo, start=False, stop=False)
                    last = pe.matmul(bank, l_lo, r_hi, start=False, stop=(i == n - 1))
                return last

            pe.sem_inc(oh_used, 4)
            pe.wait_ge(const_ok, 4)
            for t in range(NT):
                pe.wait_ge(x0_ok, 2 * t + 2)
                if t >= 2:
                    pe.wait_ge(x0T_ok, t - 1)
                for k in range(KC):
                    last = pe.transpose(ps[:, t % 2, k * P:(k + 1) * P], res[:, t % 2, k * P:(k + 1) * P],
                                        ident[:, :])
                last.then_inc(x0_mm, 1)
            pe.wait_ge(x0T_ok, NT)

            for half in range(2):
                for t in range(NT):
                    if half:
                        pe.wait_ge(a_lo, t + 1)
                    pe.matmul(ps[:, t, :], zeros[:, 0:P], zeros[:, :], start=True, stop=False)
                with pe.Fori(0, CHUNKS // 4) as c4:
                    for c in range(4):
                        pe.wait_ge(oh_ok, CHUNKS * half + 4 * c4 + c + 1)
                        for t in range(NT):
                            last = pe.matmul(ps[:, t, :], oh_s[:, c, t * P:(t + 1) * P], oh_d[:, c, :],
                                             start=False, stop=False)
                        last.then_inc(oh_used, 1)
                for t in range(NT):
                    pe.matmul(ps[:, t, :], zeros[:, 0:P], zeros[:, :], start=False, stop=True).then_inc(a_mm, 1)
            pe.wait_ge(a_lo, 2 * NT)
            pe.wait_ge(ones_ok, 1)
            for t in range(NT):
                for st in range(NT):
                    for part in (at_hi, at_lo):
                        last = pe.matmul(ps[:, 0, 2 * t:2 * t + 2], part[:, st, t * P:(t + 1) * P], ones[:, :],
                                         start=(st == 0 and part is at_hi),
                                         stop=(st == NT - 1 and part is at_lo))
            last.then_inc(deg_mm, 1)
            pe.wait_ge(deg_ok, 1)

            def gcn(use):
                for t in range(NT):
                    r = slice(t * P, (t + 1) * P)
                    product(ps[:, t, :], [(yT_hi[:, k, r], yT_lo[:, k, r], w_hi[:, 0, k, :], w_lo[:, 0, k, :])
                                          for k in range(KC)]).then_inc(g_mm, 1)
                if use:
                    pe.wait_ge(at_in, 32)
                pe.wait_ge(xs_lo_ok, NT * use + NT)
                for t in range(NT):
                    r = slice(t * P, (t + 1) * P)
                    product(ps[:, t, :], [(at_hi[:, s, r], at_lo[:, s, r], xs_hi[:, s, :], xs_lo[:, s, :])
                                          for s in range(NT)]).then_inc(agg_mm, 1)

            pe.wait_ge(y_lo, KC)
            pe.wait_ge(w_ok, 2)
            gcn(0)

            with pe.Fori(0, L) as l:
                def k_product(u, p, slot):
                    r = slice(p * P, (p + 1) * P)
                    product(ps[:, K_BANK, :], [(w_hi[:, 1, k, r], w_lo[:, 1, k, r],
                                                cond_hi[:, slot, k, :], cond_lo[:, slot, k, :])
                                               for k in range(KC)]).then_inc(k_mm, 1)

                def v_product(u, mc, slot):
                    if u is not None:
                        pe.wait_ge(v_ok, u)
                    r = slice(mc * P, (mc + 1) * P)
                    product(ps[:, V_BANK, :], [(cond_hi[:, slot, k, r], cond_lo[:, slot, k, r],
                                                w_hi[:, 2, k, :], w_lo[:, 2, k, :])
                                               for k in range(KC)]).then_inc(v_mm, 1)

                def s_product(u, g, p):
                    pe.wait_ge(k_ok, u + 1)
                    if p == 0:
                        pe.wait_ge(qb_ok, g + 1)
                    for b in range(2):
                        r = slice(b * M, (b + 1) * M)
                        last = product(ps[:, S_BANK, r], [(qbd_hi[:, p, b, :], qbd_lo[:, p, b, :],
                                                           kT_hi[:, r], kT_lo[:, r])])
                    last.then_inc(s_mm, 1)

                def p_transpose(u):
                    pe.wait_ge(pn_ok, u + 1)
                    for b in range(2):
                        for c in range(2):
                            i = 2 * b + c
                            last = pe.transpose(ps[:, T_BANK, i * P:(i + 1) * P], pn[:, b, c * P:(c + 1) * P],
                                                ident[:, :])
                    last.then_inc(t_mm, 1)

                def pv_product(u, p, slot):
                    pe.wait_ge(pT_ok, u + 1)
                    bank = PV_BANK + p // 2
                    for b in range(2):
                        at = (p % 2) * 2 * P + b * P
                        last = product(ps[:, bank, at:at + P],
                                       [(v_hi[:, slot, 2 * b + c, p * P:(p + 1) * P],
                                         v_lo[:, slot, 2 * b + c, p * P:(p + 1) * P],
                                         pT_hi[:, 2 * b + c, :], pT_lo[:, 2 * b + c, :]) for c in range(2)])
                    last.then_inc(pv_mm, 1)

                def t2(g):
                    pe.wait_ge(z2_ok, g + 1)
                    for k in range(KC):
                        last = pe.transpose(ps[:, X_BANK, k * P:(k + 1) * P], z2[:, k * P:(k + 1) * P], ident[:, :])
                    last.then_inc(t2_mm, 1)

                def q_product(g, first=False):
                    pe.wait_ge(x2_ok, g + 1)
                    if not first:
                        pe.wait_ge(h_att, g)
                    product(ps[:, Y_BANK, :], [(xT2_hi[:, k, :], xT2_lo[:, k, :], w_hi[:, 0, k, :], w_lo[:, 0, k, :])
                                               for k in range(KC)]).then_inc(q_mm, 1)

                def q_transpose(g):
                    pe.wait_ge(q_ok, g + 1)
                    for p in range(PAIRS):
                        last = pe.transpose(ps[:, X_BANK, p * P:(p + 1) * P], q_sb[:, p * P:(p + 1) * P], ident[:, :])
                    last.then_inc(qt_mm, 1)

                def wo_product(g):
                    pe.wait_ge(o_ok, g + 1)
                    product(ps[:, Y_BANK, :], [(oT_hi[:, p, :], oT_lo[:, p, :], w_hi[:, 3, p, :], w_lo[:, 3, p, :])
                                               for p in range(PAIRS)]).then_inc(wo_mm, 1)

                def unit(u, g, p, par, last=False, first=False):
                    if not (last and p == 3):
                        k_product(u + 1, (p + 1) % 4, par if p < 3 else 1 - par)
                    if p == 3 and not last:
                        q_transpose(g + 1)
                    if not first:
                        pv_product(u - 1, (p + 3) % 4, par if p else 1 - par)
                    if not (last and p >= 1):
                        v_product(u + 3, (p + 3) % 4, par if p == 0 else 1 - par)
                    p_transpose(u)
                    if not (last and p == 3):
                        s_product(u + 1, g if p < 3 else g + 1, (p + 1) % 4)
                    if p == 1 and not last:
                        t2(g + 1)
                    if p == 2 and not last:
                        q_product(g + 1)

                def body(g, i, par, last=False):
                    u, gg = UNITS * l + PAIRS * g, GROUPS * l + g
                    if not last:
                        pe.wait_ge(cond_in[1 - par], 128 * l + 32 * (i + 1 + par))
                    for p in range(1, 4):
                        unit(u + p, gg, p, par, last)
                    if not last:
                        unit(u + 4, gg + 1, 0, 1 - par)
                    else:
                        pv_product(u + 3, 3, par)
                    wo_product(gg)

                pe.wait_ge(w_ok, PIECES * l + FIRST_PIECES)
                pe.wait_ge(cond_in[0], 128 * l + 32)
                for mc in range(3):
                    v_product(UNITS * l + mc if mc else None, mc, 0)
                k_product(UNITS * l, 0, 0)
                t2(GROUPS * l)
                q_product(GROUPS * l, first=True)
                q_transpose(GROUPS * l)
                s_product(UNITS * l, GROUPS * l, 0)
                unit(UNITS * l, GROUPS * l, 0, 0, first=True)
                with pe.Fori(0, GROUPS // 2 - 1) as i:
                    body(2 * i, i, 0)
                    body(2 * i + 1, i, 1)
                body(GROUPS - 2, GROUPS // 2 - 1, 0)
                body(GROUPS - 1, GROUPS // 2 - 1, 1, last=True)

                def t3(t):
                    pe.wait_ge(z3_ok, NT * l + t + 1)
                    if t >= 3:
                        pe.wait_ge(full3_ok, NT * l + t - 2)
                    for k in range(KC):
                        last = pe.transpose(ps[:, 4 + t % 3, k * P:(k + 1) * P], z3[:, t, k * P:(k + 1) * P],
                                            ident[:, :])
                    last.then_inc(t3_mm, 1)

                def mlp_step(j, a, s, first=False):
                    half, c = s // 2, s % 2
                    if not (first and s < 2):
                        pe.wait_ge(ff_ok, 32 * l + 8 * j + 4 * a + s - 1)
                    for v in range(2):
                        last = product(ps[:, 2 * (s % 2) + v, :],
                                       [(wg_hi[:, a, k, v, c * P:(c + 1) * P], wg_lo[:, a, k, v, c * P:(c + 1) * P],
                                         xT3_hi[:, k, half * HALF:(half + 1) * HALF],
                                         xT3_lo[:, k, half * HALF:(half + 1) * HALF]) for k in range(KC)])
                    last.then_inc(u_mm, 1)

                def mlp_up(j, a):
                    pe.wait_ge(w_ok, FIRST_PIECES + PIECES * l + 8 * j + 4 * a + 2)
                    for s in range(4):
                        mlp_step(j, a, s)

                def mlp_down(j, a, first=False):
                    pe.wait_ge(w_ok, FIRST_PIECES + PIECES * l + 8 * j + 4 * a + 3)
                    pe.wait_ge(f_ok, 2 + 32 * l + 8 * j + 4 * a + 4)
                    for t in range(NT):
                        if not (first and t < 4):
                            pe.wait_ge(h_ffo, 64 * l + 16 * j + 8 * a + t - 3)
                        r = slice(t * P, (t + 1) * P)
                        product(ps[:, 4 + t % 4, :], [(f_hi[a][:, c, r], f_lo[a][:, c, r],
                                                       wf_hi[:, a, c, :], wf_lo[:, a, c, :])
                                                      for c in range(2)]).then_inc(ffo_mm, 1)

                for t in range(4):
                    t3(t)
                pe.wait_ge(w_ok, FIRST_PIECES + PIECES * l + 2)
                pe.wait_ge(x3_ok, 2 + NT * l + 4)
                for s in range(2):
                    mlp_step(0, 0, s, first=True)
                for t in range(4, NT):
                    t3(t)
                pe.wait_ge(x3_ok, 2 + NT * l + NT)
                for s in range(2, 4):
                    mlp_step(0, 0, s, first=True)
                mlp_up(0, 1)
                mlp_down(0, 0, first=True)
                with pe.Fori(1, MG // 2) as j:
                    mlp_up(j, 0)
                    mlp_down(j - 1, 1)
                    mlp_up(j, 1)
                    mlp_down(j, 0)
                mlp_down(MG // 2 - 1, 1)
                pe.wait_ge(h_ffo, 64 * l + 64)

            for t in range(NT):
                for k in range(KC):
                    last = pe.transpose(ps[:, t, k * P:(k + 1) * P], h[:, t, k * P:(k + 1) * P], ident[:, :])
                last.then_inc(hT_mm, 1)
            pe.wait_ge(y_lo, KC + NT)
            pe.wait_ge(w_ok, FIRST_PIECES + PIECES * L)
            gcn(1)


def _arrays(inputs):
    import numpy as np

    a = {n.replace("L0_gnn_", ""): np.asarray(v) for n, v in inputs.items()}
    D = a["x"].shape[1]
    P, L = 128, a["Wq"].shape[0]

    def square(w):
        return list(w.reshape(2, 2, P, D).transpose(0, 2, 1, 3).reshape(2, P, 1024))

    attention = [[square(a[n][l]) for n in ("Wq", "Wk", "Wv", "Wo")] for l in range(L)]
    attention.append([square(a["gcn_out_w"])] * 4)
    pieces = square(a["gcn_in_w"]) + [p for m in attention[0] for p in m]
    for l in range(L):
        up = a["geglu_w"][l].reshape(2, 2, P, 2, 8, 256).transpose(4, 0, 2, 1, 3, 5).reshape(8, 2, P, 1024)
        down = a["ffo_w"][l].reshape(8, 2, P, D).transpose(0, 2, 1, 3).reshape(8, P, 1024)
        for q in range(8):
            pieces += [up[q, 0], up[q, 1], down[q], attention[l + 1][q // 2][q % 2]]
    cond = a["cond"].reshape(8, 512, 4, P).transpose(0, 3, 2, 1)
    vectors = [a["bn_w"][None], a["bn_b"][None], a["ln2_w"], a["ln2_b"], a["ln3_w"], a["ln3_b"], a["geglu_b"]]
    cols = np.concatenate([v.reshape(-1, P) for v in vectors]).T
    rows = np.concatenate([a["gcn_in_b"][None], a["ffo_b"], a["gcn_out_b"][None]])
    return {"x": a["x"], "src": a["src"].reshape(P, -1), "dst": a["dst"].reshape(P, -1), "condT": cond,
            "pieces": np.stack(pieces), "cols": cols, "rows": rows}


def kernel(**inputs):
    import numpy as np
    import concourse.bacc as bacc
    from concourse.bass_utils import run_bass_kernel_spmd

    nc = bacc.Bacc("TRN2", target_bir_lowering=False, num_devices=1, dynamic_dma_scratch_size=1024)
    arrays, args = {}, []
    for name, a in _arrays(inputs).items():
        a = np.ascontiguousarray(a)
        arrays[f"in_{name}"] = a
        args.append(nc.dram_tensor(f"in_{name}", a.shape, mybir.dt.from_np(a.dtype), kind="ExternalInput").ap())
    n, d = inputs["x"].shape
    args.append(nc.dram_tensor("out", (n, d), mybir.dt.float32, kind="ExternalOutput").ap())
    gnn_preln_kernel(nc, *args)
    r = run_bass_kernel_spmd(nc, [arrays], core_ids=[0])
    return np.asarray(r.results[0]["out"])
```

```python
import concourse.bass as bass
from concourse import mybir
from contextlib import ExitStack


def gnn_preln_kernel(
    nc: bass.Bass,
    x: bass.AP,
    src: bass.AP,
    dst: bass.AP,
    condT: bass.AP,
    pieces: bass.AP,
    cols: bass.AP,
    rows: bass.AP,
    out: bass.AP,
):
    f32 = mybir.dt.float32
    f32r = mybir.dt.float32r
    f16 = mybir.dt.float16
    i32 = mybir.dt.int32
    ALU = mybir.AluOpType
    ACT = mybir.ActivationFunctionType
    AX = mybir.AxisListType

    P = 128
    N, D = x.shape
    NT, KC = N // P, D // P
    GROUPS = condT.shape[0]
    M = condT.shape[3] // 2
    PAIRS = 4
    E = src.shape[0] * src.shape[1]
    CHUNKS = E // P
    HALF = N // 2
    L = (pieces.shape[0] - 10) // 32
    UNITS = GROUPS * PAIRS
    MG = 8
    PIECES = 4 * MG
    FIRST_PIECES = 10
    COL = {"bn_w": 0, "bn_b": 4, "ln2_w": 8, "ln2_b": 24, "ln3_w": 40, "ln3_b": 56, "geglu_b": 72}
    EPS = 1e-5
    DIGIT, OFFSET, FLUSH = 8192.0, 2.0 ** 24, 32
    SHIFT = 256.0
    ROUND = 1.5 * 2.0 ** 23
    Q_SCALE = 0.125
    FLUSHES = CHUNKS // FLUSH
    assert NT == GROUPS and L * 32 == 128 and FLUSH == 4 * NT and CHUNKS == FLUSH * FLUSHES
    assert FLUSH * P * DIGIT == 2 * OFFSET and FLUSH * P * 2 == DIGIT and P * SHIFT * 2 * SHIFT == OFFSET

    with ExitStack() as ctx:
        def sb(name, shape, dt, where=ctx):
            return where.enter_context(nc.sbuf_tensor(name, shape, dt))

        def sem(name):
            return ctx.enter_context(nc.semaphore(name))

        h = sb("h", [P, NT, D], f32)
        w_hi = sb("w_hi", [P, 4, KC, D], f32r)
        w_lo = sb("w_lo", [P, 4, KC, D], f32r)
        stage = sb("stage", [P, 2, 1024], f32)
        oT_hi = sb("oT_hi", [P, PAIRS, P], f32r)
        oT_lo = sb("oT_lo", [P, PAIRS, P], f32r)
        full = sb("full", [P, 2, D], f32)
        bias_row = sb("bias_row", [P, D], f32)
        cols_sb = sb("cols_sb", [P, cols.shape[1]], f32)
        ident = sb("ident", [P, P], f32)
        mhalf = sb("mhalf", [P, NT], f32)
        ones = sb("ones", [P, 2], f32r)
        stats = sb("stats", [P, 2, 6], f32)
        mv = sb("mv", [P, 2], f32)
        veps = sb("veps", [P, 1], f32)
        rstd = sb("rstd", [P, 1], f32)
        nmx = sb("nmx", [P, 2], f32)
        rsum = sb("rsum", [P, 2], f32)
        rinv = sb("rinv", [P, 2], f32)
        deg = sb("deg", [P, NT], f32)
        dinv = sb("dinv", [P, NT], f32)
        bn = sb("bn", [P, 8], f32)
        x_stats = sb("x_stats", [P, NT, 6], f32)
        x_mv = sb("x_mv", [P, NT, 2], f32)
        x_veps = sb("x_veps", [P, NT], f32)
        x_rstd = sb("x_rstd", [P, NT], f32)

        def overlay(*uses):
            made = []
            for use in uses:
                with ExitStack() as where:
                    made.append([sb(*one, where) for one in use])
            big = max(sum(size(one) for one in use) for use in uses)
            ctx.enter_context(nc.sbuf_tensor(f"room_of_{uses[0][0][0]}", [P, big], mybir.dt.int8))
            return made

        def size(one):
            n = 2 if one[2] == f16 else 4
            for d in one[1][1:]:
                n *= d
            return n

        (at_hi,), cond, xT3 = overlay(
            [("at_hi", [P, NT, N], f32r)],
            [(f"cond{s}_{part}", [P, KC, 2 * M], f32r) for s in range(2) for part in ("hi", "lo")],
            [(f"xT3{s}_{part}", [P, KC, HALF], f32r) for s in range(2) for part in ("hi", "lo")])
        cond_hi, cond_lo, xT3_hi, xT3_lo = cond[0::2], cond[1::2], xT3[0::2], xT3[1::2]
        (at_lo,), (counts,), (z1, x1), (v_hi, v_lo), (wg_hi, wg_lo) = overlay(
            [("at_lo", [P, NT, N], f32r)],
            [("counts", [P, NT, N], f32)],
            [("z1", [P, NT, D], f32), ("x1", [P, NT, D], f32)],
            [("v_hi", [P, 2, 4, D], f32r), ("v_lo", [P, 2, 4, D], f32r)],
            [("wg_hi", [P, 2, KC, 2, 256], f32r), ("wg_lo", [P, 2, KC, 2, 256], f32r)])
        (x0T,), (sums,), (xs,), (kT_hi, kT_lo, pT_hi, pT_lo), (wf_hi, wf_lo) = overlay(
            [("x0T", [P, KC, N], f32)],
            [("sums", [P, NT, HALF], f32)],
            [("xs", [P, NT, D], f32)],
            [("kT_hi", [P, 2 * M], f32r), ("kT_lo", [P, 2 * M], f32r),
             ("pT_hi", [P, 4, P], f32r), ("pT_lo", [P, 4, P], f32r)],
            [("wf_hi", [P, 2, 2, D], f32r), ("wf_lo", [P, 2, 2, D], f32r)])
        (oh_s, oh_d, iota, shift, minus, zeros), (xs_hi,), (pe_, pn, q_sb, z2, xT2_hi, xT2_lo), (f0_hi, f0_lo) = overlay(
            [("oh_s", [P, 4, N], f16), ("oh_d", [P, 4, HALF], f16), ("iota", [P, N], f16),
             ("shift", [P, HALF], f16), ("minus", [P, P], f16), ("zeros", [P, P], f16)],
            [("xs_hi", [P, NT, D], f32r)],
            [("p_exp", [P, 2, M], f32), ("p_norm", [P, 2, M], f32), ("q_sb", [P, D], f32),
             ("z2", [P, D], f32), ("xT2_hi", [P, KC, P], f32r), ("xT2_lo", [P, KC, P], f32r)],
            [("f0_hi", [P, 2, N], f32r), ("f0_lo", [P, 2, N], f32r)])
        (c_in,), (xs_lo,), (z3,), (f1_hi, f1_lo) = overlay(
            [("c_in", [P, 2, KC * 2 * M], f32)],
            [("xs_lo", [P, NT, D], f32r)],
            [("z3", [P, NT, D], f32)],
            [("f1_hi", [P, 2, N], f32r), ("f1_lo", [P, 2, N], f32r)])
        (ends_i, ends_f), (res,), (qbd_hi, qbd_lo), (gel, ff) = overlay(
            [("ends_i", [P, 2, CHUNKS], i32), ("ends_f", [P, 4, CHUNKS], f32)],
            [("res", [P, 4, D], f32)],
            [("qbd_hi", [P, PAIRS, 2, P], f32r), ("qbd_lo", [P, PAIRS, 2, P], f32r)],
            [("gel", [P, 2, D], f32), ("ff", [P, 2, D], f32)])

        yT_hi = w_hi[:, 1:3].rearrange("p a c n -> p (a c n)").rearrange("p (k n) -> p k n", n=N)
        yT_lo = w_lo[:, 1:3].rearrange("p a c n -> p (a c n)").rearrange("p (k n) -> p k n", n=N)
        f_hi, f_lo = [f0_hi, f1_hi], [f0_lo, f1_lo]

        ps = ctx.enter_context(nc.psum_tensor("ps", [P, 8, 512], f32))
        K_BANK, V_BANK, S_BANK, T_BANK, PV_BANK, X_BANK, Y_BANK = 0, 1, 2, 3, 4, 6, 7

        cond_s = [nc.dram_tensor(f"cond_{part}_s", [GROUPS, P, KC * 2 * M], f32, kind="Internal").ap()
                  for part in ("hi", "lo")]
        at_s = [nc.dram_tensor(f"at_{part}_s", [P, NT * N], f32, kind="Internal").ap()
                for part in ("hi", "lo")]
        res_s = nc.dram_tensor("res_s", [N, D], f32, kind="Internal").ap()

        x_in = [sem("x_in0"), sem("x_in1")]
        cols_in, ends_in, row_in = sem("cols_in"), sem("ends_in"), sem("row_in")
        stage_in = [sem("stage_in0"), sem("stage_in1")]
        c_in_in = [sem("c_in_in0"), sem("c_in_in1")]
        cond_out = [sem("cond_out0"), sem("cond_out1")]
        cond_in = [sem("cond_in0"), sem("cond_in1")]
        res_out = [sem("res_out0"), sem("res_out1")]
        res_in = [sem("res_in0"), sem("res_in1")]
        at_out, at_in, out_done = sem("at_out"), sem("at_in"), sem("out_done")
        waited = sem("waited")
        const_ok, ones_ok, iota_ok, ends_ok = sem("const_ok"), sem("ones_ok"), sem("iota_ok"), sem("ends_ok")
        ln = sem("ln")
        rs = sem("rs")
        x_ln, x_rs, x1_ok = sem("x_ln"), sem("x_rs"), sem("x1_ok")
        x0_ok, res_ok, x0_mm, x0T_ok = sem("x0_ok"), sem("res_ok"), sem("x0_mm"), sem("x0T_ok")
        bn_ok, bnf_ok, y_hi, y_lo = sem("bn_ok"), sem("bnf_ok"), sem("y_hi"), sem("y_lo")
        c_hi, c_lo = sem("c_hi"), sem("c_lo")
        oh_ok, oh_used, a_mm, a_hi, a_lo = sem("oh_ok"), sem("oh_used"), sem("a_mm"), sem("a_hi"), sem("a_lo")
        a_sums, a_round, a_digit, a_low, a_dec = (sem("a_sums"), sem("a_round"), sem("a_digit"),
                                                  sem("a_low"), sem("a_dec"))
        row_mm, row_ok = sem("row_mm"), sem("row_ok")
        deg_mm, deg_ok, dinv_ok = sem("deg_mm"), sem("deg_ok"), sem("dinv_ok")
        g_mm, xs_ok, xs_hi_ok, xs_lo_ok, agg_mm, agg_s, gcn_ok = (
            sem("g_mm"), sem("xs_ok"), sem("xs_hi_ok"), sem("xs_lo_ok"), sem("agg_mm"), sem("agg_s"),
            sem("gcn_ok"))
        hT_mm = sem("hT_mm")
        w_hi_ok, w_ok = sem("w_hi_ok"), sem("w_ok")
        k_mm, k_hi_ok, k_ok = sem("k_mm"), sem("k_hi_ok"), sem("k_ok")
        v_mm, v_hi_ok, v_ok = sem("v_mm"), sem("v_hi_ok"), sem("v_ok")
        s_mm, mx_ok, exp_ok, rinv_ok, pn_ok = (sem("s_mm"), sem("mx_ok"), sem("exp_ok"), sem("rinv_ok"),
                                               sem("pn_ok"))
        t_mm, pT_hi_ok, pT_ok, pv_mm = sem("t_mm"), sem("pT_hi_ok"), sem("pT_ok"), sem("pv_mm")
        z2_ok, t2_mm, full2_ok, x2_hi_ok, x2_ok = (sem("z2_ok"), sem("t2_mm"), sem("full2_ok"),
                                                   sem("x2_hi_ok"), sem("x2_ok"))
        q_mm, q_ok, qt_mm, qb_hi_ok, qb_ok, qb_zero = (sem("q_mm"), sem("q_ok"), sem("qt_mm"),
                                                       sem("qb_hi_ok"), sem("qb_ok"), sem("qb_zero"))
        o_hi_ok, o_ok, wo_mm, h_att, z3_ok, h_bias = (sem("o_hi_ok"), sem("o_ok"), sem("wo_mm"),
                                                      sem("h_att"), sem("z3_ok"), sem("h_bias"))
        t3_mm, full3_ok, x3_hi_ok, x3_ok = sem("t3_mm"), sem("full3_ok"), sem("x3_hi_ok"), sem("x3_ok")
        u_mm, gel_ok, ff_ok, f_hi_ok, f_ok, ffo_mm, h_ffo = (
            sem("u_mm"), sem("gel_ok"), sem("ff_ok"), sem("f_hi_ok"), sem("f_ok"), sem("ffo_mm"),
            sem("h_ffo"))

        block = ctx.enter_context(nc.Block())

        def wait_apart(eng, on, value):
            eng.wait_ge(on, value)
            eng.sem_inc(waited, 1)

        def bits(ap):
            return ap.bitcast(f32)

        T3_BANK = [1, 6, 1, 6, 4, 5, 6, 4]

        def attn_place(part, which, half):
            return (w_hi, w_lo)[part][:, which, 2 * half:2 * half + 2, :].rearrange("p k n -> p (k n)")

        def up_place(part, a, r):
            return (wg_hi, wg_lo)[part][:, a, 2 * r:2 * r + 2].rearrange("p k v n -> p (k v n)")

        def mlp_place(part, j, a, s):
            if s == 0:
                return (wf_hi, wf_lo)[part][:, a].rearrange("p c n -> p (c n)")
            if s == 3 or (isinstance(j, int) and 2 * j + a == MG - 1):
                return attn_place(part, j, a)
            return up_place(part, 1 - a, s - 1)

        @block.sync
        def _(sp):
            sp.dma_start(ends_i[:, 0, :], src).then_inc(ends_in, 16)
            sp.dma_start(ends_i[:, 1, :], dst).then_inc(ends_in, 16)
            for half in range(2):
                r = slice(half * NT // 2, (half + 1) * NT // 2)
                sp.dma_start(h[:, r, :], x.rearrange("(t p) d -> p t d", p=P)[:, r, :]).then_inc(x_in[half], 16)
            sp.dma_start(cols_sb[:, :], cols).then_inc(cols_in, 16)
            sp.dma_start(bias_row[:, :], rows[0:1, :].partition_broadcast(P)).then_inc(row_in, 16)

            def piece(n, slot, first=False):
                if not first:
                    sp.wait_ge(w_ok, n - 1)
                sp.dma_start(stage[:, slot, :], pieces[n]).then_inc(stage_in[slot], 16)

            piece(0, 0, True)
            piece(1, 1, True)
            sp.dma_start(c_in[:, 0, :], condT[0].rearrange("p k n -> p (k n)")).then_inc(c_in_in[0], 16)
            for g in range(GROUPS):
                s = g % 2
                if g + 1 < GROUPS:
                    if g:
                        sp.wait_ge(c_lo, g)
                    sp.dma_start(c_in[:, 1 - s, :], condT[g + 1].rearrange("p k n -> p (k n)"))\
                      .then_inc(c_in_in[1 - s], 16)
                sp.wait_ge(c_lo, g + 1)
                for part, buf in zip(cond_s, (cond_hi, cond_lo)):
                    sp.dma_start(part[g], bits(buf[s][:, :, :].rearrange("p k n -> p (k n)"))).then_inc(cond_out[s], 16)
                if g == 3:
                    for half in range(2):
                        r = slice(half * NT // 2, (half + 1) * NT // 2)
                        sp.wait_ge(x1_ok, (half + 1) * NT // 2)
                        sp.dma_start(res_s.rearrange("(t p) d -> p t d", p=P)[:, r, :], x1[:, r, :])\
                          .then_inc(res_out[half], 16)
            sp.wait_ge(a_lo, NT)
            for part, buf in zip(at_s, (at_hi, at_lo)):
                sp.dma_start(part, bits(buf[:, :, :].rearrange("p t n -> p (t n)"))).then_inc(at_out, 16)
            for n in range(2, FIRST_PIECES):
                piece(n, n % 2)
            sp.wait_ge(gcn_ok, NT)
            sp.dma_start(bias_row[:, :], rows[1:2, :].partition_broadcast(P)).then_inc(row_in, 16)
            sp.wait_ge(agg_mm, NT)
            sp.wait_ge(at_out, 32)

            def load_cond(g, slot):
                for part, buf in zip(cond_s, (cond_hi, cond_lo)):
                    sp.dma_start(bits(buf[slot][:, :, :].rearrange("p k n -> p (k n)")), part[g])\
                      .then_inc(cond_in[slot], 16)

            load_cond(0, 0)
            load_cond(1, 1)
            with sp.Fori(0, L) as l:
                with sp.Fori(1, GROUPS // 2) as i:
                    for a in range(2):
                        sp.wait_ge(k_mm, UNITS * l + 2 * PAIRS * i + PAIRS * (a - 1))
                        load_cond(2 * i + a, a)
                with sp.Fori(0, MG // 2) as j:
                    for a in range(2):
                        for r in range(4):
                            n = FIRST_PIECES + PIECES * l + 8 * j + 4 * a + r
                            sp.wait_ge(w_ok, n - 1)
                            sp.dma_start(stage[:, r % 2, :], pieces[n]).then_inc(stage_in[r % 2], 16)
                sp.wait_ge(h_bias, GROUPS * l + GROUPS)
                sp.dma_start(bias_row[:, :], rows[bass.ds(2 + l, 1), :].partition_broadcast(P)).then_inc(row_in, 16)
                for half in range(2):
                    sp.wait_ge(u_mm, 32 * l + 30 + 2 * half)
                    load_cond(half, half)

            for slot in range(2):
                sp.wait_ge(cond_in[slot], 128 * L + 32)
            for part, buf in zip(at_s, (at_hi, at_lo)):
                sp.dma_start(bits(buf[:, :, :].rearrange("p t n -> p (t n)")), part).then_inc(at_in, 16)
            sp.wait_ge(qb_zero, 2 * (L + 1))
            for t in range(NT):
                if t >= 2:
                    sp.wait_ge(res_ok, t - 1)
                sp.dma_start(res[:, t % 2, :], res_s[t * P:(t + 1) * P, :]).then_inc(res_in[t % 2], 16)
                if t >= 1:
                    sp.wait_ge(res_ok, t)
                    sp.dma_start(out[(t - 1) * P:t * P, :], h[:, t - 1, :]).then_inc(out_done, 16)
            sp.wait_ge(res_ok, NT)
            sp.dma_start(out[(NT - 1) * P:N, :], h[:, NT - 1, :]).then_inc(out_done, 16)
            sp.wait_ge(out_done, 16 * NT)
            for s in range(2):
                sp.wait_ge(res_out[s], 16)
                sp.wait_ge(cond_out[s], 32 * GROUPS // 2)

        @block.gpsimd
        def _(pool):
            pool.sem_inc(f_ok, 2)
            pool.sem_inc(x3_ok, 2)
            pool.memset(ident[:, :], 0.0).then_inc(const_ok, 1)
            pool.memset(mhalf[:, :], -0.5).then_inc(const_ok, 1)
            pool.wait_ge(const_ok, 2)
            pool.affine_select(out=ident[:, :], in_=ident[:, :], compare_op=ALU.not_equal, fill=1.0, base=0,
                               pattern=[[-1, P]], channel_multiplier=1).then_inc(const_ok, 1)
            pool.memset(zeros[:, :], 0.0).then_inc(const_ok, 1)
            pool.memset(shift[:, :], SHIFT).then_inc(const_ok, 1)
            pool.memset(minus[:, :], -2 * SHIFT).then_inc(const_ok, 1)
            pool.iota(iota[:, :], pattern=[[1, N]], base=0, channel_multiplier=0,
                      allow_small_or_imprecise_dtypes=True).then_inc(iota_ok, 1)

            def rsqrt(k):
                wait_apart(pool, ln, 2 * k + 2)
                pool.tensor_scalar(veps[:, :], mv[:, 1:2], EPS, None, ALU.add).then_inc(rs, 1)
                pool.wait_ge(rs, 2 * k + 1)
                pool.tensor_tensor(rstd[:, :], veps[:, :], mhalf[:, 0:1], ALU.pow).then_inc(rs, 1)

            def w_low(n, slot, hi, lo):
                pool.wait_ge(w_hi_ok, n + 1)
                pool.tensor_tensor(lo, stage[:, slot, :], bits(hi), ALU.subtract).then_inc(w_ok, 1)

            pool.wait_ge(x_ln, 2 * NT)
            pool.tensor_scalar(x_veps[:, :], x_mv[:, :, 1], EPS, None, ALU.add).then_inc(x_rs, 1)
            pool.wait_ge(x_rs, 1)
            pool.tensor_tensor(x_rstd[:, :], x_veps[:, :], mhalf[:, :], ALU.pow).then_inc(x_rs, 1)

            def cond_low(g):
                s = g % 2
                if g >= 2:
                    pool.wait_ge(cond_out[s], 32 * (g // 2))
                pool.wait_ge(c_hi, g + 1)
                pool.tensor_tensor(cond_lo[s][:, :, :].rearrange("p k n -> p (k n)"), c_in[:, s, :],
                                   bits(cond_hi[s][:, :, :].rearrange("p k n -> p (k n)")), ALU.subtract)\
                    .then_inc(c_lo, 1)

            for k in range(KC):
                rsqrt(k)
                pool.wait_ge(y_hi, k + 1)
                pool.tensor_tensor(yT_lo[:, k, :], full[:, :, :].rearrange("p a n -> p (a n)"),
                                   bits(yT_hi[:, k, :]), ALU.subtract).then_inc(y_lo, 1)
                cond_low(k)
            for n in range(2):
                w_low(n, n, attn_place(0, 0, n), attn_place(1, 0, n))
            for g in range(KC, GROUPS):
                cond_low(g)
            def zero_q():
                pool.memset(bits(qbd_hi[:, :, :, :]), 0.0).then_inc(qb_zero, 1)
                pool.memset(bits(qbd_lo[:, :, :, :]), 0.0).then_inc(qb_zero, 1)

            for t in range(NT):
                pool.wait_ge(a_hi, t + 1)
                pool.tensor_tensor(at_lo[:, t, :], counts[:, t, :], bits(at_hi[:, t, :]), ALU.subtract)\
                    .then_inc(a_lo, 1)
            zero_q()
            pool.wait_ge(deg_ok, 1)
            pool.tensor_tensor(dinv[:, :], deg[:, :], mhalf[:, :], ALU.pow).then_inc(dinv_ok, 1)

            def xs_split(use):
                for t in range(NT):
                    pool.wait_ge(xs_hi_ok, NT * use + t + 1)
                    pool.tensor_tensor(xs_lo[:, t, :], xs[:, t, :], bits(xs_hi[:, t, :]), ALU.subtract)\
                        .then_inc(xs_lo_ok, 1)

            xs_split(0)
            for n in range(2, FIRST_PIECES):
                w_low(n, n % 2, attn_place(0, (n - 2) // 2, n % 2), attn_place(1, (n - 2) // 2, n % 2))

            with pool.Fori(0, L) as l:
                norm0 = KC + 2 * NT * l

                def x2_low(g):
                    pool.wait_ge(x2_hi_ok, GROUPS * l + g + 1)
                    pool.tensor_tensor(xT2_lo[:, :, :].rearrange("p k n -> p (k n)"), full[:, 0, :],
                                       bits(xT2_hi[:, :, :].rearrange("p k n -> p (k n)")),
                                       ALU.subtract).then_inc(x2_ok, 1)

                rsqrt(norm0)
                x2_low(0)
                with pool.Fori(0, GROUPS - 1) as g:
                    rsqrt(norm0 + 2 * g + 1)
                    x2_low(g + 1)
                    rsqrt(norm0 + 2 * g + 2)

                def x3_low(t):
                    r = slice(t % 4 * P, (t % 4 + 1) * P)
                    pool.wait_ge(x3_hi_ok, NT * l + t + 1)
                    pool.tensor_tensor(xT3_lo[t // 4][:, :, r],
                                       full[:, t % 2, :].rearrange("p (k n) -> p k n", n=P),
                                       bits(xT3_hi[t // 4][:, :, r]), ALU.subtract).then_inc(x3_ok, 1)

                def f_low(j, a, s):
                    half, c = s // 2, s % 2
                    pool.wait_ge(f_hi_ok, 32 * l + 8 * j + 4 * a + s + 1)
                    pool.tensor_tensor(f_lo[a][:, c, half * HALF:(half + 1) * HALF], ff[:, s % 2, :],
                                       bits(f_hi[a][:, c, half * HALF:(half + 1) * HALF]),
                                       ALU.subtract).then_inc(f_ok, 1)

                def mlp_step(j, a, s, weights=True):
                    if weights:
                        w_low(FIRST_PIECES + PIECES * l + 8 * j + 4 * a + 2 + s, s % 2,
                              mlp_place(0, j, a, s), mlp_place(1, j, a, s))
                    f_low(j, a, s)

                def mlp_group(j, a, last=False):
                    for s in range(4):
                        mlp_step(j, a, s, not (last and s >= 2))

                for r in range(2):
                    w_low(FIRST_PIECES + PIECES * l + r, r, up_place(0, 0, r), up_place(1, 0, r))
                for t in range(4):
                    x3_low(t)
                mlp_step(0, 0, 0)
                rsqrt(norm0 + 2 * NT - 1)
                for t in range(4, NT):
                    x3_low(t)
                mlp_step(0, 0, 1)
                mlp_step(0, 0, 2)
                mlp_step(0, 0, 3)
                mlp_group(0, 1)
                with pool.Fori(1, MG // 2 - 1) as j:
                    mlp_group(j, 0)
                    mlp_group(j, 1)
                mlp_group(MG // 2 - 1, 0)
                mlp_group(MG // 2 - 1, 1, last=True)
                wait_apart(pool, f_ok, 2 + 32 * l + 32)
                zero_q()

            for t in range(NT):
                pool.wait_ge(y_hi, KC + t + 1)
                pool.tensor_tensor(yT_lo[:, :, t * P:(t + 1) * P],
                                   full[:, t % 2, :].rearrange("p (k n) -> p k n", n=P),
                                   bits(yT_hi[:, :, t * P:(t + 1) * P]), ALU.subtract).then_inc(y_lo, 1)
            xs_split(1)

        @block.scalar
        def _(act):
            def w_high(n, slot, place):
                wait_apart(act, stage_in[slot], 8 * n + (16 if slot == 0 else 8))
                act.activation(place, stage[:, slot, :], ACT.Copy).then_inc(w_hi_ok, 1)

            for t in range(NT):
                act.wait_ge(x0_mm, t + 1)
                act.activation(x0T[:, :, t * P:(t + 1) * P],
                               ps[:, t, :].rearrange("p (k n) -> p k n", n=P), ACT.Relu)\
                    .then_inc(x0T_ok, 1)

            def cond_high(g):
                s = g % 2
                if g >= 2:
                    act.wait_ge(cond_out[s], 32 * (g // 2))
                act.wait_ge(c_in_in[s], 16 * (g // 2 + 1))
                act.activation(cond_hi[s][:, :, :].rearrange("p k n -> p (k n)"), c_in[:, s, :], ACT.Copy)\
                    .then_inc(c_hi, 1)

            for k in range(KC):
                act.wait_ge(bnf_ok, k + 1)
                act.activation(yT_hi[:, k, :], full[:, :, :].rearrange("p a n -> p (a n)"), ACT.Copy)\
                    .then_inc(y_hi, 1)
                cond_high(k)
            for n in range(2):
                w_high(n, n, attn_place(0, 0, n))
            act.wait_ge(cols_in, 16)
            act.activation(ones[:, :], cols_sb[:, 0:2], ACT.Copy, bias=1.0, scale=0.0).then_inc(ones_ok, 1)

            def a_digits(f):
                for t in range(NT):
                    act.wait_ge(a_sums, NT * f + t + 1)
                    if not isinstance(f, int) or f:
                        act.wait_ge(a_dec, NT * f - NT + t + 1)
                    act.activation(h[:, t, :], sums[:, t, :], ACT.Copy, bias=ROUND, scale=1 / DIGIT)\
                        .then_inc(a_round, 1)
                for t in range(NT):
                    wait_apart(act, a_round, NT * f + t + 1)
                    act.activation(h[:, t, :], h[:, t, :], ACT.Copy, bias=-ROUND).then_inc(a_digit, 1)

            act.wait_ge(x1_ok, NT)
            a_digits(0)
            for g in range(KC, GROUPS):
                cond_high(g)
            with act.Fori(1, FLUSHES) as f:
                a_digits(f)
            for s in range(2):
                act.wait_ge(cond_out[s], 32 * GROUPS // 2)
            for t in range(NT):
                act.wait_ge(a_dec, NT * FLUSHES - NT + t + 1)
                act.activation(at_hi[:, t, :], counts[:, t, :], ACT.Copy).then_inc(a_hi, 1)

            def xs_high(use):
                for t in range(NT):
                    act.wait_ge(xs_ok, NT * use + t + 1)
                    act.activation(xs_hi[:, t, :], xs[:, t, :], ACT.Copy).then_inc(xs_hi_ok, 1)

            xs_high(0)
            act.wait_ge(g_mm, NT)
            for n in range(2, FIRST_PIECES):
                w_high(n, n % 2, attn_place(0, (n - 2) // 2, n % 2))

            with act.Fori(0, L) as l:
                def v_high(u, mc, slot, bank=V_BANK):
                    act.wait_ge(v_mm, u + 1)
                    act.activation(v_hi[:, slot, mc, :], ps[:, bank, :], ACT.Copy).then_inc(v_hi_ok, 1)

                def k_high(u):
                    act.wait_ge(k_mm, u + 1)
                    act.activation(kT_hi[:, :], ps[:, K_BANK, :], ACT.Copy).then_inc(k_hi_ok, 1)

                def x2_high(g):
                    act.wait_ge(full2_ok, g + 1)
                    act.activation(xT2_hi[:, :, :].rearrange("p k n -> p (k n)"), full[:, 0, :], ACT.Copy)\
                        .then_inc(x2_hi_ok, 1)

                def q_copy(g):
                    act.wait_ge(q_mm, g + 1)
                    act.activation(q_sb[:, :], ps[:, Y_BANK, :], ACT.Copy, scale=Q_SCALE).then_inc(q_ok, 1)

                def q_high(g):
                    act.wait_ge(qt_mm, g + 1)
                    for e in range(2):
                        r = slice(64 * e, 64 * e + 64)
                        last = act.activation(
                            qbd_hi[r, :, :, r],
                            ps[r, X_BANK, :].rearrange("d (p b n) -> d p b n", p=PAIRS, b=2), ACT.Copy)
                    last.then_inc(qb_hi_ok, 1)

                def o_high(g):
                    act.wait_ge(pv_mm, PAIRS * g + PAIRS)
                    for e in range(2):
                        r = slice(64 * e, 64 * e + 64)
                        o_ps = ps[r, PV_BANK:PV_BANK + 2, :].rearrange("d a (p b n) -> d (a p b) n", p=2, b=2)
                        last = act.activation(oT_hi[r, :, :].rearrange("d p (b n) -> d (p b) n", b=2),
                                              o_ps[:, :, r], ACT.Copy)
                    last.then_inc(o_hi_ok, 1)

                def x3_high(t):
                    act.wait_ge(full3_ok, NT * l + t + 1)
                    act.activation(xT3_hi[t // 4][:, :, t % 4 * P:(t % 4 + 1) * P],
                                   full[:, t % 2, :].rearrange("p (k n) -> p k n", n=P), ACT.Copy)\
                        .then_inc(x3_hi_ok, 1)

                def unit(u, g, p, par, last=False, first=False):
                    act.wait_ge(mx_ok, u + 1)
                    for b in range(2):
                        e = act.activation(pe_[:, b, :], ps[:, S_BANK, b * M:(b + 1) * M], ACT.Exp,
                                           bias=nmx[:, b:b + 1], accum_out=rsum[:, b:b + 1])
                    e.then_inc(exp_ok, 1)
                    if not (last and p == 3):
                        k_high(u + 1)
                    if p == 2 and not last:
                        x2_high(g + 1)
                    if p == 3 and not last:
                        q_high(g + 1)
                    if p == 0 and not first:
                        o_high(g - 1)
                    if not (last and p >= 1 or first):
                        v_high(u + 3, (p + 3) % 4, par if p == 0 else 1 - par)
                    act.wait_ge(t_mm, u + 1)
                    act.activation(pT_hi[:, :, :].rearrange("p c n -> p (c n)"), ps[:, T_BANK, :], ACT.Copy)\
                        .then_inc(pT_hi_ok, 1)
                    if p == 2 and not last:
                        q_copy(g + 1)
                    if p == 1 and last:
                        for r in range(2):
                            w_high(FIRST_PIECES + PIECES * l + r, r, up_place(0, 0, r))
                    if p in (1, 2) and last:
                        x3_high(2 * p - 2)
                        x3_high(2 * p - 1)

                def body(g, par, last=False):
                    u, gg = UNITS * l + PAIRS * g, GROUPS * l + g
                    for p in range(1, 4):
                        unit(u + p, gg, p, par, last)
                    if not last:
                        unit(u + 4, gg + 1, 0, 1 - par)

                for mc in range(2):
                    v_high(UNITS * l + mc, mc, 0, V_BANK + mc)
                x2_high(GROUPS * l)
                v_high(UNITS * l + 2, 2, 0, V_BANK + 2)
                q_copy(GROUPS * l)
                k_high(UNITS * l)
                act.wait_ge(qb_zero, 2 * l + 2)
                q_high(GROUPS * l)
                v_high(UNITS * l + 3, 3, 0, V_BANK + 3)
                unit(UNITS * l, GROUPS * l, 0, 0, first=True)
                with act.Fori(0, GROUPS // 2 - 1) as i:
                    body(2 * i, 0)
                    body(2 * i + 1, 1)
                body(GROUPS - 2, 0)
                body(GROUPS - 1, 1, last=True)
                o_high(GROUPS * l + GROUPS - 1)

                def mlp_step(j, a, s, weights=True):
                    n = 32 * l + 8 * j + 4 * a + s
                    half, c = s // 2, s % 2
                    b = COL["geglu_b"] + 32 * l + 16 + 4 * j + 2 * a + c
                    wait_apart(act, u_mm, n + 1)
                    act.activation(gel[:, s % 2, :], ps[:, 2 * (s % 2) + 1, :], ACT.Gelu,
                                   bias=cols_sb[:, bass.ds(b, 1)]).then_inc(gel_ok, 1)
                    if weights:
                        w_high(FIRST_PIECES + PIECES * l + 8 * j + 4 * a + 2 + s, s % 2, mlp_place(0, j, a, s))
                    act.wait_ge(ff_ok, n + 1)
                    act.activation(f_hi[a][:, c, half * HALF:(half + 1) * HALF], ff[:, s % 2, :], ACT.Copy)\
                        .then_inc(f_hi_ok, 1)

                def mlp_group(j, a, last=False):
                    for s in range(4):
                        mlp_step(j, a, s, not (last and s >= 2))

                mlp_step(0, 0, 0)
                for t in range(4, NT):
                    x3_high(t)
                mlp_step(0, 0, 1)
                mlp_step(0, 0, 2)
                mlp_step(0, 0, 3)
                mlp_group(0, 1)
                with act.Fori(1, MG // 2 - 1) as j:
                    mlp_group(j, 0)
                    mlp_group(j, 1)
                mlp_group(MG // 2 - 1, 0)
                mlp_group(MG // 2 - 1, 1, last=True)

            act.wait_ge(w_ok, FIRST_PIECES + PIECES * L)
            for t in range(NT):
                act.wait_ge(bnf_ok, KC + t + 1)
                act.activation(yT_hi[:, :, t * P:(t + 1) * P],
                               full[:, t % 2, :].rearrange("p (k n) -> p k n", n=P), ACT.Copy)\
                    .then_inc(y_hi, 1)
            xs_high(1)

        @block.vector
        def _(dve):
            dve.sem_inc(h_att, 1)

            def norm_stats(k, parts):
                for n, part in enumerate(parts):
                    st = dve.bn_stats(stats[:, n, :], part)
                st.then_inc(ln, 1)
                wait_apart(dve, ln, 2 * k + 1)
                dve.bn_aggr(mv[:, :], stats[:, 0:len(parts), :].rearrange("p a s -> p (a s)"))\
                    .then_inc(ln, 1)

            def norm_wait(k):
                dve.wait_ge(ln, 2 * k + 2)
                dve.wait_ge(rs, 2 * k + 2)

            def norm(k, parts):
                norm_stats(k, parts)
                norm_wait(k)

            dve.wait_ge(ends_in, 32)
            dve.tensor_copy(ends_f[:, 0, :], ends_i[:, 0, :]).then_inc(ends_ok, 1)
            dve.tensor_copy(ends_f[:, 3, :], ends_i[:, 1, :]).then_inc(ends_ok, 1)
            dve.wait_ge(ends_ok, 2)
            dve.tensor_scalar(ends_f[:, 2, :], ends_f[:, 3, :], float(HALF), None, ALU.is_ge).then_inc(ends_ok, 1)
            dve.wait_ge(ends_ok, 3)
            dve.scalar_tensor_tensor(ends_f[:, 1, :], ends_f[:, 2, :], -float(HALF), ends_f[:, 3, :],
                                     ALU.mult, ALU.add).then_inc(ends_ok, 1)
            dve.wait_ge(ends_ok, 4)
            dve.tensor_scalar(ends_f[:, 2, :], ends_f[:, 2, :], DIGIT - 1, 1.0, ALU.mult, ALU.add)\
                .then_inc(ends_ok, 1)

            for t in range(NT):
                if t % (NT // 2) == 0:
                    dve.wait_ge(x_in[t // (NT // 2)], 16)
                dve.bn_stats(x_stats[:, t, :], h[:, t, :]).then_inc(x_ln, 1)
            for t in range(NT):
                dve.wait_ge(x_ln, NT)
                dve.bn_aggr(x_mv[:, t, :], x_stats[:, t, :]).then_inc(x_ln, 1)
            dve.wait_ge(x_ln, 2 * NT)
            dve.wait_ge(x_rs, 2)
            for t in range(NT):
                dve.tensor_scalar(z1[:, t, :], h[:, t, :], x_mv[:, t, 0:1], x_rstd[:, t:t + 1],
                                  ALU.subtract, ALU.mult).then_inc(x0_ok, 1)

            def x_sum(t):
                dve.wait_ge(x0_ok, t + 1)
                dve.scalar_tensor_tensor(x1[:, t, :], z1[:, t, :], 0.0, h[:, t, :], ALU.max, ALU.add)\
                    .then_inc(x1_ok, 1)

            def batchnorm(k):
                norm(k, [x0T[:, k, 0:HALF], x0T[:, k, HALF:N]])
                sc, sh = bn[:, 2 * k:2 * k + 1], bn[:, 2 * k + 1:2 * k + 2]
                w, b = (cols_sb[:, COL[n] + k:COL[n] + k + 1] for n in ("bn_w", "bn_b"))
                dve.tensor_scalar(sc, rstd[:, :], w, None, ALU.mult).then_inc(bn_ok, 1)
                dve.wait_ge(bn_ok, 3 * k + 1)
                dve.tensor_scalar(sh, mv[:, 0:1], sc, None, ALU.mult).then_inc(bn_ok, 1)
                dve.wait_ge(bn_ok, 3 * k + 2)
                dve.tensor_tensor(sh, b, sh, ALU.subtract).then_inc(bn_ok, 1)
                dve.wait_ge(bn_ok, 3 * k + 3)
                if k:
                    dve.wait_ge(y_lo, k)
                dve.tensor_scalar(full[:, :, :].rearrange("p a n -> p (a n)"), x0T[:, k, :], sc, sh,
                                  ALU.mult, ALU.add).then_inc(bnf_ok, 1)

            def one_hots(n):
                for c in range(4):
                    dve.wait_ge(oh_used, n + c + 1)
                    dve.tensor_scalar(oh_s[:, c, :], iota[:, :], ends_f[:, 0, bass.ds(n + c, 1)],
                                      None, ALU.is_equal)
                    dve.tensor_scalar(oh_d[:, c, :], iota[:, 0:HALF], ends_f[:, 1, bass.ds(n + c, 1)],
                                      ends_f[:, 2, bass.ds(n + c, 1)], ALU.is_equal, ALU.mult)\
                        .then_inc(oh_ok, 1)

            def take_sums(f):
                if not isinstance(f, int) or f:
                    wait_apart(dve, a_low, NT * f)
                    wait_apart(dve, a_dec, NT * f)
                for t in range(NT):
                    dve.wait_ge(a_mm, NT * f + t + 1)
                    dve.tensor_copy(sums[:, t, :], ps[:, t, :]).then_inc(a_sums, 1)

            def add_digits(f, t, first=False):
                one = slice(t, t + 1) if isinstance(t, int) else bass.ds(t, 1)
                low, high = counts[:, one, 0:HALF], counts[:, one, HALF:N]
                wait_apart(dve, a_digit, NT * f + t + 1)
                if first:
                    dve.scalar_tensor_tensor(low, h[:, one, :], -DIGIT, sums[:, one, :], ALU.mult, ALU.add)\
                        .then_inc(a_low, 1)
                    dve.tensor_scalar(high, h[:, one, :], OFFSET / DIGIT, None, ALU.add).then_inc(a_dec, 1)
                else:
                    dve.scalar_tensor_tensor(sums[:, one, :], h[:, one, :], -DIGIT, sums[:, one, :],
                                             ALU.mult, ALU.add).then_inc(a_low, 1)
                    dve.scalar_tensor_tensor(high, h[:, one, :], OFFSET / DIGIT, high, ALU.add, ALU.add)
                    wait_apart(dve, a_low, NT * f + t + 1)
                    dve.tensor_tensor(low, low, sums[:, one, :], ALU.add).then_inc(a_dec, 1)

            dve.wait_ge(iota_ok, 1)
            dve.wait_ge(ends_ok, 5)
            dve.wait_ge(cols_in, 16)
            for k in range(KC):
                for i in range(2):
                    one_hots(8 * k + 4 * i)
                if k == 0:
                    dve.wait_ge(x0T_ok, NT)
                batchnorm(k)
                x_sum(2 * k)
                x_sum(2 * k + 1)
            for half in range(2):
                dve.wait_ge(res_out[half], 16)
            take_sums(0)
            with dve.Fori(0, NT) as t:
                one_hots(FLUSH + 4 * t)
                add_digits(0, t, first=True)
            take_sums(1)
            with dve.Fori(2, FLUSHES) as f:
                with dve.Fori(0, NT) as t:
                    one_hots(FLUSH * f + 4 * t)
                    add_digits(f - 1, t)
                take_sums(f)
            for t in range(NT):
                add_digits(FLUSHES - 1, t)
            for half in range(2):
                dve.wait_ge(row_mm, half + 1)
                dve.tensor_copy(sums[0:2, half, :], ps[0:2, 7 - half, :]).then_inc(row_ok, 1)
            dve.wait_ge(deg_mm, 1)
            dve.tensor_scalar(deg[:, :], ps[:, 7, 0:2 * NT:2], 1.0, None, ALU.add).then_inc(deg_ok, 1)
            dve.wait_ge(dinv_ok, 1)

            def gcn(use):
                for t in range(NT):
                    dve.wait_ge(g_mm, NT * use + t + 1)
                    dve.tensor_scalar(xs[:, t, :], ps[:, t, :], dinv[:, t:t + 1], None, ALU.mult)\
                        .then_inc(xs_ok, 1)
                dve.wait_ge(row_in, 16 if use == 0 else 16 * (L + 2))
                for t in range(NT):
                    dve.wait_ge(agg_mm, NT * use + t + 1)
                    dve.tensor_tensor(xs[:, t, :], ps[:, t, :], xs[:, t, :], ALU.add).then_inc(agg_s, 1)
                    dve.wait_ge(agg_s, NT * use + t + 1)
                    dve.scalar_tensor_tensor(h[:, t, :], xs[:, t, :], dinv[:, t:t + 1], bias_row[:, :],
                                             ALU.mult, ALU.add).then_inc(gcn_ok, 1)

            gcn(0)
            dve.wait_ge(gcn_ok, NT)

            with dve.Fori(0, L) as l:
                norm0 = KC + 2 * NT * l

                def v_low(u, mc, slot, bank=V_BANK):
                    dve.wait_ge(v_hi_ok, u + 1)
                    dve.tensor_tensor(v_lo[:, slot, mc, :], ps[:, bank, :], bits(v_hi[:, slot, mc, :]),
                                      ALU.subtract).then_inc(v_ok, 1)

                def k_low(u):
                    dve.wait_ge(k_hi_ok, u + 1)
                    dve.tensor_tensor(kT_lo[:, :], ps[:, K_BANK, :], bits(kT_hi[:, :]), ALU.subtract)\
                        .then_inc(k_ok, 1)

                def x2_full(g):
                    dve.wait_ge(t2_mm, g + 1)
                    for k in range(KC):
                        last = dve.tensor_scalar(full[:, 0, k * P:(k + 1) * P], ps[:, X_BANK, k * P:(k + 1) * P],
                                                 cols_sb[:, bass.ds(COL["ln2_w"] + KC * l + k, 1)],
                                                 cols_sb[:, bass.ds(COL["ln2_b"] + KC * l + k, 1)],
                                                 ALU.mult, ALU.add)
                    last.then_inc(full2_ok, 1)

                def q_low(g):
                    dve.wait_ge(qb_hi_ok, g + 1)
                    for e in range(2):
                        r = slice(64 * e, 64 * e + 64)
                        last = dve.tensor_tensor(
                            qbd_lo[r, :, :, r], ps[r, X_BANK, :].rearrange("d (p b n) -> d p b n", p=PAIRS, b=2),
                            bits(qbd_hi[r, :, :, r]), ALU.subtract)
                    last.then_inc(qb_ok, 1)

                def o_low(g):
                    dve.wait_ge(o_hi_ok, g + 1)
                    for e in range(2):
                        r = slice(64 * e, 64 * e + 64)
                        o_ps = ps[r, PV_BANK:PV_BANK + 2, :].rearrange("d a (p b n) -> d (a p b) n", p=2, b=2)
                        last = dve.tensor_tensor(oT_lo[r, :, :].rearrange("d p (b n) -> d (p b) n", b=2),
                                                 o_ps[:, :, r],
                                                 bits(oT_hi[r, :, :]).rearrange("d p (b n) -> d (p b) n", b=2),
                                                 ALU.subtract)
                    last.then_inc(o_ok, 1)

                def x3_full(t):
                    dve.wait_ge(t3_mm, NT * l + t + 1)
                    dve.wait_ge(x3_ok, NT * l + t + 1)
                    for k in range(KC):
                        last = dve.tensor_scalar(full[:, t % 2, k * P:(k + 1) * P],
                                                 ps[:, T3_BANK[t], k * P:(k + 1) * P],
                                                 cols_sb[:, bass.ds(COL["ln3_w"] + KC * l + k, 1)],
                                                 cols_sb[:, bass.ds(COL["ln3_b"] + KC * l + k, 1)],
                                                 ALU.mult, ALU.add)
                    last.then_inc(full3_ok, 1)

                def maxima(u):
                    dve.wait_ge(s_mm, u + 1)
                    dve.tensor_reduce(nmx[:, :], ps[:, S_BANK, :].rearrange("p (b m) -> p b m", b=2),
                                      AX.X, ALU.max, negate=True).then_inc(mx_ok, 1)

                def softmax(u):
                    dve.wait_ge(exp_ok, u + 1)
                    dve.reciprocal(rinv[:, :], rsum[:, :]).then_inc(rinv_ok, 1)
                    dve.wait_ge(rinv_ok, u + 1)
                    for b in range(2):
                        last = dve.tensor_scalar(pn[:, b, :], pe_[:, b, :], rinv[:, b:b + 1], None, ALU.mult)
                    last.then_inc(pn_ok, 1)

                def unit(u, g, p, par, last=False, first=False, t=0):
                    softmax(u)
                    if not (last and p == 3):
                        k_low(u + 1)
                    if p == 2 and not last:
                        x2_full(g + 1)
                    if p == 1 and not last:
                        norm_stats(norm0 + 2 * t + 1, [h[:, t + 1, :]])
                    if p == 3 and not last:
                        q_low(g + 1)
                    if p == 0 and not first:
                        o_low(g - 1)
                    if not (last and p >= 1 or first):
                        v_low(u + 3, (p + 3) % 4, par if p == 0 else 1 - par)
                    if p == 1 and not last:
                        z2_of(t + 1, 2 * t + 1)
                    dve.wait_ge(pT_hi_ok, u + 1)
                    dve.tensor_tensor(pT_lo[:, :, :].rearrange("p c n -> p (c n)"), ps[:, T_BANK, :],
                                      bits(pT_hi[:, :, :].rearrange("p c n -> p (c n)")), ALU.subtract)\
                        .then_inc(pT_ok, 1)
                    if not (last and p == 3):
                        maxima(u + 1)
                    if p in (1, 2) and last:
                        x3_full(2 * p - 2)
                        x3_full(2 * p - 1)

                def residual(g):
                    gg = GROUPS * l + g
                    dve.wait_ge(wo_mm, gg + 1)
                    dve.tensor_tensor(h[:, g, :], h[:, g, :], ps[:, Y_BANK, :], ALU.add).then_inc(h_att, 1)
                    wait_apart(dve, h_att, gg + 2)
                    norm(norm0 + 2 * g + 2 if not isinstance(g, int) or g < NT - 1 else norm0 + 2 * NT - 1,
                         [h[:, g, :]])
                    dve.tensor_scalar(z3[:, g, :], h[:, g, :], mv[:, 0:1], rstd[:, 0:1],
                                      ALU.subtract, ALU.mult).then_inc(z3_ok, 1)
                    dve.wait_ge(z3_ok, gg + 1)
                    dve.tensor_tensor(h[:, g, :], h[:, g, :], bias_row[:, :], ALU.add).then_inc(h_bias, 1)

                def z2_of(g, k):
                    norm_wait(norm0 + k)
                    dve.tensor_scalar(z2[:, :], h[:, g, :], mv[:, 0:1], rstd[:, 0:1],
                                      ALU.subtract, ALU.mult).then_inc(z2_ok, 1)

                def body(g, par, last=False):
                    u, gg = UNITS * l + PAIRS * g, GROUPS * l + g
                    for p in range(1, 4):
                        unit(u + p, gg, p, par, last, t=g)
                    if not last:
                        unit(u + 4, gg + 1, 0, 1 - par)
                        residual(g)
                    else:
                        o_low(gg)

                dve.wait_ge(row_in, 16 * l + 32)
                norm_stats(norm0, [h[:, 0, :]])
                z2_of(0, 0)
                for mc in range(2):
                    v_low(UNITS * l + mc, mc, 0, V_BANK + mc)
                x2_full(GROUPS * l)
                v_low(UNITS * l + 2, 2, 0, V_BANK + 2)
                k_low(UNITS * l)
                q_low(GROUPS * l)
                v_low(UNITS * l + 3, 3, 0, V_BANK + 3)
                maxima(UNITS * l)
                unit(UNITS * l, GROUPS * l, 0, 0, first=True)
                with dve.Fori(0, GROUPS // 2 - 1) as i:
                    body(2 * i, 0)
                    body(2 * i + 1, 1)
                body(GROUPS - 2, 0)
                body(GROUPS - 1, 1, last=True)

                def mlp_step(j, a, s):
                    n = 32 * l + 8 * j + 4 * a + s
                    c = s % 2
                    dve.wait_ge(f_ok, n + 1)
                    dve.wait_ge(gel_ok, n + 1)
                    dve.scalar_tensor_tensor(
                        ff[:, s % 2, :], ps[:, 2 * (s % 2), :],
                        cols_sb[:, bass.ds(COL["geglu_b"] + 32 * l + 4 * j + 2 * a + c, 1)],
                        gel[:, s % 2, :], ALU.add, ALU.mult).then_inc(ff_ok, 1)

                def mlp_add(j, a):
                    for t in range(NT):
                        dve.wait_ge(ffo_mm, 64 * l + 16 * j + 8 * a + t + 1)
                        dve.tensor_tensor(h[:, t, :], h[:, t, :], ps[:, 4 + t % 4, :], ALU.add)\
                            .then_inc(h_ffo, 1)

                mlp_step(0, 0, 0)
                residual(GROUPS - 1)
                for t in range(4, NT):
                    x3_full(t)
                mlp_step(0, 0, 1)
                mlp_step(0, 0, 2)
                mlp_step(0, 0, 3)
                for s in range(4):
                    mlp_step(0, 1, s)
                mlp_add(0, 0)
                with dve.Fori(1, MG // 2) as j:
                    for s in range(4):
                        mlp_step(j, 0, s)
                    mlp_add(j - 1, 1)
                    for s in range(4):
                        mlp_step(j, 1, s)
                    mlp_add(j, 0)
                mlp_add(MG // 2 - 1, 1)
                dve.wait_ge(h_ffo, 64 * l + 64)

            for t in range(NT):
                dve.wait_ge(hT_mm, t + 1)
                if t >= 2:
                    dve.wait_ge(y_lo, KC + t - 1)
                dve.tensor_copy(full[:, t % 2, :], ps[:, t, :]).then_inc(bnf_ok, 1)
            gcn(1)
            for t in range(NT):
                dve.wait_ge(gcn_ok, NT + t + 1)
                dve.wait_ge(res_in[t % 2], 16 * (t // 2 + 1))
                dve.tensor_tensor(h[:, t, :], h[:, t, :], res[:, t % 2, :], ALU.add).then_inc(res_ok, 1)

        @block.tensor
        def _(pe):
            def product(bank, steps):
                n = len(steps)
                for i, (l_hi, l_lo, r_hi, r_lo) in enumerate(steps):
                    pe.matmul(bank, l_hi, r_hi, start=(i == 0), stop=False)
                    pe.matmul(bank, l_hi, r_lo, start=False, stop=False)
                    last = pe.matmul(bank, l_lo, r_hi, start=False, stop=(i == n - 1))
                return last

            pe.sem_inc(oh_used, 4)
            pe.wait_ge(const_ok, 6)
            for t in range(NT):
                pe.wait_ge(x0_ok, t + 1)
                for k in range(KC):
                    last = pe.transpose(ps[:, t, k * P:(k + 1) * P], z1[:, t, k * P:(k + 1) * P], ident[:, :])
                last.then_inc(x0_mm, 1)

            def count(f):
                for t in range(NT):
                    if isinstance(f, int):
                        pe.wait_ge(x0T_ok, t + 1)
                    else:
                        pe.wait_ge(a_sums, NT * f - NT + t + 1)
                    pe.matmul(ps[:, t, :], minus[:, :], shift[:, :], start=True, stop=False)
                with pe.Fori(0, NT) as c4:
                    for c in range(4):
                        pe.wait_ge(oh_ok, FLUSH * f + 4 * c4 + c + 1)
                        for t in range(NT):
                            last = pe.matmul(ps[:, t, :], oh_s[:, c, t * P:(t + 1) * P], oh_d[:, c, :],
                                             start=False, stop=False)
                        last.then_inc(oh_used, 1)
                for t in range(NT):
                    pe.matmul(ps[:, t, :], zeros[:, :], shift[:, :], start=False, stop=True).then_inc(a_mm, 1)

            count(0)
            with pe.Fori(1, FLUSHES) as f:
                count(f)

            def g_product(t):
                r = slice(t * P, (t + 1) * P)
                product(ps[:, t, :], [(yT_hi[:, k, r], yT_lo[:, k, r], w_hi[:, 0, k, :], w_lo[:, 0, k, :])
                                      for k in range(KC)]).then_inc(g_mm, 1)

            def aggregate(use):
                pe.wait_ge(xs_lo_ok, NT * use + NT)
                for t in range(NT):
                    r = slice(t * P, (t + 1) * P)
                    product(ps[:, t, :], [(at_hi[:, s, r], at_lo[:, s, r], xs_hi[:, s, :], xs_lo[:, s, :])
                                          for s in range(NT)]).then_inc(agg_mm, 1)

            pe.wait_ge(y_lo, KC)
            pe.wait_ge(w_ok, 2)
            for t in range(6):
                pe.wait_ge(a_sums, NT * FLUSHES - NT + t + 1)
                g_product(t)
            pe.wait_ge(a_sums, NT * FLUSHES)
            pe.wait_ge(a_lo, NT)
            pe.wait_ge(ones_ok, 1)
            for half in range(2):
                r = slice(half * HALF, (half + 1) * HALF)
                for st in range(NT):
                    pe.matmul(ps[0:2, 7 - half, :], ones[:, :], at_hi[:, st, r], start=(st == 0), stop=False)
                    last = pe.matmul(ps[0:2, 7 - half, :], ones[:, :], at_lo[:, st, r], start=False,
                                     stop=(st == NT - 1))
                last.then_inc(row_mm, 1)
            pe.wait_ge(row_ok, 2)
            for t in range(NT):
                last = pe.transpose(ps[:, 7, 2 * t:2 * t + 2], sums[0:2, t // 4, t % 4 * P:(t % 4 + 1) * P],
                                    ident[0:2, 0:2])
            last.then_inc(deg_mm, 1)
            g_product(6)
            pe.wait_ge(deg_ok, 1)
            g_product(7)
            aggregate(0)

            with pe.Fori(0, L) as l:
                def k_product(u, p, slot):
                    r = slice(p * P, (p + 1) * P)
                    product(ps[:, K_BANK, :], [(w_hi[:, 1, k, r], w_lo[:, 1, k, r],
                                                cond_hi[slot][:, k, :], cond_lo[slot][:, k, :])
                                               for k in range(KC)]).then_inc(k_mm, 1)

                def v_product(u, mc, slot, bank=V_BANK):
                    if u is not None:
                        pe.wait_ge(v_ok, u)
                    r = slice(mc * P, (mc + 1) * P)
                    product(ps[:, bank, :], [(cond_hi[slot][:, k, r], cond_lo[slot][:, k, r],
                                                w_hi[:, 2, k, :], w_lo[:, 2, k, :])
                                               for k in range(KC)]).then_inc(v_mm, 1)

                def s_product(u, g, p):
                    pe.wait_ge(k_ok, u + 1)
                    if p == 0:
                        pe.wait_ge(qb_ok, g + 1)
                    for b in range(2):
                        r = slice(b * M, (b + 1) * M)
                        last = product(ps[:, S_BANK, r], [(qbd_hi[:, p, b, :], qbd_lo[:, p, b, :],
                                                           kT_hi[:, r], kT_lo[:, r])])
                    last.then_inc(s_mm, 1)

                def p_transpose(u):
                    pe.wait_ge(pn_ok, u + 1)
                    for b in range(2):
                        for c in range(2):
                            i = 2 * b + c
                            last = pe.transpose(ps[:, T_BANK, i * P:(i + 1) * P], pn[:, b, c * P:(c + 1) * P],
                                                ident[:, :])
                    last.then_inc(t_mm, 1)

                def pv_product(u, p, slot):
                    pe.wait_ge(pT_ok, u + 1)
                    bank = PV_BANK + p // 2
                    for b in range(2):
                        at = (p % 2) * 2 * P + b * P
                        last = product(ps[:, bank, at:at + P],
                                       [(v_hi[:, slot, 2 * b + c, p * P:(p + 1) * P],
                                         v_lo[:, slot, 2 * b + c, p * P:(p + 1) * P],
                                         pT_hi[:, 2 * b + c, :], pT_lo[:, 2 * b + c, :]) for c in range(2)])
                    last.then_inc(pv_mm, 1)

                def t2(g):
                    pe.wait_ge(z2_ok, g + 1)
                    for k in range(KC):
                        last = pe.transpose(ps[:, X_BANK, k * P:(k + 1) * P], z2[:, k * P:(k + 1) * P], ident[:, :])
                    last.then_inc(t2_mm, 1)

                def q_product(g, first=False):
                    pe.wait_ge(x2_ok, g + 1)
                    if not first:
                        pe.wait_ge(h_att, g)
                    product(ps[:, Y_BANK, :], [(xT2_hi[:, k, :], xT2_lo[:, k, :], w_hi[:, 0, k, :], w_lo[:, 0, k, :])
                                               for k in range(KC)]).then_inc(q_mm, 1)

                def q_transpose(g):
                    pe.wait_ge(q_ok, g + 1)
                    for p in range(PAIRS):
                        last = pe.transpose(ps[:, X_BANK, p * P:(p + 1) * P], q_sb[:, p * P:(p + 1) * P], ident[:, :])
                    last.then_inc(qt_mm, 1)

                def wo_product(g):
                    pe.wait_ge(o_ok, g + 1)
                    product(ps[:, Y_BANK, :], [(oT_hi[:, p, :], oT_lo[:, p, :], w_hi[:, 3, p, :], w_lo[:, 3, p, :])
                                               for p in range(PAIRS)]).then_inc(wo_mm, 1)

                def t3(t):
                    pe.wait_ge(z3_ok, NT * l + t + 1)
                    if t in (2, 3, 7):
                        pe.wait_ge(full3_ok, NT * l + {2: 1, 3: 2, 7: 5}[t])
                    for k in range(KC):
                        last = pe.transpose(ps[:, T3_BANK[t], k * P:(k + 1) * P], z3[:, t, k * P:(k + 1) * P],
                                            ident[:, :])
                    last.then_inc(t3_mm, 1)

                def mlp_step(j, a, s, first=False, between=None):
                    half, c = s // 2, s % 2
                    if not (first and s < 2):
                        pe.wait_ge(ff_ok, 32 * l + 8 * j + 4 * a + s - 1)
                    for v in range(2):
                        if v and between:
                            between()
                        last = product(ps[:, 2 * (s % 2) + v, :],
                                       [(wg_hi[:, a, k, v, c * P:(c + 1) * P], wg_lo[:, a, k, v, c * P:(c + 1) * P],
                                        xT3_hi[half][:, k, :], xT3_lo[half][:, k, :]) for k in range(KC)])
                    last.then_inc(u_mm, 1)

                def unit(u, g, p, par, last=False, first=False):
                    if not (last and p == 3):
                        k_product(u + 1, (p + 1) % 4, par if p < 3 else 1 - par)
                    if p == 2 and not last:
                        t2(g + 1)
                    if p == 3 and not last:
                        q_transpose(g + 1)
                    if not first:
                        pv_product(u - 1, (p + 3) % 4, par if p else 1 - par)
                    if not (last and p >= 1 or first):
                        v_product(u + 3, (p + 3) % 4, par if p == 0 else 1 - par)
                    if p == 0 and not first:
                        wo_product(g - 1)
                    p_transpose(u)
                    if not (last and p == 3):
                        s_product(u + 1, g if p < 3 else g + 1, (p + 1) % 4)
                    if p == 2 and not last:
                        q_product(g + 1)
                    if p in (1, 2) and last:
                        t3(2 * p - 2)
                        t3(2 * p - 1)

                def body(g, i, par, last=False):
                    u, gg = UNITS * l + PAIRS * g, GROUPS * l + g
                    if not last:
                        pe.wait_ge(cond_in[1 - par], 128 * l + 32 * (i + 1 + par))
                    for p in range(1, 4):
                        unit(u + p, gg, p, par, last)
                    if not last:
                        unit(u + 4, gg + 1, 0, 1 - par)
                    else:
                        pv_product(u + 3, 3, par)

                pe.wait_ge(w_ok, PIECES * l + FIRST_PIECES)
                pe.wait_ge(cond_in[0], 128 * l + 32)
                for mc in range(2):
                    v_product(None, mc, 0, V_BANK + mc)
                t2(GROUPS * l)
                v_product(None, 2, 0, V_BANK + 2)
                q_product(GROUPS * l, first=True)
                k_product(UNITS * l, 0, 0)
                q_transpose(GROUPS * l)
                v_product(None, 3, 0, V_BANK + 3)
                pe.wait_ge(v_ok, UNITS * l + 3)
                s_product(UNITS * l, GROUPS * l, 0)
                unit(UNITS * l, GROUPS * l, 0, 0, first=True)
                with pe.Fori(0, GROUPS // 2 - 1) as i:
                    body(2 * i, i, 0)
                    body(2 * i + 1, i, 1)
                body(GROUPS - 2, GROUPS // 2 - 1, 0)
                body(GROUPS - 1, GROUPS // 2 - 1, 1, last=True)

                def mlp_up(j, a):
                    pe.wait_ge(w_ok, FIRST_PIECES + PIECES * l + 8 * j + 4 * a + 1)
                    for s in range(4):
                        mlp_step(j, a, s)

                def mlp_down(j, a, first=False):
                    pe.wait_ge(w_ok, FIRST_PIECES + PIECES * l + 8 * j + 4 * a + 3)
                    pe.wait_ge(f_ok, 2 + 32 * l + 8 * j + 4 * a + 4)
                    for t in range(NT):
                        if not (first and t < 4):
                            pe.wait_ge(h_ffo, 64 * l + 16 * j + 8 * a + t - 3)
                        r = slice(t * P, (t + 1) * P)
                        product(ps[:, 4 + t % 4, :], [(f_hi[a][:, c, r], f_lo[a][:, c, r],
                                                       wf_hi[:, a, c, :], wf_lo[:, a, c, :])
                                                      for c in range(2)]).then_inc(ffo_mm, 1)

                pe.wait_ge(w_ok, FIRST_PIECES + PIECES * l + 2)
                pe.wait_ge(x3_ok, 2 + NT * l + 4)
                mlp_step(0, 0, 0, first=True)
                wo_product(GROUPS * l + GROUPS - 1)
                for t in range(4, 7):
                    t3(t)
                mlp_step(0, 0, 1, first=True, between=lambda: t3(7))
                pe.wait_ge(x3_ok, 2 + NT * l + NT)
                mlp_step(0, 0, 2, first=True)
                mlp_step(0, 0, 3, first=True)
                mlp_up(0, 1)
                mlp_down(0, 0, first=True)
                with pe.Fori(1, MG // 2) as j:
                    mlp_up(j, 0)
                    mlp_down(j - 1, 1)
                    mlp_up(j, 1)
                    mlp_down(j, 0)
                mlp_down(MG // 2 - 1, 1)

            pe.wait_ge(h_ffo, 64 * L)
            for t in range(NT):
                for k in range(KC):
                    last = pe.transpose(ps[:, t, k * P:(k + 1) * P], h[:, t, k * P:(k + 1) * P], ident[:, :])
                last.then_inc(hT_mm, 1)
            pe.wait_ge(y_lo, KC + NT)
            pe.wait_ge(w_ok, FIRST_PIECES + PIECES * L)
            for t in range(NT):
                g_product(t)
            pe.wait_ge(at_in, 32)
            aggregate(1)


def _arrays(inputs):
    import numpy as np

    a = {n.replace("L0_gnn_", ""): np.asarray(v) for n, v in inputs.items()}
    D = a["x"].shape[1]
    P, L = 128, a["Wq"].shape[0]

    def square(w):
        return list(w.reshape(2, 2, P, D).transpose(0, 2, 1, 3).reshape(2, P, 1024))

    attention = [[square(a[n][l]) for n in ("Wq", "Wk", "Wv", "Wo")] for l in range(L)]
    attention.append([square(a["gcn_out_w"])] * 4)
    pieces = square(a["gcn_in_w"]) + [p for m in attention[0] for p in m]
    for l in range(L):
        up = a["geglu_w"][l].reshape(2, 2, P, 2, 8, 256).transpose(4, 0, 2, 1, 3, 5).reshape(8, 2, P, 1024)
        down = a["ffo_w"][l].reshape(8, 2, P, D).transpose(0, 2, 1, 3).reshape(8, P, 1024)
        pieces += [up[0, 0], up[0, 1]]
        for q in range(8):
            pieces += [down[q], *(up[q + 1] if q < 7 else []), attention[l + 1][q // 2][q % 2]]
    cond = a["cond"].reshape(8, 512, 4, P).transpose(0, 3, 2, 1)
    vectors = [a["bn_w"][None], a["bn_b"][None], a["ln2_w"], a["ln2_b"], a["ln3_w"], a["ln3_b"], a["geglu_b"]]
    cols = np.concatenate([v.reshape(-1, P) for v in vectors]).T
    rows = np.concatenate([a["gcn_in_b"][None], a["ffo_b"], a["gcn_out_b"][None]])
    return {"x": a["x"], "src": a["src"].reshape(P, -1), "dst": a["dst"].reshape(P, -1), "condT": cond,
            "pieces": np.stack(pieces), "cols": cols, "rows": rows}


def kernel(**inputs):
    import numpy as np
    import concourse.bacc as bacc
    from concourse.bass_utils import run_bass_kernel_spmd

    nc = bacc.Bacc("TRN2", target_bir_lowering=False, num_devices=1, dynamic_dma_scratch_size=1024)
    arrays, args = {}, []
    for name, a in _arrays(inputs).items():
        a = np.ascontiguousarray(a)
        arrays[f"in_{name}"] = a
        args.append(nc.dram_tensor(f"in_{name}", a.shape, mybir.dt.from_np(a.dtype), kind="ExternalInput").ap())
    n, d = inputs["x"].shape
    args.append(nc.dram_tensor("out", (n, d), mybir.dt.float32, kind="ExternalOutput").ap())
    gnn_preln_kernel(nc, *args)
    r = run_bass_kernel_spmd(nc, [arrays], core_ids=[0])
    return np.asarray(r.results[0]["out"])
```

```python
import concourse.bass as bass
from concourse import mybir
from contextlib import ExitStack


def gnn_preln_kernel(
    nc: bass.Bass,
    x: bass.AP,
    src: bass.AP,
    dst: bass.AP,
    condT: bass.AP,
    pieces: bass.AP,
    cols: bass.AP,
    rows: bass.AP,
    out: bass.AP,
):
    f32 = mybir.dt.float32
    f32r = mybir.dt.float32r
    f16 = mybir.dt.float16
    i32 = mybir.dt.int32
    ALU = mybir.AluOpType
    ACT = mybir.ActivationFunctionType
    AX = mybir.AxisListType

    P = 128
    N, D = x.shape
    NT, KC = N // P, D // P
    GROUPS = condT.shape[0]
    M = condT.shape[3] // 2
    PAIRS = 4
    E = src.shape[0] * src.shape[1]
    CHUNKS = E // P
    HALF = N // 2
    L = (pieces.shape[0] - 10) // 32
    UNITS = GROUPS * PAIRS
    MG = 8
    PIECES = 4 * MG
    FIRST_PIECES = 10
    COL = {"bn_w": 0, "bn_b": 4, "ln2_w": 8, "ln2_b": 24, "ln3_w": 40, "ln3_b": 56, "geglu_b": 72}
    EPS = 1e-5
    DIGIT, OFFSET, FLUSH = 8192.0, 2.0 ** 24, 32
    SHIFT = 256.0
    ROUND = 1.5 * 2.0 ** 23
    Q_SCALE = 0.125
    FLUSHES = CHUNKS // FLUSH
    assert NT == GROUPS and L * 32 == 128 and FLUSH == 4 * NT and CHUNKS == FLUSH * FLUSHES
    assert FLUSH * P * DIGIT == 2 * OFFSET and FLUSH * P * 2 == DIGIT and P * SHIFT * 2 * SHIFT == OFFSET

    with ExitStack() as ctx:
        def sb(name, shape, dt, where=ctx):
            return where.enter_context(nc.sbuf_tensor(name, shape, dt))

        def sem(name):
            return ctx.enter_context(nc.semaphore(name))

        h = sb("h", [P, NT, D], f32)
        w_hi = sb("w_hi", [P, 4, KC, D], f32r)
        w_lo = sb("w_lo", [P, 4, KC, D], f32r)
        stage = sb("stage", [P, 2, 1024], f32)
        oT_hi = sb("oT_hi", [P, PAIRS, P], f32r)
        oT_lo = sb("oT_lo", [P, PAIRS, P], f32r)
        o_full = sb("o_full", [P, PAIRS, P], f32)
        full = sb("full", [P, 2, D], f32)
        bias_row = sb("bias_row", [P, D], f32)
        cols_sb = sb("cols_sb", [P, cols.shape[1]], f32)
        ident = sb("ident", [P, P], f32)
        mhalf = sb("mhalf", [P, NT], f32)
        ones = sb("ones", [P, 2], f32r)
        stats = sb("stats", [P, 2, 6], f32)
        mv = sb("mv", [P, 2], f32)
        veps = sb("veps", [P, 1], f32)
        rstd = sb("rstd", [P, 1], f32)
        nmx = sb("nmx", [P, 2], f32)
        rsum = sb("rsum", [P, 2], f32)
        rinv = sb("rinv", [P, 2], f32)
        deg = sb("deg", [P, NT], f32)
        dinv = sb("dinv", [P, NT], f32)
        bn = sb("bn", [P, 8], f32)
        x_stats = sb("x_stats", [P, NT, 6], f32)
        x_mv = sb("x_mv", [P, NT, 2], f32)
        x_veps = sb("x_veps", [P, NT], f32)
        x_rstd = sb("x_rstd", [P, NT], f32)

        def overlay(*uses):
            made = []
            for use in uses:
                with ExitStack() as where:
                    made.append([sb(*one, where) for one in use])
            big = max(sum(size(one) for one in use) for use in uses)
            ctx.enter_context(nc.sbuf_tensor(f"room_of_{uses[0][0][0]}", [P, big], mybir.dt.int8))
            return made

        def size(one):
            n = 2 if one[2] == f16 else 4
            for d in one[1][1:]:
                n *= d
            return n

        (at_hi,), cond, xT3 = overlay(
            [("at_hi", [P, NT, N], f32r)],
            [(f"cond{s}_{part}", [P, KC, 2 * M], f32r) for s in range(2) for part in ("hi", "lo")],
            [(f"xT3{s}_{part}", [P, KC, HALF], f32r) for s in range(2) for part in ("hi", "lo")])
        cond_hi, cond_lo, xT3_hi, xT3_lo = cond[0::2], cond[1::2], xT3[0::2], xT3[1::2]
        (at_lo,), (counts,), (z1, x1), (v_hi, v_lo), (wg_hi, wg_lo) = overlay(
            [("at_lo", [P, NT, N], f32r)],
            [("counts", [P, NT, N], f32)],
            [("z1", [P, NT, D], f32), ("x1", [P, NT, D], f32)],
            [("v_hi", [P, 2, 4, D], f32r), ("v_lo", [P, 2, 4, D], f32r)],
            [("wg_hi", [P, 2, KC, 2, 256], f32r), ("wg_lo", [P, 2, KC, 2, 256], f32r)])
        (x0T,), (sums,), (xs,), (kT_hi, kT_lo, pT), (wf_hi, wf_lo) = overlay(
            [("x0T", [P, KC, N], f32)],
            [("sums", [P, NT, HALF], f32)],
            [("xs", [P, NT, D], f32)],
            [("kT_hi", [P, 2 * M], f32r), ("kT_lo", [P, 2 * M], f32r),
             ("pT", [P, 4, 2, P], f32r)],
            [("wf_hi", [P, 2, 2, D], f32r), ("wf_lo", [P, 2, 2, D], f32r)])
        (oh_s, oh_d, iota, shift, minus), (xs_hi,), (pe_, pn, q_sb, z2, xT2_hi, xT2_lo), (f0_hi, f0_lo) = overlay(
            [("oh_s", [P, 4, N], f16), ("oh_d", [P, 4, HALF], f16), ("iota", [P, N], f16),
             ("shift", [P, HALF], f16), ("minus", [P, P], f16)],
            [("xs_hi", [P, NT, D], f32r)],
            [("p_exp", [P, 2, M], f32), ("p_norm", [P, 2, M], f32), ("q_sb", [P, D], f32),
             ("z2", [P, D], f32), ("xT2_hi", [P, KC, P], f32r), ("xT2_lo", [P, KC, P], f32r)],
            [("f0_hi", [P, 2, N], f32r), ("f0_lo", [P, 2, N], f32r)])
        (c_in,), (xs_lo,), (z3,), (f1_hi, f1_lo) = overlay(
            [("c_in", [P, 2, KC * 2 * M], f32)],
            [("xs_lo", [P, NT, D], f32r)],
            [("z3", [P, NT, D], f32)],
            [("f1_hi", [P, 2, N], f32r), ("f1_lo", [P, 2, N], f32r)])
        (ends_i, ends_f), (qbd_hi, qbd_lo), (gel, ff) = overlay(
            [("ends_i", [P, 2, CHUNKS], i32), ("ends_f", [P, 4, CHUNKS], f32)],
            [("qbd_hi", [P, PAIRS, 2, P], f32r), ("qbd_lo", [P, PAIRS, 2, P], f32r)],
            [("gel", [P, 2, D], f32), ("ff", [P, 2, D], f32)])

        yT_hi = w_hi[:, 1:3].rearrange("p a c n -> p (a c n)").rearrange("p (k n) -> p k n", n=N)
        yT_lo = w_lo[:, 1:3].rearrange("p a c n -> p (a c n)").rearrange("p (k n) -> p k n", n=N)
        f_hi, f_lo = [f0_hi, f1_hi], [f0_lo, f1_lo]

        ps = ctx.enter_context(nc.psum_tensor("ps", [P, 8, 512], f32))
        K_BANK, V_BANK, S_BANK, T_BANK, PV_BANK, X_BANK, Y_BANK = 0, 1, 2, 3, 4, 6, 7

        cond_s = [nc.dram_tensor(f"cond_{part}_s", [GROUPS, P, KC * 2 * M], f32, kind="Internal").ap()
                  for part in ("hi", "lo")]
        at_s = [nc.dram_tensor(f"at_{part}_s", [P, NT * N], f32, kind="Internal").ap()
                for part in ("hi", "lo")]
        res_s = nc.dram_tensor("res_s", [N, D], f32, kind="Internal").ap()

        x_in = [sem("x_in0"), sem("x_in1")]
        cols_in, ends_in, row_in = sem("cols_in"), sem("ends_in"), sem("row_in")
        stage_in = [sem("stage_in0"), sem("stage_in1")]
        c_in_in = [sem("c_in_in0"), sem("c_in_in1")]
        cond_out = [sem("cond_out0"), sem("cond_out1")]
        cond_in = [sem("cond_in0"), sem("cond_in1")]
        res_out = [sem("res_out0"), sem("res_out1")]
        res_in = [sem("res_in0"), sem("res_in1")]
        at_out, at_in, out_done = sem("at_out"), sem("at_in"), sem("out_done")
        waited = sem("waited")
        const_ok, ones_ok, iota_ok, ends_ok = sem("const_ok"), sem("ones_ok"), sem("iota_ok"), sem("ends_ok")
        ln = sem("ln")
        rs = sem("rs")
        x_ln, x_rs, x1_ok = sem("x_ln"), sem("x_rs"), sem("x1_ok")
        x0_ok, res_ok, x0_mm, x0T_ok = sem("x0_ok"), sem("res_ok"), sem("x0_mm"), sem("x0T_ok")
        bn_ok, bnf_ok, y_hi, y_lo = sem("bn_ok"), sem("bnf_ok"), sem("y_hi"), sem("y_lo")
        c_hi, c_lo = sem("c_hi"), sem("c_lo")
        oh_ok, oh_used, a_mm, a_hi, a_lo = sem("oh_ok"), sem("oh_used"), sem("a_mm"), sem("a_hi"), sem("a_lo")
        a_sums, a_round, a_digit, a_low, a_dec = (sem("a_sums"), sem("a_round"), sem("a_digit"),
                                                  sem("a_low"), sem("a_dec"))
        a_lo_odd, xs_lo_odd, agg_half = sem("a_lo_odd"), sem("xs_lo_odd"), sem("agg_half")
        row_mm, row_ok = sem("row_mm"), sem("row_ok")
        deg_mm, deg_ok, dinv_ok = sem("deg_mm"), sem("deg_ok"), sem("dinv_ok")
        g_mm, xs_ok, xs_hi_ok, xs_lo_ok, agg_mm, agg_s, gcn_ok = (
            sem("g_mm"), sem("xs_ok"), sem("xs_hi_ok"), sem("xs_lo_ok"), sem("agg_mm"), sem("agg_s"),
            sem("gcn_ok"))
        hT_mm = sem("hT_mm")
        w_hi_ok, w_ok = sem("w_hi_ok"), sem("w_ok")
        k_mm, k_hi_ok, k_ok = sem("k_mm"), sem("k_hi_ok"), sem("k_ok")
        v_mm, v_hi_ok, v_ok = sem("v_mm"), sem("v_hi_ok"), sem("v_ok")
        s_mm, mx_ok, exp_ok, rinv_ok, pn_ok = (sem("s_mm"), sem("mx_ok"), sem("exp_ok"), sem("rinv_ok"),
                                               sem("pn_ok"))
        t_mm, pT_hi_ok, pT_ok, pv_mm = sem("t_mm"), sem("pT_hi_ok"), sem("pT_ok"), sem("pv_mm")
        z2_ok, t2_mm, full2_ok, x2_hi_ok, x2_ok = (sem("z2_ok"), sem("t2_mm"), sem("full2_ok"),
                                                   sem("x2_hi_ok"), sem("x2_ok"))
        q_mm, q_ok, qt_mm, qb_hi_ok, qb_ok, qb_zero = (sem("q_mm"), sem("q_ok"), sem("qt_mm"),
                                                       sem("qb_hi_ok"), sem("qb_ok"), sem("qb_zero"))
        o_part_ok = sem("o_part_ok")
        o_hi_ok, o_ok, wo_mm, h_att, z3_ok, h_bias = (sem("o_hi_ok"), sem("o_ok"), sem("wo_mm"),
                                                      sem("h_att"), sem("z3_ok"), sem("h_bias"))
        t3_mm, full3_ok, x3_hi_ok, x3_ok = sem("t3_mm"), sem("full3_ok"), sem("x3_hi_ok"), sem("x3_ok")
        u_mm, gel_ok, ff_ok, f_hi_ok, f_ok, ffo_mm, h_ffo = (
            sem("u_mm"), sem("gel_ok"), sem("ff_ok"), sem("f_hi_ok"), sem("f_ok"), sem("ffo_mm"),
            sem("h_ffo"))

        block = ctx.enter_context(nc.Block())

        def wait_apart(eng, on, value):
            eng.wait_ge(on, value)
            eng.sem_inc(waited, 1)

        def bits(ap):
            return ap.bitcast(f32)

        T3_BANK = [6, 6, 1, 1, 0, 0, 4, 5]

        def step_bank(j, a, s, v):
            return (6, 1)[v] if isinstance(j, int) and (j, a, s) == (0, 0, 0) else 2 * (s % 2) + v

        def attn_place(part, which, half):
            return (w_hi, w_lo)[part][:, which, 2 * half:2 * half + 2, :].rearrange("p k n -> p (k n)")

        def up_place(part, a, r):
            return (wg_hi, wg_lo)[part][:, a, 2 * r:2 * r + 2].rearrange("p k v n -> p (k v n)")

        def mlp_place(part, j, a, s):
            if s == 0:
                return (wf_hi, wf_lo)[part][:, a].rearrange("p c n -> p (c n)")
            if s == 3 or (isinstance(j, int) and 2 * j + a == MG - 1):
                return attn_place(part, j, a)
            return up_place(part, 1 - a, s - 1)

        @block.sync
        def _(sp):
            sp.dma_start(ends_i[:, 0, :], src).then_inc(ends_in, 16)
            sp.dma_start(ends_i[:, 1, :], dst).then_inc(ends_in, 16)
            for half in range(2):
                r = slice(half * NT // 2, (half + 1) * NT // 2)
                sp.dma_start(h[:, r, :], x.rearrange("(t p) d -> p t d", p=P)[:, r, :]).then_inc(x_in[half], 16)
            sp.dma_start(cols_sb[:, :], cols).then_inc(cols_in, 16)
            sp.dma_start(bias_row[:, :], rows[0:1, :].partition_broadcast(P)).then_inc(row_in, 16)

            def piece(n, slot, first=False):
                if not first:
                    sp.wait_ge(w_ok, n - 1)
                sp.dma_start(stage[:, slot, :], pieces[n]).then_inc(stage_in[slot], 16)

            piece(0, 0, True)
            piece(1, 1, True)
            sp.dma_start(c_in[:, 0, :], condT[0].rearrange("p k n -> p (k n)")).then_inc(c_in_in[0], 16)
            for g in range(GROUPS):
                s = g % 2
                if g + 1 < GROUPS:
                    if g:
                        sp.wait_ge(c_lo, g)
                    sp.dma_start(c_in[:, 1 - s, :], condT[g + 1].rearrange("p k n -> p (k n)"))\
                      .then_inc(c_in_in[1 - s], 16)
                sp.wait_ge(c_lo, g + 1)
                for part, buf in zip(cond_s, (cond_hi, cond_lo)):
                    sp.dma_start(part[g], bits(buf[s][:, :, :].rearrange("p k n -> p (k n)"))).then_inc(cond_out[s], 16)
                if g in (1, 2):
                    r = slice((g - 1) * NT // 2, g * NT // 2)
                    sp.wait_ge(x1_ok, g * NT // 2)
                    sp.dma_start(res_s.rearrange("(t p) d -> p t d", p=P)[:, r, :], x1[:, r, :])\
                      .then_inc(res_out[g - 1], 16)
            for n in range(2, 4):
                piece(n, n % 2)
            sp.wait_ge(a_lo, NT // 2)
            sp.wait_ge(a_lo_odd, NT // 2)
            for part, buf in zip(at_s, (at_hi, at_lo)):
                sp.dma_start(part, bits(buf[:, :, :].rearrange("p t n -> p (t n)"))).then_inc(at_out, 16)
            for n in range(4, FIRST_PIECES):
                piece(n, n % 2)

            def load_cond(g, slot):
                for part, buf in zip(cond_s, (cond_hi, cond_lo)):
                    sp.dma_start(bits(buf[slot][:, :, :].rearrange("p k n -> p (k n)")), part[g])\
                      .then_inc(cond_in[slot], 16)

            sp.wait_ge(at_out, 32)
            sp.wait_ge(agg_half, 1)
            load_cond(0, 0)
            sp.wait_ge(agg_mm, NT)
            load_cond(1, 1)
            sp.wait_ge(gcn_ok, NT)
            sp.dma_start(bias_row[:, :], rows[1:2, :].partition_broadcast(P)).then_inc(row_in, 16)
            with sp.Fori(0, L) as l:
                with sp.Fori(1, GROUPS // 2) as i:
                    for a in range(2):
                        sp.wait_ge(k_mm, UNITS * l + 2 * PAIRS * i + PAIRS * (a - 1))
                        load_cond(2 * i + a, a)
                with sp.Fori(0, MG // 2) as j:
                    for a in range(2):
                        for r in range(4):
                            n = FIRST_PIECES + PIECES * l + 8 * j + 4 * a + r
                            sp.wait_ge(w_ok, n - 1)
                            sp.dma_start(stage[:, r % 2, :], pieces[n]).then_inc(stage_in[r % 2], 16)
                sp.wait_ge(h_bias, GROUPS * l + GROUPS)
                sp.dma_start(bias_row[:, :], rows[bass.ds(2 + l, 1), :].partition_broadcast(P)).then_inc(row_in, 16)
                for half in range(2):
                    sp.wait_ge(u_mm, 32 * l + 30 + 2 * half)
                    load_cond(half, half)

            for slot in range(2):
                sp.wait_ge(cond_in[slot], 128 * L + 32)
            for part, buf in zip(at_s, (at_hi, at_lo)):
                sp.dma_start(bits(buf[:, :, :].rearrange("p t n -> p (t n)")), part).then_inc(at_in, 16)
            sp.wait_ge(w_ok, FIRST_PIECES + PIECES * L)
            for half, buf in enumerate((w_hi, w_lo)):
                r = slice(half * NT // 2, (half + 1) * NT // 2)
                sp.dma_start(bits(buf[:, 3]), res_s.rearrange("(t p) d -> p t d", p=P)[:, r, :])\
                  .then_inc(res_in[half], 16)
            for t in range(NT):
                sp.wait_ge(res_ok, t + 1)
                sp.dma_start(out[t * P:(t + 1) * P, :], h[:, t, :]).then_inc(out_done, 16)
            sp.wait_ge(out_done, 16 * NT)
            for s in range(2):
                sp.wait_ge(res_out[s], 16)
                sp.wait_ge(cond_out[s], 32 * GROUPS // 2)

        @block.gpsimd
        def _(pool):
            pool.sem_inc(f_ok, 2)
            pool.sem_inc(x3_ok, 2)
            pool.memset(ident[:, :], 0.0).then_inc(const_ok, 1)
            pool.memset(mhalf[:, :], -0.5).then_inc(const_ok, 1)
            pool.wait_ge(const_ok, 2)
            pool.affine_select(out=ident[:, :], in_=ident[:, :], compare_op=ALU.not_equal, fill=1.0, base=0,
                               pattern=[[-1, P]], channel_multiplier=1).then_inc(const_ok, 1)
            pool.memset(shift[:, :], SHIFT).then_inc(const_ok, 1)
            pool.memset(minus[:, :], -2 * SHIFT).then_inc(const_ok, 1)
            pool.iota(iota[:, :], pattern=[[1, N]], base=0, channel_multiplier=0,
                      allow_small_or_imprecise_dtypes=True).then_inc(iota_ok, 1)

            def rsqrt(k):
                wait_apart(pool, ln, 2 * k + 2)
                pool.tensor_scalar(veps[:, :], mv[:, 1:2], EPS, None, ALU.add).then_inc(rs, 1)
                pool.wait_ge(rs, 2 * k + 1)
                pool.tensor_tensor(rstd[:, :], veps[:, :], mhalf[:, 0:1], ALU.pow).then_inc(rs, 1)

            def w_low(n, slot, hi, lo):
                pool.wait_ge(w_hi_ok, n + 1)
                pool.tensor_tensor(lo, stage[:, slot, :], bits(hi), ALU.subtract).then_inc(w_ok, 1)

            for half in range(2):
                r = slice(half * NT // 2, (half + 1) * NT // 2)
                pool.wait_ge(x_ln, NT * half + NT)
                pool.tensor_scalar(x_veps[:, r], x_mv[:, r, 1], EPS, None, ALU.add).then_inc(x_rs, 1)
                pool.wait_ge(x_rs, 2 * half + 1)
                pool.tensor_tensor(x_rstd[:, r], x_veps[:, r], mhalf[:, r], ALU.pow).then_inc(x_rs, 1)

            def cond_low(g):
                s = g % 2
                if g >= 2:
                    pool.wait_ge(cond_out[s], 32 * (g // 2))
                pool.wait_ge(c_hi, g + 1)
                pool.tensor_tensor(cond_lo[s][:, :, :].rearrange("p k n -> p (k n)"), c_in[:, s, :],
                                   bits(cond_hi[s][:, :, :].rearrange("p k n -> p (k n)")), ALU.subtract)\
                    .then_inc(c_lo, 1)

            for k in range(KC):
                rsqrt(k)
                pool.wait_ge(y_hi, k + 1)
                pool.tensor_tensor(yT_lo[:, k, :], full[:, :, :].rearrange("p a n -> p (a n)"),
                                   bits(yT_hi[:, k, :]), ALU.subtract).then_inc(y_lo, 1)
                cond_low(k)
            for n in range(2):
                w_low(n, n, attn_place(0, 0, n), attn_place(1, 0, n))
            for g in range(KC, GROUPS):
                cond_low(g)
            def zero_q():
                pool.memset(bits(qbd_hi[:, :, :, :]), 0.0).then_inc(qb_zero, 1)
                pool.memset(bits(qbd_lo[:, :, :, :]), 0.0).then_inc(qb_zero, 1)

            for t in range(0, NT, 2):
                pool.wait_ge(a_hi, t + 1)
                pool.tensor_tensor(at_lo[:, t, :], counts[:, t, :], bits(at_hi[:, t, :]), ALU.subtract)\
                    .then_inc(a_lo, 1)
            zero_q()
            pool.wait_ge(deg_ok, 1)
            pool.tensor_tensor(dinv[:, :], deg[:, :], mhalf[:, :], ALU.pow).then_inc(dinv_ok, 1)

            def xs_split(use):
                for t in range(0, NT, 2):
                    pool.wait_ge(xs_hi_ok, NT * use + t + 1)
                    pool.tensor_tensor(xs_lo[:, t, :], xs[:, t, :], bits(xs_hi[:, t, :]), ALU.subtract)\
                        .then_inc(xs_lo_ok, 1)

            xs_split(0)
            for n in range(2, FIRST_PIECES):
                w_low(n, n % 2, attn_place(0, (n - 2) // 2, n % 2), attn_place(1, (n - 2) // 2, n % 2))

            with pool.Fori(0, L) as l:
                norm0 = KC + 2 * NT * l

                def x2_low(g):
                    pool.wait_ge(x2_hi_ok, GROUPS * l + g + 1)
                    pool.tensor_tensor(xT2_lo[:, :, :].rearrange("p k n -> p (k n)"), full[:, 0, :],
                                       bits(xT2_hi[:, :, :].rearrange("p k n -> p (k n)")),
                                       ALU.subtract).then_inc(x2_ok, 1)

                rsqrt(norm0)
                x2_low(0)
                rsqrt(norm0 + 1)
                x2_low(1)
                with pool.Fori(1, GROUPS - 1) as g:
                    rsqrt(norm0 + 2 * g)
                    rsqrt(norm0 + 2 * g + 1)
                    x2_low(g + 1)

                def x3_low(t):
                    r = slice(t % 4 * P, (t % 4 + 1) * P)
                    pool.wait_ge(x3_hi_ok, NT * l + t + 1)
                    pool.tensor_tensor(xT3_lo[t // 4][:, :, r],
                                       full[:, t % 2, :].rearrange("p (k n) -> p k n", n=P),
                                       bits(xT3_hi[t // 4][:, :, r]), ALU.subtract).then_inc(x3_ok, 1)

                def f_low(j, a, s):
                    half, c = s // 2, s % 2
                    pool.wait_ge(f_hi_ok, 32 * l + 8 * j + 4 * a + s + 1)
                    pool.tensor_tensor(f_lo[a][:, c, half * HALF:(half + 1) * HALF], ff[:, s % 2, :],
                                       bits(f_hi[a][:, c, half * HALF:(half + 1) * HALF]),
                                       ALU.subtract).then_inc(f_ok, 1)

                def weights_low(j, a, s):
                    w_low(FIRST_PIECES + PIECES * l + 8 * j + 4 * a + 2 + s, s % 2,
                          mlp_place(0, j, a, s), mlp_place(1, j, a, s))

                def mlp_step(j, a, s, weights=True):
                    if weights:
                        weights_low(j, a, s)
                    f_low(j, a, s)

                def mlp_group(j, a, last=False):
                    for s in range(4):
                        mlp_step(j, a, s, not (last and s >= 2))

                x3_low(0)
                x3_low(1)
                for r in range(2):
                    w_low(FIRST_PIECES + PIECES * l + r, r, up_place(0, 0, r), up_place(1, 0, r))
                    if r == 0:
                        rsqrt(norm0 + 2 * NT - 2)
                for t in range(2, 7):
                    x3_low(t)
                rsqrt(norm0 + 2 * NT - 1)
                weights_low(0, 0, 0)
                x3_low(7)
                f_low(0, 0, 0)
                mlp_step(0, 0, 1)
                mlp_step(0, 0, 2)
                mlp_step(0, 0, 3)
                mlp_group(0, 1)
                with pool.Fori(1, MG // 2 - 1) as j:
                    mlp_group(j, 0)
                    mlp_group(j, 1)
                mlp_group(MG // 2 - 1, 0)
                mlp_group(MG // 2 - 1, 1, last=True)
                wait_apart(pool, f_ok, 2 + 32 * l + 32)
                zero_q()

            for t in range(NT):
                pool.wait_ge(y_hi, KC + t + 1)
                pool.tensor_tensor(yT_lo[:, :, t * P:(t + 1) * P],
                                   full[:, t % 2, :].rearrange("p (k n) -> p k n", n=P),
                                   bits(yT_hi[:, :, t * P:(t + 1) * P]), ALU.subtract).then_inc(y_lo, 1)
            xs_split(1)

        @block.scalar
        def _(act):
            def w_high(n, slot, place):
                wait_apart(act, stage_in[slot], 8 * n + (16 if slot == 0 else 8))
                act.activation(place, stage[:, slot, :], ACT.Copy).then_inc(w_hi_ok, 1)

            for t in range(NT):
                act.wait_ge(x0_mm, t + 1)
                act.activation(x0T[:, :, t * P:(t + 1) * P],
                               ps[:, t, :].rearrange("p (k n) -> p k n", n=P), ACT.Relu)\
                    .then_inc(x0T_ok, 1)

            def cond_high(g):
                s = g % 2
                if g >= 2:
                    act.wait_ge(cond_out[s], 32 * (g // 2))
                act.wait_ge(c_in_in[s], 16 * (g // 2 + 1))
                act.activation(cond_hi[s][:, :, :].rearrange("p k n -> p (k n)"), c_in[:, s, :], ACT.Copy)\
                    .then_inc(c_hi, 1)

            for k in range(KC):
                act.wait_ge(bnf_ok, k + 1)
                act.activation(yT_hi[:, k, :], full[:, :, :].rearrange("p a n -> p (a n)"), ACT.Copy)\
                    .then_inc(y_hi, 1)
                cond_high(k)
            for n in range(2):
                w_high(n, n, attn_place(0, 0, n))
            act.wait_ge(cols_in, 16)
            act.activation(ones[:, :], cols_sb[:, 0:2], ACT.Copy, bias=1.0, scale=0.0).then_inc(ones_ok, 1)

            def a_digits(f):
                for t in range(NT):
                    act.wait_ge(a_sums, NT * f + t + 1)
                    if not isinstance(f, int) or f:
                        act.wait_ge(a_dec, NT * f - NT + t + 1)
                    act.activation(h[:, t, :], sums[:, t, :], ACT.Copy, bias=ROUND, scale=1 / DIGIT)\
                        .then_inc(a_round, 1)
                for t in range(NT):
                    wait_apart(act, a_round, NT * f + t + 1)
                    act.activation(h[:, t, :], h[:, t, :], ACT.Copy, bias=-ROUND).then_inc(a_digit, 1)

            act.wait_ge(x1_ok, NT)
            a_digits(0)
            for g in range(KC, GROUPS):
                cond_high(g)
            with act.Fori(1, FLUSHES) as f:
                a_digits(f)
            for s in range(2):
                act.wait_ge(cond_out[s], 32 * GROUPS // 2)
            for t in range(NT):
                act.wait_ge(a_dec, NT * FLUSHES - NT + t + 1)
                act.activation(at_hi[:, t, :], counts[:, t, :], ACT.Copy).then_inc(a_hi, 1)

            def xs_high(use):
                for t in range(NT):
                    act.wait_ge(xs_ok, NT * use + t + 1)
                    act.activation(xs_hi[:, t, :], xs[:, t, :], ACT.Copy).then_inc(xs_hi_ok, 1)

            xs_high(0)
            act.wait_ge(g_mm, NT)
            for n in range(2, FIRST_PIECES):
                w_high(n, n % 2, attn_place(0, (n - 2) // 2, n % 2))

            with act.Fori(0, L) as l:
                def v_high(u, mc, slot, bank=V_BANK):
                    act.wait_ge(v_mm, u + 1)
                    act.activation(v_hi[:, slot, mc, :], ps[:, bank, :], ACT.Copy).then_inc(v_hi_ok, 1)

                def k_high(u):
                    act.wait_ge(k_mm, u + 1)
                    act.activation(kT_hi[:, :], ps[:, K_BANK, :], ACT.Copy).then_inc(k_hi_ok, 1)

                def x2_high(g):
                    act.wait_ge(full2_ok, g + 1)
                    act.activation(xT2_hi[:, :, :].rearrange("p k n -> p (k n)"), full[:, 0, :], ACT.Copy)\
                        .then_inc(x2_hi_ok, 1)

                def q_copy(g):
                    act.wait_ge(q_mm, g + 1)
                    act.activation(q_sb[:, :], ps[:, Y_BANK, :], ACT.Copy, scale=Q_SCALE).then_inc(q_ok, 1)

                def q_high(g):
                    act.wait_ge(qt_mm, g + 1)
                    for e in range(2):
                        r = slice(64 * e, 64 * e + 64)
                        last = act.activation(
                            qbd_hi[r, :, :, r],
                            ps[r, X_BANK, :].rearrange("d (p b n) -> d p b n", p=PAIRS, b=2), ACT.Copy)
                    last.then_inc(qb_hi_ok, 1)

                def o_high(g):
                    act.wait_ge(o_part_ok, 2 + PAIRS * g + PAIRS)
                    act.activation(oT_hi[:, :, :], o_full[:, :, :], ACT.Copy).then_inc(o_hi_ok, 1)

                def x3_high(t):
                    act.wait_ge(t3_mm, NT * l + t + 1)
                    wait_apart(act, x3_ok, NT * l + t + 1)
                    for k in range(KC):
                        last = act.activation(full[:, t % 2, k * P:(k + 1) * P],
                                              ps[:, T3_BANK[t], k * P:(k + 1) * P], ACT.Identity,
                                              scale=cols_sb[:, bass.ds(COL["ln3_w"] + KC * l + k, 1)],
                                              bias=cols_sb[:, bass.ds(COL["ln3_b"] + KC * l + k, 1)])
                    last.then_inc(full3_ok, 1)
                    act.wait_ge(full3_ok, NT * l + t + 1)
                    act.activation(xT3_hi[t // 4][:, :, t % 4 * P:(t % 4 + 1) * P],
                                   full[:, t % 2, :].rearrange("p (k n) -> p k n", n=P), ACT.Copy)\
                        .then_inc(x3_hi_ok, 1)

                def unit(u, g, p, par, last=False, first=False, opens_last=False):
                    act.wait_ge(mx_ok, u + 1)
                    for b in range(2):
                        e = act.activation(pe_[:, b, :], ps[:, S_BANK, b * M:(b + 1) * M], ACT.Exp,
                                           bias=nmx[:, b:b + 1], accum_out=rsum[:, b:b + 1])
                    e.then_inc(exp_ok, 1)
                    if not (last and p == 3):
                        k_high(u + 1)
                    if opens_last:
                        x3_high(0)
                    if p == 2 and last:
                        x3_high(3)
                    if p == 3 and last:
                        x3_high(4)
                    if p == 3 and not last:
                        q_high(g + 1)
                    if p == 0 and not first:
                        o_high(g - 1)
                    if not (last and p >= 1 or first):
                        v_high(u + 3, (p + 3) % 4, par if p == 0 else 1 - par)
                    if opens_last:
                        x3_high(1)
                    if p == 1 and last:
                        for r in range(2):
                            w_high(FIRST_PIECES + PIECES * l + r, r, up_place(0, 0, r))
                    act.wait_ge(t_mm, u + 1)
                    act.activation(pT[:, :, 0, :], ps[:, T_BANK, :].rearrange("p (c n) -> p c n", n=P),
                                   ACT.Copy)\
                        .then_inc(pT_hi_ok, 1)
                    if p == 1 and not last:
                        x2_high(g + 1)
                    if p == 2 and not last:
                        q_copy(g + 1)
                    if p == 1 and last:
                        x3_high(2)
                    if p == 3 and last:
                        x3_high(5)

                def body(g, par, last=False):
                    u, gg = UNITS * l + PAIRS * g, GROUPS * l + g
                    for p in range(1, 4):
                        unit(u + p, gg, p, par, last)
                    if not last:
                        unit(u + 4, gg + 1, 0, 1 - par, opens_last=isinstance(g, int) and g == GROUPS - 2)

                for mc in range(2):
                    v_high(UNITS * l + mc, mc, 0, V_BANK + mc)
                x2_high(GROUPS * l)
                v_high(UNITS * l + 2, 2, 0, V_BANK + 2)
                k_high(UNITS * l)
                q_copy(GROUPS * l)
                act.wait_ge(qb_zero, 2 * l + 2)
                q_high(GROUPS * l)
                v_high(UNITS * l + 3, 3, 0, V_BANK + 3)
                unit(UNITS * l, GROUPS * l, 0, 0, first=True)
                with act.Fori(0, GROUPS // 2 - 1) as i:
                    body(2 * i, 0)
                    body(2 * i + 1, 1)
                body(GROUPS - 2, 0)
                body(GROUPS - 1, 1, last=True)
                o_high(GROUPS * l + GROUPS - 1)

                def gelu(j, a, s, weights=True):
                    b = COL["geglu_b"] + 32 * l + 16 + 4 * j + 2 * a + s % 2
                    wait_apart(act, u_mm, 32 * l + 8 * j + 4 * a + s + 1)
                    act.activation(gel[:, s % 2, :], ps[:, step_bank(j, a, s, 1), :], ACT.Gelu,
                                   bias=cols_sb[:, bass.ds(b, 1)]).then_inc(gel_ok, 1)
                    if weights:
                        w_high(FIRST_PIECES + PIECES * l + 8 * j + 4 * a + 2 + s, s % 2, mlp_place(0, j, a, s))

                def f_high(j, a, s):
                    half, c = s // 2, s % 2
                    act.wait_ge(ff_ok, 32 * l + 8 * j + 4 * a + s + 1)
                    act.activation(f_hi[a][:, c, half * HALF:(half + 1) * HALF], ff[:, s % 2, :], ACT.Copy)\
                        .then_inc(f_hi_ok, 1)

                def mlp_step(j, a, s, weights=True):
                    gelu(j, a, s, weights)
                    f_high(j, a, s)

                def mlp_group(j, a, last=False):
                    for s in range(4):
                        mlp_step(j, a, s, not (last and s >= 2))

                x3_high(6)
                gelu(0, 0, 0)
                x3_high(7)
                f_high(0, 0, 0)
                mlp_step(0, 0, 1)
                mlp_step(0, 0, 2)
                mlp_step(0, 0, 3)
                mlp_group(0, 1)
                with act.Fori(1, MG // 2 - 1) as j:
                    mlp_group(j, 0)
                    mlp_group(j, 1)
                mlp_group(MG // 2 - 1, 0)
                mlp_group(MG // 2 - 1, 1, last=True)

            act.wait_ge(w_ok, FIRST_PIECES + PIECES * L)
            for t in range(NT):
                act.wait_ge(bnf_ok, KC + t + 1)
                act.activation(yT_hi[:, :, t * P:(t + 1) * P],
                               full[:, t % 2, :].rearrange("p (k n) -> p k n", n=P), ACT.Copy)\
                    .then_inc(y_hi, 1)
            xs_high(1)

        @block.vector
        def _(dve):
            dve.sem_inc(o_part_ok, 2)
            dve.sem_inc(h_att, 1)

            def norm_stats(k, parts):
                for n, part in enumerate(parts):
                    st = dve.bn_stats(stats[:, n, :], part)
                st.then_inc(ln, 1)
                wait_apart(dve, ln, 2 * k + 1)
                dve.bn_aggr(mv[:, :], stats[:, 0:len(parts), :].rearrange("p a s -> p (a s)"))\
                    .then_inc(ln, 1)

            def norm_wait(k):
                dve.wait_ge(ln, 2 * k + 2)
                dve.wait_ge(rs, 2 * k + 2)

            def norm(k, parts):
                norm_stats(k, parts)
                norm_wait(k)

            dve.wait_ge(ends_in, 32)
            dve.tensor_copy(ends_f[:, 0, :], ends_i[:, 0, :]).then_inc(ends_ok, 1)
            dve.tensor_copy(ends_f[:, 3, :], ends_i[:, 1, :]).then_inc(ends_ok, 1)
            dve.wait_ge(ends_ok, 2)
            dve.tensor_scalar(ends_f[:, 2, :], ends_f[:, 3, :], float(HALF), None, ALU.is_ge).then_inc(ends_ok, 1)
            dve.wait_ge(ends_ok, 3)
            dve.scalar_tensor_tensor(ends_f[:, 1, :], ends_f[:, 2, :], -float(HALF), ends_f[:, 3, :],
                                     ALU.mult, ALU.add).then_inc(ends_ok, 1)
            dve.wait_ge(ends_ok, 4)
            dve.tensor_scalar(ends_f[:, 2, :], ends_f[:, 2, :], DIGIT - 1, 1.0, ALU.mult, ALU.add)\
                .then_inc(ends_ok, 1)

            for half in range(2):
                tiles = range(half * NT // 2, (half + 1) * NT // 2)
                dve.wait_ge(x_in[half], 16)
                for t in tiles:
                    dve.bn_stats(x_stats[:, t, :], h[:, t, :]).then_inc(x_ln, 1)
                dve.wait_ge(x_ln, NT * half + NT // 2)
                for t in tiles:
                    dve.bn_aggr(x_mv[:, t, :], x_stats[:, t, :]).then_inc(x_ln, 1)
            dve.wait_ge(x_ln, 2 * NT)
            for t in range(NT):
                dve.wait_ge(x_rs, 2 * (t // (NT // 2)) + 2)
                dve.tensor_scalar(z1[:, t, :], h[:, t, :], x_mv[:, t, 0:1], x_rstd[:, t:t + 1],
                                  ALU.subtract, ALU.mult).then_inc(x0_ok, 1)

            def x_sum(t):
                dve.wait_ge(x0_ok, t + 1)
                dve.scalar_tensor_tensor(x1[:, t, :], z1[:, t, :], 0.0, h[:, t, :], ALU.max, ALU.add)\
                    .then_inc(x1_ok, 1)

            def batchnorm(k):
                norm(k, [x0T[:, k, 0:HALF], x0T[:, k, HALF:N]])
                sc, sh = bn[:, 2 * k:2 * k + 1], bn[:, 2 * k + 1:2 * k + 2]
                w, b = (cols_sb[:, COL[n] + k:COL[n] + k + 1] for n in ("bn_w", "bn_b"))
                dve.tensor_scalar(sc, rstd[:, :], w, None, ALU.mult).then_inc(bn_ok, 1)
                dve.wait_ge(bn_ok, 3 * k + 1)
                dve.tensor_scalar(sh, mv[:, 0:1], sc, None, ALU.mult).then_inc(bn_ok, 1)
                dve.wait_ge(bn_ok, 3 * k + 2)
                dve.tensor_tensor(sh, b, sh, ALU.subtract).then_inc(bn_ok, 1)
                dve.wait_ge(bn_ok, 3 * k + 3)
                if k:
                    dve.wait_ge(y_lo, k)
                dve.tensor_scalar(full[:, :, :].rearrange("p a n -> p (a n)"), x0T[:, k, :], sc, sh,
                                  ALU.mult, ALU.add).then_inc(bnf_ok, 1)

            def one_hots(n, counted):
                for c in range(4):
                    dve.wait_ge(oh_used, counted + c + 1)
                    dve.tensor_scalar(oh_s[:, c, :], iota[:, :], ends_f[:, 0, bass.ds(n + c, 1)],
                                      None, ALU.is_equal)
                    dve.tensor_scalar(oh_d[:, c, :], iota[:, 0:HALF], ends_f[:, 1, bass.ds(n + c, 1)],
                                      ends_f[:, 2, bass.ds(n + c, 1)], ALU.is_equal, ALU.mult)\
                        .then_inc(oh_ok, 1)

            def take_sums(f):
                if not isinstance(f, int) or f:
                    wait_apart(dve, a_low, NT * f)
                    wait_apart(dve, a_dec, NT * f)
                for t in range(NT):
                    dve.wait_ge(a_mm, NT * f + t + 1)
                    dve.tensor_copy(sums[:, t, :], ps[:, t, :]).then_inc(a_sums, 1)

            def add_digits(f, t, first=False):
                one = slice(t, t + 1) if isinstance(t, int) else bass.ds(t, 1)
                low, high = counts[:, one, 0:HALF], counts[:, one, HALF:N]
                wait_apart(dve, a_digit, NT * f + t + 1)
                if first:
                    dve.scalar_tensor_tensor(low, h[:, one, :], -DIGIT, sums[:, one, :], ALU.mult, ALU.add)\
                        .then_inc(a_low, 1)
                    dve.tensor_scalar(high, h[:, one, :], OFFSET / DIGIT, None, ALU.add).then_inc(a_dec, 1)
                else:
                    dve.scalar_tensor_tensor(sums[:, one, :], h[:, one, :], -DIGIT, sums[:, one, :],
                                             ALU.mult, ALU.add).then_inc(a_low, 1)
                    dve.scalar_tensor_tensor(high, h[:, one, :], OFFSET / DIGIT, high, ALU.add, ALU.add)
                    wait_apart(dve, a_low, NT * f + t + 1)
                    dve.tensor_tensor(low, low, sums[:, one, :], ALU.add).then_inc(a_dec, 1)

            def a_low_odd(t):
                dve.wait_ge(a_hi, t + 1)
                dve.tensor_tensor(at_lo[:, t, :], counts[:, t, :], bits(at_hi[:, t, :]), ALU.subtract)\
                    .then_inc(a_lo_odd, 1)

            dve.wait_ge(iota_ok, 1)
            dve.wait_ge(ends_ok, 5)
            dve.wait_ge(cols_in, 16)
            for k in range(KC):
                for i in range(2):
                    one_hots(8 * k + 4 * i, 8 * k + 4 * i)
                if k == 0:
                    dve.wait_ge(x0T_ok, NT)
                batchnorm(k)
                for t in (range(0, 2), range(2, 5), range(5, NT), ())[k]:
                    x_sum(t)
            dve.wait_ge(bnf_ok, KC)
            take_sums(0)
            for half in range(2):
                dve.wait_ge(res_out[half], 16)
            with dve.Fori(0, NT) as t:
                one_hots(FLUSH + 4 * t, FLUSH - 1 + 4 * t)
                add_digits(0, t, first=True)
            take_sums(1)
            with dve.Fori(2, FLUSHES) as f:
                with dve.Fori(0, NT) as t:
                    one_hots(FLUSH * f + 4 * t, (FLUSH - 1) * f + 4 * t)
                    add_digits(f - 1, t)
                take_sums(f)
            for t in range(NT):
                add_digits(FLUSHES - 1, t)
                if t in (2, 4, 6):
                    a_low_odd(t - 1)
            a_low_odd(NT - 1)
            dve.wait_ge(row_mm, 1)
            for half in range(2):
                dve.tensor_copy(sums[0:2, half, :], ps[0:2, 7 - half, :]).then_inc(row_ok, 1)
            dve.wait_ge(deg_mm, 1)
            dve.tensor_scalar(deg[:, :], ps[:, 7, 0:2 * NT:2], 1.0, None, ALU.add).then_inc(deg_ok, 1)
            dve.wait_ge(dinv_ok, 1)

            def gcn(use):
                for half in range(2):
                    for t in range(half * NT // 2, (half + 1) * NT // 2):
                        dve.wait_ge(g_mm, NT * use + t + 1)
                        dve.tensor_scalar(xs[:, t, :], ps[:, t, :], dinv[:, t:t + 1], None, ALU.mult)\
                            .then_inc(xs_ok, 1)
                    for t in range(half * NT // 2 + 1, (half + 1) * NT // 2, 2):
                        dve.wait_ge(xs_hi_ok, NT * use + t + 1)
                        dve.tensor_tensor(xs_lo[:, t, :], xs[:, t, :], bits(xs_hi[:, t, :]), ALU.subtract)\
                            .then_inc(xs_lo_odd, 1)
                dve.wait_ge(row_in, 16 if use == 0 else 16 * (L + 2))
                for t in range(NT):
                    dve.wait_ge(agg_mm, NT * use + t + 1)
                    dve.tensor_tensor(xs[:, t, :], ps[:, t, :], xs[:, t, :], ALU.add).then_inc(agg_s, 1)
                    dve.wait_ge(agg_s, NT * use + t + 1)
                    dve.scalar_tensor_tensor(h[:, t, :], xs[:, t, :], dinv[:, t:t + 1], bias_row[:, :],
                                             ALU.mult, ALU.add).then_inc(gcn_ok, 1)
                    if use:
                        half = t // (NT // 2)
                        dve.wait_ge(gcn_ok, NT + t + 1)
                        dve.wait_ge(res_in[half], 16)
                        dve.tensor_tensor(h[:, t, :], h[:, t, :], bits((w_hi, w_lo)[half][:, 3, t % (NT // 2), :]),
                                          ALU.add).then_inc(res_ok, 1)

            gcn(0)
            dve.wait_ge(gcn_ok, NT)

            with dve.Fori(0, L) as l:
                norm0 = KC + 2 * NT * l

                def v_low(u, mc, slot, bank=V_BANK):
                    dve.wait_ge(v_hi_ok, u + 1)
                    dve.tensor_tensor(v_lo[:, slot, mc, :], ps[:, bank, :], bits(v_hi[:, slot, mc, :]),
                                      ALU.subtract).then_inc(v_ok, 1)

                def k_low(u):
                    dve.wait_ge(k_hi_ok, u + 1)
                    dve.tensor_tensor(kT_lo[:, :], ps[:, K_BANK, :], bits(kT_hi[:, :]), ALU.subtract)\
                        .then_inc(k_ok, 1)

                def x2_full(g):
                    dve.wait_ge(t2_mm, g + 1)
                    for k in range(KC):
                        last = dve.tensor_scalar(full[:, 0, k * P:(k + 1) * P], ps[:, X_BANK, k * P:(k + 1) * P],
                                                 cols_sb[:, bass.ds(COL["ln2_w"] + KC * l + k, 1)],
                                                 cols_sb[:, bass.ds(COL["ln2_b"] + KC * l + k, 1)],
                                                 ALU.mult, ALU.add)
                    last.then_inc(full2_ok, 1)

                def q_low(g):
                    dve.wait_ge(qb_hi_ok, g + 1)
                    for e in range(2):
                        r = slice(64 * e, 64 * e + 64)
                        last = dve.tensor_tensor(
                            qbd_lo[r, :, :, r], ps[r, X_BANK, :].rearrange("d (p b n) -> d p b n", p=PAIRS, b=2),
                            bits(qbd_hi[r, :, :, r]), ALU.subtract)
                    last.then_inc(qb_ok, 1)

                def o_part(u, p):
                    dve.wait_ge(pv_mm, u + 1)
                    for e in range(2):
                        r = slice(64 * e, 64 * e + 64)
                        o_ps = ps[r, PV_BANK + p % 2, :].rearrange("d (b t n) -> d b t n", b=2, t=2)
                        last = dve.tensor_reduce(o_full[r, p, :].rearrange("d (b n) -> d b n", b=2),
                                                 o_ps[:, :, :, r].rearrange("d b t n -> d b n t"), AX.X, ALU.add)
                    last.then_inc(o_part_ok, 1)

                def o_low(g):
                    dve.wait_ge(o_hi_ok, g + 1)
                    dve.tensor_tensor(oT_lo[:, :, :], o_full[:, :, :], bits(oT_hi[:, :, :]), ALU.subtract)\
                        .then_inc(o_ok, 1)

                def maxima(u):
                    dve.wait_ge(s_mm, u + 1)
                    dve.tensor_reduce(nmx[:, :], ps[:, S_BANK, :].rearrange("p (b m) -> p b m", b=2),
                                      AX.X, ALU.max, negate=True).then_inc(mx_ok, 1)

                def softmax(u):
                    dve.wait_ge(exp_ok, u + 1)
                    dve.reciprocal(rinv[:, :], rsum[:, :]).then_inc(rinv_ok, 1)
                    dve.wait_ge(rinv_ok, u + 1)
                    for b in range(2):
                        last = dve.tensor_scalar(pn[:, b, :], pe_[:, b, :], rinv[:, b:b + 1], None, ALU.mult)
                    last.then_inc(pn_ok, 1)

                def unit(u, g, p, par, last=False, first=False, t=0):
                    ln2 = p == 0 and not (isinstance(t, int) and t == GROUPS - 1)
                    ln3 = p == 1 and not (isinstance(t, int) and t == 0)
                    softmax(u)
                    if not (last and p == 3):
                        k_low(u + 1)
                    if ln2:
                        norm_stats(norm0 + (1 if first else 2 * t), [h[:, t + 1, :]])
                    if ln3:
                        residual(t - 1, norm0 + 2 * t + (0 if last else 1))
                    if p == 3 and not last:
                        q_low(g + 1)
                    if not first:
                        o_part(u - 1, (p + 3) % 4)
                    if not (last and p >= 1 or first):
                        v_low(u + 3, (p + 3) % 4, par if p == 0 else 1 - par)
                    if p == 0 and not first:
                        o_low(g - 1)
                    if ln2:
                        z2_of(t + 1, 1 if first else 2 * t)
                    if ln3:
                        z3_of(t - 1, norm0 + 2 * t + (0 if last else 1))
                    dve.wait_ge(pT_hi_ok, u + 1)
                    dve.tensor_tensor(pT[:, :, 1, :], ps[:, T_BANK, :].rearrange("p (c n) -> p c n", n=P),
                                      bits(pT[:, :, 0, :]), ALU.subtract)\
                        .then_inc(pT_ok, 1)
                    if not (last and p == 3):
                        maxima(u + 1)
                    if p == 1 and not last:
                        x2_full(g + 1)

                def residual(g, k):
                    dve.wait_ge(wo_mm, GROUPS * l + g + 1)
                    dve.tensor_tensor(h[:, g, :], h[:, g, :], ps[:, Y_BANK, :], ALU.add).then_inc(h_att, 1)
                    wait_apart(dve, h_att, GROUPS * l + g + 2)
                    norm_stats(k, [h[:, g, :]])

                def z3_of(g, k):
                    norm_wait(k)
                    dve.tensor_scalar(z3[:, g, :], h[:, g, :], mv[:, 0:1], rstd[:, 0:1],
                                      ALU.subtract, ALU.mult).then_inc(z3_ok, 1)
                    dve.wait_ge(z3_ok, GROUPS * l + g + 1)
                    dve.tensor_tensor(h[:, g, :], h[:, g, :], bias_row[:, :], ALU.add).then_inc(h_bias, 1)

                def z2_of(g, k):
                    norm_wait(norm0 + k)
                    dve.tensor_scalar(z2[:, :], h[:, g, :], mv[:, 0:1], rstd[:, 0:1],
                                      ALU.subtract, ALU.mult).then_inc(z2_ok, 1)

                def body(g, par, last=False):
                    u, gg = UNITS * l + PAIRS * g, GROUPS * l + g
                    for p in range(1, 4):
                        unit(u + p, gg, p, par, last, t=g)
                    if not last:
                        unit(u + 4, gg + 1, 0, 1 - par, t=g + 1)
                    else:
                        o_part(u + 3, 3)
                        o_low(gg)

                norm_stats(norm0, [h[:, 0, :]])
                z2_of(0, 0)
                for mc in range(2):
                    v_low(UNITS * l + mc, mc, 0, V_BANK + mc)
                x2_full(GROUPS * l)
                v_low(UNITS * l + 2, 2, 0, V_BANK + 2)
                k_low(UNITS * l)
                q_low(GROUPS * l)
                v_low(UNITS * l + 3, 3, 0, V_BANK + 3)
                maxima(UNITS * l)
                unit(UNITS * l, GROUPS * l, 0, 0, first=True)
                dve.wait_ge(row_in, 16 * l + 32)
                body(0, 0)
                with dve.Fori(0, GROUPS // 2 - 2) as i:
                    body(2 * i + 1, 1)
                    body(2 * i + 2, 0)
                body(GROUPS - 3, 1)
                body(GROUPS - 2, 0)
                body(GROUPS - 1, 1, last=True)

                def mlp_step(j, a, s):
                    n = 32 * l + 8 * j + 4 * a + s
                    c = s % 2
                    dve.wait_ge(f_ok, n + 1)
                    dve.wait_ge(gel_ok, n + 1)
                    dve.scalar_tensor_tensor(
                        ff[:, s % 2, :], ps[:, step_bank(j, a, s, 0), :],
                        cols_sb[:, bass.ds(COL["geglu_b"] + 32 * l + 4 * j + 2 * a + c, 1)],
                        gel[:, s % 2, :], ALU.add, ALU.mult).then_inc(ff_ok, 1)

                def mlp_add(j, a):
                    for t in range(NT):
                        dve.wait_ge(ffo_mm, 64 * l + 16 * j + 8 * a + t + 1)
                        dve.tensor_tensor(h[:, t, :], h[:, t, :], ps[:, 4 + t % 4, :], ALU.add)\
                            .then_inc(h_ffo, 1)

                residual(NT - 1, norm0 + 2 * NT - 1)
                z3_of(NT - 1, norm0 + 2 * NT - 1)
                mlp_step(0, 0, 0)
                mlp_step(0, 0, 1)
                mlp_step(0, 0, 2)
                mlp_step(0, 0, 3)
                for s in range(4):
                    mlp_step(0, 1, s)
                mlp_add(0, 0)
                with dve.Fori(1, MG // 2) as j:
                    for s in range(4):
                        mlp_step(j, 0, s)
                    mlp_add(j - 1, 1)
                    for s in range(4):
                        mlp_step(j, 1, s)
                    mlp_add(j, 0)
                mlp_add(MG // 2 - 1, 1)
                dve.wait_ge(h_ffo, 64 * l + 64)

            for t in range(NT):
                dve.wait_ge(hT_mm, t + 1)
                if t >= 2:
                    dve.wait_ge(y_lo, KC + t - 1)
                dve.tensor_copy(full[:, t % 2, :], ps[:, t, :]).then_inc(bnf_ok, 1)
            gcn(1)

        @block.tensor
        def _(pe):
            def product(bank, steps, first=True, last=True):
                n = len(steps)
                for i, (l_hi, l_lo, r_hi, r_lo) in enumerate(steps):
                    pe.matmul(bank, l_hi, r_hi, start=(first and i == 0), stop=False)
                    pe.matmul(bank, l_hi, r_lo, start=False, stop=False)
                    end = pe.matmul(bank, l_lo, r_hi, start=False, stop=(last and i == n - 1))
                return end

            pe.sem_inc(oh_used, 4)
            pe.wait_ge(const_ok, 5)
            for t in range(NT):
                pe.wait_ge(x0_ok, t + 1)
                for k in range(KC):
                    last = pe.transpose(ps[:, t, k * P:(k + 1) * P], z1[:, t, k * P:(k + 1) * P], ident[:, :])
                last.then_inc(x0_mm, 1)

            def count(f):
                for t in range(NT):
                    if isinstance(f, int):
                        pe.wait_ge(x0T_ok, t + 1)
                    else:
                        pe.wait_ge(a_sums, NT * f - NT + t + 1)
                    pe.matmul(ps[:, t, :], minus[:, :], shift[:, :], start=True, stop=False)
                def chunks(c4, flush_ends=False):
                    for c in range(4):
                        pe.wait_ge(oh_ok, FLUSH * f + 4 * c4 + c + 1)
                        closes = flush_ends and c == 3
                        for t in range(NT):
                            last = pe.matmul(ps[:, t, :], oh_s[:, c, t * P:(t + 1) * P], oh_d[:, c, :],
                                             start=False, stop=closes)
                            if closes:
                                last.then_inc(a_mm, 1)
                        if not closes:
                            last.then_inc(oh_used, 1)

                with pe.Fori(0, NT - 1) as c4:
                    chunks(c4)
                chunks(NT - 1, flush_ends=True)

            count(0)
            with pe.Fori(1, FLUSHES) as f:
                count(f)

            def g_product(t):
                r = slice(t * P, (t + 1) * P)
                product(ps[:, t, :], [(yT_hi[:, k, r], yT_lo[:, k, r], w_hi[:, 0, k, :], w_lo[:, 0, k, :])
                                      for k in range(KC)]).then_inc(g_mm, 1)

            def aggregate(use):
                for half in range(2):
                    for t in range(NT):
                        r = slice(t * P, (t + 1) * P)
                        if not half:
                            pe.wait_ge(xs_ok, NT * use + t + 1)
                        for s in range(half * NT // 2, (half + 1) * NT // 2):
                            if not t:
                                pe.wait_ge((xs_lo_ok, xs_lo_odd)[s % 2], NT // 2 * use + s // 2 + 1)
                            last = product(ps[:, t, :],
                                           [(at_hi[:, s, r], at_lo[:, s, r], xs_hi[:, s, :], xs_lo[:, s, :])],
                                           first=(s == 0), last=(s == NT - 1))
                        if half:
                            last.then_inc(agg_mm, 1)
                    if not half:
                        last.then_inc(agg_half, 1)

            pe.wait_ge(y_lo, KC)
            pe.wait_ge(w_ok, 2)
            for t in range(6):
                pe.wait_ge(a_sums, NT * FLUSHES - NT + t + 1)
                g_product(t)
            pe.wait_ge(a_sums, NT * FLUSHES)
            pe.wait_ge(ones_ok, 1)
            for st in range(NT):
                pe.wait_ge((a_lo, a_lo_odd)[st % 2], st // 2 + 1)
                for half in range(2):
                    r = slice(half * HALF, (half + 1) * HALF)
                    pe.matmul(ps[0:2, 7 - half, :], ones[:, :], at_hi[:, st, r], start=(st == 0), stop=False)
                    last = pe.matmul(ps[0:2, 7 - half, :], ones[:, :], at_lo[:, st, r], start=False,
                                     stop=(st == NT - 1))
            last.then_inc(row_mm, 1)
            pe.wait_ge(row_ok, 2)
            for t in range(NT):
                last = pe.transpose(ps[:, 7, 2 * t:2 * t + 2], sums[0:2, t // 4, t % 4 * P:(t % 4 + 1) * P],
                                    ident[0:2, 0:2])
            last.then_inc(deg_mm, 1)
            g_product(6)
            pe.wait_ge(deg_ok, 1)
            g_product(7)
            aggregate(0)
            pe.wait_ge(agg_s, NT)

            with pe.Fori(0, L) as l:
                def k_product(u, p, slot):
                    r = slice(p * P, (p + 1) * P)
                    product(ps[:, K_BANK, :], [(w_hi[:, 1, k, r], w_lo[:, 1, k, r],
                                                cond_hi[slot][:, k, :], cond_lo[slot][:, k, :])
                                               for k in range(KC)]).then_inc(k_mm, 1)

                def v_product(u, mc, slot, bank=V_BANK):
                    if u is not None:
                        pe.wait_ge(v_ok, u)
                    r = slice(mc * P, (mc + 1) * P)
                    product(ps[:, bank, :], [(cond_hi[slot][:, k, r], cond_lo[slot][:, k, r],
                                                w_hi[:, 2, k, :], w_lo[:, 2, k, :])
                                               for k in range(KC)]).then_inc(v_mm, 1)

                def s_product(u, g, p):
                    pe.wait_ge(k_ok, u + 1)
                    if p == 0:
                        pe.wait_ge(qb_ok, g + 1)
                    for b in range(2):
                        r = slice(b * M, (b + 1) * M)
                        last = product(ps[:, S_BANK, r], [(qbd_hi[:, p, b, :], qbd_lo[:, p, b, :],
                                                           kT_hi[:, r], kT_lo[:, r])])
                    last.then_inc(s_mm, 1)

                def p_transpose(u):
                    pe.wait_ge(pn_ok, u + 1)
                    for b in range(2):
                        for c in range(2):
                            i = 2 * b + c
                            last = pe.transpose(ps[:, T_BANK, i * P:(i + 1) * P], pn[:, b, c * P:(c + 1) * P],
                                                ident[:, :])
                    last.then_inc(t_mm, 1)

                def pv_product(u, p, slot):
                    pe.wait_ge(pT_ok, u + 1)
                    pe.wait_ge(o_part_ok, u + 1)
                    for b in range(2):
                        both = ps[:, PV_BANK + p % 2, b * 2 * P:(b + 1) * 2 * P]
                        upper = ps[:, PV_BANK + p % 2, b * 2 * P:b * 2 * P + P]
                        r = slice(p * P, (p + 1) * P)
                        pe.matmul(both, v_hi[:, slot, 2 * b, r], pT[:, 2 * b, :, :].rearrange("p t n -> p (t n)"),
                                  start=True, stop=False)
                        for c in range(2):
                            pe.matmul(upper, v_lo[:, slot, 2 * b + c, r], pT[:, 2 * b + c, 0, :],
                                      start=False, stop=False)
                        last = pe.matmul(both, v_hi[:, slot, 2 * b + 1, r],
                                         pT[:, 2 * b + 1, :, :].rearrange("p t n -> p (t n)"),
                                         start=False, stop=True)
                    last.then_inc(pv_mm, 1)

                def t2(g):
                    pe.wait_ge(z2_ok, g + 1)
                    for k in range(KC):
                        last = pe.transpose(ps[:, X_BANK, k * P:(k + 1) * P], z2[:, k * P:(k + 1) * P], ident[:, :])
                    last.then_inc(t2_mm, 1)

                def q_product(g, first=False):
                    pe.wait_ge(x2_ok, g + 1)
                    if not first:
                        pe.wait_ge(h_att, g)
                    product(ps[:, Y_BANK, :], [(xT2_hi[:, k, :], xT2_lo[:, k, :], w_hi[:, 0, k, :], w_lo[:, 0, k, :])
                                               for k in range(KC)]).then_inc(q_mm, 1)

                def q_transpose(g):
                    pe.wait_ge(q_ok, g + 1)
                    for p in range(PAIRS):
                        last = pe.transpose(ps[:, X_BANK, p * P:(p + 1) * P], q_sb[:, p * P:(p + 1) * P], ident[:, :])
                    last.then_inc(qt_mm, 1)

                def wo_product(g):
                    pe.wait_ge(o_ok, g + 1)
                    product(ps[:, Y_BANK, :], [(oT_hi[:, p, :], oT_lo[:, p, :], w_hi[:, 3, p, :], w_lo[:, 3, p, :])
                                               for p in range(PAIRS)]).then_inc(wo_mm, 1)

                def t3(t):
                    pe.wait_ge(z3_ok, NT * l + t + 1)
                    if t in (1, 3, 5):
                        pe.wait_ge(full3_ok, NT * l + {1: 1, 3: 3, 5: 5}[t])
                    for k in range(KC):
                        last = pe.transpose(ps[:, T3_BANK[t], k * P:(k + 1) * P], z3[:, t, k * P:(k + 1) * P],
                                            ident[:, :])
                    last.then_inc(t3_mm, 1)

                def mlp_product(j, a, s, v, r=slice(0, HALF)):
                    half, c = s // 2, s % 2
                    return product(ps[:, step_bank(j, a, s, v), r],
                                   [(wg_hi[:, a, k, v, c * P:(c + 1) * P], wg_lo[:, a, k, v, c * P:(c + 1) * P],
                                     xT3_hi[half][:, k, r], xT3_lo[half][:, k, r]) for k in range(KC)])

                def mlp_step(j, a, s):
                    pe.wait_ge(ff_ok, 32 * l + 8 * j + 4 * a + s - 1)
                    mlp_product(j, a, s, 0)
                    mlp_product(j, a, s, 1).then_inc(u_mm, 1)

                def unit(u, g, p, par, last=False, first=False, opens_last=False, group0=False):
                    if not (last and p == 3):
                        k_product(u + 1, (p + 1) % 4, par if p < 3 else 1 - par)
                    if opens_last:
                        t3(0)
                    if p == 1 and not group0:
                        wo_product(g - 1)
                    if p == 3 and not last:
                        q_transpose(g + 1)
                    if p == 3 and last:
                        pe.wait_ge(full3_ok, NT * l + 4)
                        mlp_product(0, 0, 0, 1, slice(0, 2 * P))
                    if not first:
                        pv_product(u - 1, (p + 3) % 4, par if p else 1 - par)
                    if not (last and p >= 1 or first):
                        v_product(u + 3, (p + 3) % 4, par if p == 0 else 1 - par)
                    if opens_last:
                        t3(1)
                    if p == 2 and last:
                        t3(3)
                        pe.wait_ge(w_ok, FIRST_PIECES + PIECES * l + 2)
                        pe.wait_ge(x3_ok, 2 + NT * l + 2)
                        mlp_product(0, 0, 0, 0, slice(0, 2 * P))
                    if p == 3 and last:
                        pe.wait_ge(x3_ok, 2 + NT * l + 4)
                        mlp_product(0, 0, 0, 0, slice(2 * P, HALF))
                    p_transpose(u)
                    if not (last and p == 3):
                        s_product(u + 1, g if p < 3 else g + 1, (p + 1) % 4)
                    if p == 2 and not last:
                        q_product(g + 1)
                    if p == 1 and not last:
                        t2(g + 1)
                    if p == 1 and last:
                        pe.wait_ge(v_ok, UNITS * l + UNITS)
                        t3(2)
                    if p == 2 and last:
                        t3(4)
                    if p == 3 and last:
                        t3(5)
                        mlp_product(0, 0, 0, 1, slice(2 * P, HALF)).then_inc(u_mm, 1)

                def body(g, i, par, last=False):
                    u, gg = UNITS * l + PAIRS * g, GROUPS * l + g
                    if not last:
                        pe.wait_ge(cond_in[1 - par], 128 * l + 32 * (i + 1 + par))
                    for p in range(1, 4):
                        unit(u + p, gg, p, par, last, group0=isinstance(g, int) and g == 0)
                    if not last:
                        unit(u + 4, gg + 1, 0, 1 - par, opens_last=isinstance(g, int) and g == GROUPS - 2)
                    else:
                        pv_product(u + 3, 3, par)

                pe.wait_ge(w_ok, PIECES * l + FIRST_PIECES)
                pe.wait_ge(cond_in[0], 128 * l + 32)
                for mc in range(2):
                    v_product(None, mc, 0, V_BANK + mc)
                t2(GROUPS * l)
                v_product(None, 2, 0, V_BANK + 2)
                k_product(UNITS * l, 0, 0)
                q_product(GROUPS * l, first=True)
                q_transpose(GROUPS * l)
                v_product(None, 3, 0, V_BANK + 3)
                pe.wait_ge(v_ok, UNITS * l + 3)
                s_product(UNITS * l, GROUPS * l, 0)
                unit(UNITS * l, GROUPS * l, 0, 0, first=True)
                body(0, 0, 0)
                with pe.Fori(0, GROUPS // 2 - 2) as i:
                    body(2 * i + 1, i, 1)
                    body(2 * i + 2, i + 1, 0)
                body(GROUPS - 3, GROUPS // 2 - 2, 1)
                body(GROUPS - 2, GROUPS // 2 - 1, 0)
                body(GROUPS - 1, GROUPS // 2 - 1, 1, last=True)

                def mlp_up(j, a):
                    pe.wait_ge(w_ok, FIRST_PIECES + PIECES * l + 8 * j + 4 * a + 1)
                    for s in range(4):
                        mlp_step(j, a, s)

                def mlp_down(j, a, first=False):
                    pe.wait_ge(w_ok, FIRST_PIECES + PIECES * l + 8 * j + 4 * a + 3)
                    pe.wait_ge(f_ok, 2 + 32 * l + 8 * j + 4 * a + 4)
                    for t in range(NT):
                        if not (first and t < 4):
                            pe.wait_ge(h_ffo, 64 * l + 16 * j + 8 * a + t - 3)
                        r = slice(t * P, (t + 1) * P)
                        product(ps[:, 4 + t % 4, :], [(f_hi[a][:, c, r], f_lo[a][:, c, r],
                                                       wf_hi[:, a, c, :], wf_lo[:, a, c, :])
                                                      for c in range(2)]).then_inc(ffo_mm, 1)

                pe.wait_ge(o_part_ok, 2 + UNITS * l + UNITS - 1)
                t3(6)
                mlp_product(0, 0, 1, 0)
                wo_product(GROUPS * l + GROUPS - 1)
                mlp_product(0, 0, 1, 1).then_inc(u_mm, 1)
                t3(7)
                pe.wait_ge(x3_ok, 2 + NT * l + 6)
                mlp_product(0, 0, 2, 0, slice(0, 2 * P))
                pe.wait_ge(ff_ok, 32 * l + 1)
                mlp_product(0, 0, 2, 1, slice(0, 2 * P))
                pe.wait_ge(x3_ok, 2 + NT * l + NT)
                mlp_product(0, 0, 2, 0, slice(2 * P, HALF))
                mlp_product(0, 0, 2, 1, slice(2 * P, HALF)).then_inc(u_mm, 1)
                mlp_step(0, 0, 3)
                mlp_up(0, 1)
                mlp_down(0, 0, first=True)
                with pe.Fori(1, MG // 2) as j:
                    mlp_up(j, 0)
                    mlp_down(j - 1, 1)
                    mlp_up(j, 1)
                    mlp_down(j, 0)
                mlp_down(MG // 2 - 1, 1)

            pe.wait_ge(h_ffo, 64 * L)
            for t in range(NT):
                for k in range(KC):
                    last = pe.transpose(ps[:, t, k * P:(k + 1) * P], h[:, t, k * P:(k + 1) * P], ident[:, :])
                last.then_inc(hT_mm, 1)
            pe.wait_ge(w_ok, FIRST_PIECES + PIECES * L)
            for t in range(NT):
                pe.wait_ge(y_lo, KC + t + 1)
                g_product(t)
            pe.wait_ge(at_in, 32)
            aggregate(1)


def _arrays(inputs):
    import numpy as np

    a = {n.replace("L0_gnn_", ""): np.asarray(v) for n, v in inputs.items()}
    D = a["x"].shape[1]
    P, L = 128, a["Wq"].shape[0]

    def square(w):
        return list(w.reshape(2, 2, P, D).transpose(0, 2, 1, 3).reshape(2, P, 1024))

    attention = [[square(a[n][l]) for n in ("Wq", "Wk", "Wv", "Wo")] for l in range(L)]
    attention.append([square(a["gcn_out_w"])] * 4)
    pieces = square(a["gcn_in_w"]) + [p for m in attention[0] for p in m]
    for l in range(L):
        up = a["geglu_w"][l].reshape(2, 2, P, 2, 8, 256).transpose(4, 0, 2, 1, 3, 5).reshape(8, 2, P, 1024)
        down = a["ffo_w"][l].reshape(8, 2, P, D).transpose(0, 2, 1, 3).reshape(8, P, 1024)
        pieces += [up[0, 0], up[0, 1]]
        for q in range(8):
            pieces += [down[q], *(up[q + 1] if q < 7 else []), attention[l + 1][q // 2][q % 2]]
    cond = a["cond"].reshape(8, 512, 4, P).transpose(0, 3, 2, 1)
    vectors = [a["bn_w"][None], a["bn_b"][None], a["ln2_w"], a["ln2_b"], a["ln3_w"], a["ln3_b"], a["geglu_b"]]
    cols = np.concatenate([v.reshape(-1, P) for v in vectors]).T
    rows = np.concatenate([a["gcn_in_b"][None], a["ffo_b"], a["gcn_out_b"][None]])
    return {"x": a["x"], "src": a["src"].reshape(P, -1), "dst": a["dst"].reshape(P, -1), "condT": cond,
            "pieces": np.stack(pieces), "cols": cols, "rows": rows}


def kernel(**inputs):
    import numpy as np
    import concourse.bacc as bacc
    from concourse.bass_utils import run_bass_kernel_spmd

    nc = bacc.Bacc("TRN2", target_bir_lowering=False, num_devices=1, dynamic_dma_scratch_size=1024)
    arrays, args = {}, []
    for name, a in _arrays(inputs).items():
        a = np.ascontiguousarray(a)
        arrays[f"in_{name}"] = a
        args.append(nc.dram_tensor(f"in_{name}", a.shape, mybir.dt.from_np(a.dtype), kind="ExternalInput").ap())
    n, d = inputs["x"].shape
    args.append(nc.dram_tensor("out", (n, d), mybir.dt.float32, kind="ExternalOutput").ap())
    gnn_preln_kernel(nc, *args)
    r = run_bass_kernel_spmd(nc, [arrays], core_ids=[0])
    return np.asarray(r.results[0]["out"])
```
